# Optimizing a Trainium2 kernel written in Bass

```python
import numpy as np
import jax
import jax.numpy as jnp

def _softmax(x, axis=-1):
    return jax.nn.softmax(x, axis=axis)

def _gelu(x):
    return jax.nn.gelu(x, approximate=True)

def _silu(x):
    return jax.nn.silu(x)

def _sigmoid(x):
    return jax.nn.sigmoid(x)

def _layernorm(x, axis=-1, eps=1e-05):
    m = jnp.mean(x, axis=axis, keepdims=True)
    v = jnp.var(x, axis=axis, keepdims=True)
    return (x - m) / jnp.sqrt(v + eps)

def _scatter_add(tgt, idx, src, axis=0):
    return tgt.at[idx].add(src)

def _segment_sum(src, seg, n):
    return jax.ops.segment_sum(src, seg, n)
kernel_name = 'mk_decoder_postln_d1_seqx_r8_3f353b'

def setup_inputs(seed: int=0):
    np.random.seed(seed)
    _w = jnp.asarray

    def _rec_inputs():
        import jax
        import jax.numpy as jnp
        _rk = jax.random.key(seed)
        x = 7.22e-05 + 1 * jax.random.normal(jax.random.fold_in(_rk, 1), (128, 64, 128), jnp.float32)
        _lenS = 64 - jax.random.randint(jax.random.fold_in(_rk, 7), (128,), 0, max(1, 64 // 4) + 1, jnp.int32)
        _lenS2 = 64 - jax.random.randint(jax.random.fold_in(_rk, 8), (128,), 0, max(1, 64 // 4) + 1, jnp.int32)
        _ctx_1024P = jax.random.normal(jax.random.fold_in(_rk, 11), (128, 16, 128), jnp.float32)
        _ctx_1024c = jax.random.dirichlet(jax.random.fold_in(_rk, 511), 0.3 * jnp.ones((16,), jnp.float32), (128, 64))
        _ctx_1024t = jnp.einsum('bsk,bkd->bsd', _ctx_1024c, _ctx_1024P)
        _ctx_1024t = _ctx_1024t * jax.lax.rsqrt(jnp.mean(jnp.square(_ctx_1024t)) + 1e-12) * 0.953939
        ctx_1024 = 4.13588e-05 + 0.999923 * (_ctx_1024t + 0.3 * jax.random.normal(jax.random.fold_in(_rk, 611), (128, 64, 128), jnp.float32))
        _validS = jnp.arange(64)[None, :] < _lenS[:, None]
        _validS2 = jnp.arange(64)[None, :] < _lenS2[:, None]
        _causal = jnp.tril(jnp.ones((64, 64), dtype=bool))
        mask_Bx1xSxS2_bf0 = jnp.logical_not(jnp.ones((128, 1, 64, 64), dtype=bool))
        return (x, ctx_1024, mask_Bx1xSxS2_bf0)
    x, ctx_1024, mask_Bx1xSxS2_bf0 = _rec_inputs()

    def _L0_attn_setup():
        import jax, jax.numpy as jnp
        import numpy as np
        H = 4
        CHUNK = 64
        EPS = 1e-05
        GATE_NORM = 16.0

        def _gla_forward(hidden_states, Wq, Wk, Wv, Wg, Wgk1, Wgk2, bgk2, rms_w, Wo):
            B, T, D = hidden_states.shape
            Kd, Vd = (Wq.shape[1], Wv.shape[1])
            Dk, Dv = (Kd // H, Vd // H)
            scale = Dk ** (-0.5)

            def heads(x, d):
                return x.reshape(B, T, H, d).transpose(0, 2, 1, 3)
            q = heads(hidden_states @ Wq, Dk)
            k = heads(hidden_states @ Wk, Dk)
            v = heads(hidden_states @ Wv, Dv)
            gk = jax.nn.log_sigmoid(hidden_states @ Wgk1 @ Wgk2 + bgk2) / GATE_NORM
            gk = heads(gk, Dk)
            N = T // CHUNK

            def chunks(x):
                return x.reshape(B, H, N, CHUNK, x.shape[-1]).transpose(2, 0, 1, 3, 4)
            qc, kc, vc, gc = (chunks(q), chunks(k), chunks(v), chunks(gk))
            g = jnp.cumsum(gc, axis=-2)
            mask = jnp.tril(jnp.ones((CHUNK, CHUNK), bool))

            def step(S, inp):
                qi, ki, vi, gi = inp
                g_last = gi[..., -1:, :]
                qg = qi * jnp.exp(gi) * scale
                A = jnp.einsum('bhcd,bhjd->bhcj', qg, ki * jnp.exp(-gi))
                A = jnp.where(mask, A, 0.0)
                o = jnp.einsum('bhcd,bhde->bhce', qg, S) + jnp.einsum('bhcj,bhje->bhce', A, vi)
                kg = ki * jnp.exp(g_last - gi)
                S = S * jnp.exp(g_last)[..., 0, :, None] + jnp.einsum('bhcd,bhce->bhde', kg, vi)
                return (S, o)
            S0 = jnp.zeros((B, H, Dk, Dv), hidden_states.dtype)
            _, o = jax.lax.scan(step, S0, (qc, kc, vc, gc))
            o = o.transpose(1, 2, 0, 3, 4).reshape(B, H, T, Dv).transpose(0, 2, 1, 3)
            gt = (hidden_states @ Wg).reshape(B, T, H, Dv)
            o = o * jax.lax.rsqrt(jnp.mean(o * o, axis=-1, keepdims=True) + EPS) * rms_w
            o = o * (gt * jax.nn.sigmoid(gt))
            return o.reshape(B, T, Vd) @ Wo
        key = jax.random.key(seed)
        ks = jax.random.split(key, 10)
        B, T, D = (4, 256, 128)
        Kd, Vd, LR = (128, 256, 16)
        s = 0.02
        return {'hidden_states': jax.random.normal(ks[0], (B, T, D), jnp.float32), 'Wq': jax.random.normal(ks[1], (D, Kd), jnp.float32) * s, 'Wk': jax.random.normal(ks[2], (D, Kd), jnp.float32) * s, 'Wv': jax.random.normal(ks[3], (D, Vd), jnp.float32) * s, 'Wg': jax.random.normal(ks[4], (D, Vd), jnp.float32) * s, 'Wgk1': jax.random.normal(ks[5], (D, LR), jnp.float32) * s, 'Wgk2': jax.random.normal(ks[6], (LR, Kd), jnp.float32) * s, 'bgk2': jnp.zeros((Kd,), jnp.float32), 'rms_w': jnp.ones((Vd // H,), jnp.float32), 'Wo': jax.random.normal(ks[7], (Vd, D), jnp.float32) * s}
    _L0_attn_all = _L0_attn_setup()
    _L0_attn_in = {k: v for k, v in _L0_attn_all.items() if k in ('Wq', 'Wk', 'Wv', 'Wg', 'Wgk1', 'Wgk2', 'bgk2', 'rms_w', 'Wo')}
    del _L0_attn_all

    def _L0_xattn_setup():
        import jax, jax.numpy as jnp
        import numpy as np
        D_MODEL = 128
        NUM_HEAD = 16
        DK = D_MODEL // NUM_HEAD
        B, S = (4, 256)
        NEG = -1000000000.0
        key = jax.random.key(seed)
        ks = jax.random.split(key, 12)
        sc = 1.0 / np.sqrt(D_MODEL)
        return {'q': jax.random.normal(ks[0], (B, S, D_MODEL), jnp.float32), 'k': jax.random.normal(ks[1], (B, S, D_MODEL), jnp.float32), 'v': jax.random.normal(ks[2], (B, S, D_MODEL), jnp.float32), 'mask': jnp.zeros((B, 1, S, S), dtype=bool), 'wq': jax.random.normal(ks[3], (D_MODEL, D_MODEL), jnp.float32) * sc, 'bq': jnp.zeros((D_MODEL,), jnp.float32), 'wk': jax.random.normal(ks[4], (D_MODEL, D_MODEL), jnp.float32) * sc, 'bk': jnp.zeros((D_MODEL,), jnp.float32), 'wv': jax.random.normal(ks[5], (D_MODEL, D_MODEL), jnp.float32) * sc, 'bv': jnp.zeros((D_MODEL,), jnp.float32), 'wo': jax.random.normal(ks[6], (D_MODEL, D_MODEL), jnp.float32) * sc, 'bo': jnp.zeros((D_MODEL,), jnp.float32)}
    _L0_xattn_all = _L0_xattn_setup()
    _L0_xattn_in = {k: v for k, v in _L0_xattn_all.items() if k in ('wq', 'bq', 'wk', 'bk', 'wv', 'bv', 'wo', 'bo')}
    del _L0_xattn_all

    def _L0_ffn_setup():
        import jax, jax.numpy as jnp
        import numpy as np
        B, S, D = (4, 256, 128)
        E, F = (8, 512)
        key = jax.random.key(seed)
        ks = jax.random.split(key, 5)
        x = jax.random.normal(ks[0], (B, S, D), dtype=jnp.float32)
        switch_w = jax.random.normal(ks[1], (D, E), dtype=jnp.float32) * D ** (-0.5)
        switch_b = jnp.zeros((E,), dtype=jnp.float32)
        w1 = jax.random.normal(ks[2], (E, D, F), dtype=jnp.float32) * D ** (-0.5)
        b1 = jnp.zeros((E, F), dtype=jnp.float32)
        w2 = jax.random.normal(ks[3], (E, F, D), dtype=jnp.float32) * F ** (-0.5)
        b2 = jnp.zeros((E, D), dtype=jnp.float32)
        return {'x': x, 'switch_w': switch_w, 'switch_b': switch_b, 'w1': w1, 'b1': b1, 'w2': w2, 'b2': b2}
    _L0_ffn_all = _L0_ffn_setup()
    _L0_ffn_in = {k: v for k, v in _L0_ffn_all.items() if k in ('switch_w', 'switch_b', 'w1', 'b1', 'w2', 'b2')}
    del _L0_ffn_all
    return {'x': x, 'ctx_1024': ctx_1024, 'mask_Bx1xSxS2_bf0': mask_Bx1xSxS2_bf0, 'L0_attn_Wq': _L0_attn_in['Wq'], 'L0_attn_Wk': _L0_attn_in['Wk'], 'L0_attn_Wv': _L0_attn_in['Wv'], 'L0_attn_Wg': _L0_attn_in['Wg'], 'L0_attn_Wgk1': _L0_attn_in['Wgk1'], 'L0_attn_Wgk2': _L0_attn_in['Wgk2'], 'L0_attn_bgk2': _L0_attn_in['bgk2'], 'L0_attn_rms_w': _L0_attn_in['rms_w'], 'L0_attn_Wo': _L0_attn_in['Wo'], 'L0_xattn_wq': _L0_xattn_in['wq'], 'L0_xattn_bq': _L0_xattn_in['bq'], 'L0_xattn_wk': _L0_xattn_in['wk'], 'L0_xattn_bk': _L0_xattn_in['bk'], 'L0_xattn_wv': _L0_xattn_in['wv'], 'L0_xattn_bv': _L0_xattn_in['bv'], 'L0_xattn_wo': _L0_xattn_in['wo'], 'L0_xattn_bo': _L0_xattn_in['bo'], 'L0_ffn_switch_w': _L0_ffn_in['switch_w'], 'L0_ffn_switch_b': _L0_ffn_in['switch_b'], 'L0_ffn_w1': _L0_ffn_in['w1'], 'L0_ffn_b1': _L0_ffn_in['b1'], 'L0_ffn_w2': _L0_ffn_in['w2'], 'L0_ffn_b2': _L0_ffn_in['b2']}

def reference(x, ctx_1024, mask_Bx1xSxS2_bf0, L0_attn_Wq, L0_attn_Wk, L0_attn_Wv, L0_attn_Wg, L0_attn_Wgk1, L0_attn_Wgk2, L0_attn_bgk2, L0_attn_rms_w, L0_attn_Wo, L0_xattn_wq, L0_xattn_bq, L0_xattn_wk, L0_xattn_bk, L0_xattn_wv, L0_xattn_bv, L0_xattn_wo, L0_xattn_bo, L0_ffn_switch_w, L0_ffn_switch_b, L0_ffn_w1, L0_ffn_b1, L0_ffn_w2, L0_ffn_b2):
    import jax
    import jax.numpy as jnp

    def _L0_attn_ref(hidden_states, Wq, Wk, Wv, Wg, Wgk1, Wgk2, bgk2, rms_w, Wo):
        import jax, jax.numpy as jnp
        import numpy as np
        H = 4
        CHUNK = 64
        EPS = 1e-05
        GATE_NORM = 16.0

        def _gla_forward(hidden_states, Wq, Wk, Wv, Wg, Wgk1, Wgk2, bgk2, rms_w, Wo):
            B, T, D = hidden_states.shape
            Kd, Vd = (Wq.shape[1], Wv.shape[1])
            Dk, Dv = (Kd // H, Vd // H)
            scale = Dk ** (-0.5)

            def heads(x, d):
                return x.reshape(B, T, H, d).transpose(0, 2, 1, 3)
            q = heads(hidden_states @ Wq, Dk)
            k = heads(hidden_states @ Wk, Dk)
            v = heads(hidden_states @ Wv, Dv)
            gk = jax.nn.log_sigmoid(hidden_states @ Wgk1 @ Wgk2 + bgk2) / GATE_NORM
            gk = heads(gk, Dk)
            N = T // CHUNK

            def chunks(x):
                return x.reshape(B, H, N, CHUNK, x.shape[-1]).transpose(2, 0, 1, 3, 4)
            qc, kc, vc, gc = (chunks(q), chunks(k), chunks(v), chunks(gk))
            g = jnp.cumsum(gc, axis=-2)
            mask = jnp.tril(jnp.ones((CHUNK, CHUNK), bool))

            def step(S, inp):
                qi, ki, vi, gi = inp
                g_last = gi[..., -1:, :]
                qg = qi * jnp.exp(gi) * scale
                A = jnp.einsum('bhcd,bhjd->bhcj', qg, ki * jnp.exp(-gi))
                A = jnp.where(mask, A, 0.0)
                o = jnp.einsum('bhcd,bhde->bhce', qg, S) + jnp.einsum('bhcj,bhje->bhce', A, vi)
                kg = ki * jnp.exp(g_last - gi)
                S = S * jnp.exp(g_last)[..., 0, :, None] + jnp.einsum('bhcd,bhce->bhde', kg, vi)
                return (S, o)
            S0 = jnp.zeros((B, H, Dk, Dv), hidden_states.dtype)
            _, o = jax.lax.scan(step, S0, (qc, kc, vc, gc))
            o = o.transpose(1, 2, 0, 3, 4).reshape(B, H, T, Dv).transpose(0, 2, 1, 3)
            gt = (hidden_states @ Wg).reshape(B, T, H, Dv)
            o = o * jax.lax.rsqrt(jnp.mean(o * o, axis=-1, keepdims=True) + EPS) * rms_w
            o = o * (gt * jax.nn.sigmoid(gt))
            return o.reshape(B, T, Vd) @ Wo
        return _gla_forward(hidden_states, Wq, Wk, Wv, Wg, Wgk1, Wgk2, bgk2, rms_w, Wo)

    def _L0_xattn_ref(q, k, v, mask, wq, bq, wk, bk, wv, bv, wo, bo):
        import jax, jax.numpy as jnp
        import numpy as np
        D_MODEL = 128
        NUM_HEAD = 16
        DK = D_MODEL // NUM_HEAD
        B, S = (4, 256)
        NEG = -1000000000.0
        b, s, _ = q.shape
        Q = (q @ wq + bq).reshape(b, s, NUM_HEAD, DK).transpose(0, 2, 1, 3)
        K = (k @ wk + bk).reshape(b, -1, NUM_HEAD, DK).transpose(0, 2, 1, 3)
        V = (v @ wv + bv).reshape(b, -1, NUM_HEAD, DK).transpose(0, 2, 1, 3)
        score = jnp.einsum('bhqd,bhkd->bhqk', Q, K) / np.sqrt(DK)
        score = jnp.where(mask, NEG, score)
        attn = jax.nn.softmax(score, axis=-1)
        x = jnp.einsum('bhqk,bhkd->bhqd', attn, V)
        x = x.transpose(0, 2, 1, 3).reshape(b, s, NUM_HEAD * DK)
        return x @ wo + bo

    def _L0_ffn_ref(x, switch_w, switch_b, w1, b1, w2, b2):
        import jax, jax.numpy as jnp
        import numpy as np
        B, S, D = (4, 256, 128)
        E, F = (8, 512)
        b, s, d = x.shape
        t = x.reshape(-1, d)
        logits = t @ switch_w + switch_b
        route_prob = jax.nn.softmax(logits, axis=-1)
        route_prob_max = jnp.max(route_prob, axis=-1)
        routes = jnp.argmax(route_prob, axis=-1)
        out = jnp.zeros_like(t)
        n_experts = w1.shape[0]
        for e in range(n_experts):
            h = jax.nn.gelu(t @ w1[e] + b1[e])
            y = h @ w2[e] + b2[e]
            mask = (routes == e)[:, None]
            out = jnp.where(mask, y, out)
        out = out * route_prob_max[:, None]
        return out.reshape(b, s, d)
    x = _layernorm(x + _L0_attn_ref(x, L0_attn_Wq, L0_attn_Wk, L0_attn_Wv, L0_attn_Wg, L0_attn_Wgk1, L0_attn_Wgk2, L0_attn_bgk2, L0_attn_rms_w, L0_attn_Wo), axis=-1)
    x = _layernorm(x + _L0_xattn_ref(x, ctx_1024, ctx_1024, mask_Bx1xSxS2_bf0, L0_xattn_wq, L0_xattn_bq, L0_xattn_wk, L0_xattn_bk, L0_xattn_wv, L0_xattn_bv, L0_xattn_wo, L0_xattn_bo), axis=-1)
    x = _layernorm(x + _L0_ffn_ref(x, L0_ffn_switch_w, L0_ffn_switch_b, L0_ffn_w1, L0_ffn_b1, L0_ffn_w2, L0_ffn_b2), axis=-1)
    return x

_drawn_inputs = setup_inputs


def setup_inputs(seed=0):
    import zlib

    import numpy as np

    out = dict(_drawn_inputs(seed))
    spreads = {'L0_attn_bgk2': (0.0, 2.0),
     'L0_attn_rms_w': (1.0, 0.6),
     'L0_xattn_bq': (0.0, 0.1),
     'L0_xattn_bk': (0.0, 2.0),
     'L0_xattn_bv': (0.0, 0.1),
     'L0_xattn_bo': (0.0, 0.1),
     'L0_ffn_switch_b': (0.0, 0.1),
     'L0_ffn_b1': (0.0, 0.322),
     'L0_ffn_b2': (0.0, 0.1)}
    factors = {'L0_attn_Wgk1': 42.28, 'L0_attn_Wgk2': 38.871}
    for name, (base, spread) in spreads.items():
        noise = np.random.default_rng([zlib.crc32(name.encode()), seed]).standard_normal(out[name].shape)
        drawn = base * np.exp(spread * noise) if base else spread * noise
        out[name] = jnp.asarray(drawn.astype(out[name].dtype))
    for name, factor in factors.items():
        out[name] = (out[name] * factor).astype(out[name].dtype)
    return out
```

```python
import concourse.bass as bass
from concourse import mybir

F32 = mybir.dt.float32
I32 = mybir.dt.int32
U8 = mybir.dt.uint8
ALU = mybir.AluOpType
ACT = mybir.ActivationFunctionType
AX = mybir.AxisListType

P = 128
BATCH, SEQ, D = 128, 64, 128
TOKENS = BATCH * SEQ
TILES = TOKENS // P
GROUP = 512
GT = GROUP // P
GB = GROUP // SEQ
GROUPS = TOKENS // GROUP
HA, DKA, DVA = 4, 32, 64
VD = HA * DVA
LOWRANK = 16
GATE_NORM = 16.0
HX, DX = 16, 8
NEG = -1.0e9
KEEP = 3.0e38
EPS = 1e-5
EXPERTS, FF = 8, 512
FC = FF // P
ROW = D + 2
XTILES = TILES + EXPERTS - 1
CLAMP = 40.0
SILU_CLAMP = -44.0


def decoder_layer(nc, x, xT, ctxT, mask, Wq, Wk, Wv, Wg, Wgk1, Wgk2, bgk2, rms_w, Wo,
                  wq, bq, wk, bk, wv, bv, wo, bo, switch_w, switch_b, w1, b1T, w2, b2, out):
    sorted_x = nc.dram_tensor("sorted_x", (XTILES * P, ROW), F32, kind="Internal").ap()

    with (
        nc.sbuf_tensor("stream", [P, TILES, ROW], F32) as stream,
        nc.sbuf_tensor("streamT", [P, TOKENS], F32) as streamT,
        nc.sbuf_tensor("ident", [P, P], F32) as ident,
        nc.sbuf_tensor("eps", [P, 1], F32) as eps,
        nc.psum_tensor("banks", [P, 8, 512], F32) as banks,
    ):
        linear_attention(nc, x, xT, Wq, Wk, Wv, Wg, Wgk1, Wgk2, bgk2, rms_w, Wo,
                         stream, streamT, ident, eps, banks)
        with nc.sbuf_tensor("logits", [P, TILES, EXPERTS], F32) as logits:
            cross_attention(nc, ctxT, mask, wq, bq, wk, bk, wv, bv, wo, bo, switch_w, sorted_x,
                            stream, streamT, ident, eps, banks, logits)
            experts(nc, switch_b, w1, b1T, w2, b2, sorted_x, out,
                    stream, ident, eps, banks, logits)


def linear_attention(nc, x, xT, Wq, Wk, Wv, Wg, Wgk1, Wgk2, bgk2, rms_w, Wo,
                     stream, streamT, ident, eps, banks):
    from contextlib import ExitStack
    ctx = ExitStack()
    with ctx:
        def sb(name, shape, dt=F32):
            return ctx.enter_context(nc.sbuf_tensor("a_" + name, shape, dt))

        def sem(name):
            return ctx.enter_context(nc.semaphore("a_" + name))

        wq_s, wk_s = sb("wq", [P, P]), sb("wk", [P, P])
        wv_s, wg_s = sb("wv", [P, VD]), sb("wg", [P, VD])
        gk1_s = sb("gk1", [P, P])
        gk2_s = sb("gk2", [P, P])
        bgk_s, rms_s = sb("bgk", [P, 1]), sb("rms", [P, 1])
        wo_s = sb("wo", [P, 2, D])
        head_mean = sb("head_mean", [P, P])
        causal = sb("causal", [P, P])
        lowrank = sb("lowrank", [P, GROUP])
        uclamp = sb("uclamp", [P, GROUP])
        espl = sb("espl", [P, GROUP])
        lspl = sb("lspl", [P, GROUP])
        negsig = sb("negsig", [P, GROUP])
        egd = sb("egd", [P, 2, GROUP])
        qg = sb("qg", [P, 2, GT, HA, P])
        kn = sb("kn", [P, 2, GROUP])
        val = sb("val", [P, 2, GT, VD])
        gate = sb("gate", [P, 2, 2, GROUP])
        gexp = sb("gexp", [P, 2, GROUP])
        glog = sb("glog", [P, 2, 2, GROUP])
        scores = sb("scores", [P, 2, HA, P])
        square = sb("square", [P, 2, GROUP])
        lms = sb("lms", [P, 2, GROUP])
        wlog = sb("wlog", [P, 2, GROUP])
        wexp = sb("wexp", [P, 2, GROUP])
        onorm = sb("onorm", [P, 2, GROUP])
        ogate = sb("ogate", [P, 2, GROUP])
        xTs = sb("xT", [P, 2, GROUP])
        resid = sb("resid", [P, GT, D])
        xn = sb("xn", [P, GT, D])
        stats = sb("stats", [P, GT, 6])
        moments = sb("moments", [P, GT, 2])
        lvar = sb("lvar", [P, GT])
        rstd = sb("rstd", [P, GT])

        s_w, s_wl = sem("weights"), sem("late_weights")
        s_zero, s_const, s_wo = sem("zeros"), sem("constants"), sem("wo_scaled")
        s_x = [sem("x0"), sem("x1")]
        (lr_mm, u_mm, q_mm, k_mm, v_mm, g_mm, at_mm, ot_mm, ms_mm, wo_mm, xt_mm) = map(sem, (
            "lr_mm", "u_mm", "q_mm", "k_mm", "v_mm", "g_mm", "at_mm", "ot_mm", "ms_mm", "wo_mm",
            "xt_mm"))
        (lr_ev, espl_d, lspl_d, val_d, egd_d, gexp_d, glog_d, sq_d, lms_d, wexp_d, lvar_d, rstd_d,
         xt_ev) = map(sem, ("lr_ev", "espl", "lspl", "val", "egd", "gexp", "glog", "sq", "lms",
                            "wexp", "lvar", "rstd", "xt_ev"))
        (sc_ev, wlog_d, on_d, uc_d, ns_d, y_d, st_d, mom_d, ln_d, gate_d, qg_d, kn_d) = map(
            sem, ("sc_ev", "wlog", "onorm", "uclamp", "negsig", "resid", "stats",
                  "moments", "ln", "gate", "qg", "kn"))
        og_d, keep_d, s_dz = sem("ogate"), sem("keep"), sem("dve_zeros")
        carry_d = sem("carry")

        LR_BANK, Q_BANK, K_BANK, EV0, EV1, AT_BANK, OT_BANK = 0, 1, 2, 3, 4, 5, 6

        with nc.Block() as block:
            def steps(eng, body):
                body(-1, 1, 0, True, False, False)
                body(0, 0, 0, True, True, False)
                with eng.Fori(0, (GROUPS - 2) // 2) as pair:
                    for k in range(2):
                        body(pair * 2 + (1 + k), 1 - k, pair + 1, True, True, True)
                body(GROUPS - 1, 1, None, False, True, True)
                body(GROUPS, 0, None, False, False, True)

            def past(i, first):
                return not isinstance(i, int) or i >= first

            @block.sync
            def _(sp):
                sp.wait_ge(s_zero, 2)
                for dst, src in ((gk1_s[:, 0:LOWRANK], Wgk1), (gk2_s[0:LOWRANK, :], Wgk2),
                                 (wq_s[:], Wq), (wk_s[:], Wk), (wv_s[:], Wv), (wg_s[:], Wg),
                                 (bgk_s[:], bgk2[:, None])):
                    sp.dma_start(dst, src).then_inc(s_w, 16)

                def body(i, p, er, early, mid, late):
                    e = 1 - p
                    if early:
                        if past(i, 1):
                            sp.wait_ge(g_mm, 2 * i)
                        sp.dma_start(xTs[:, e, :], xT[:, bass.ds((i + 1) * GROUP, GROUP)]
                                     ).then_inc(s_x[e], 16)
                        sp.dma_start(stream[:, bass.ds((i + 1) * GT, GT), 0:D],
                                     x[bass.ds((i + 1) * GROUP, GROUP), :].rearrange(
                                         "(t p) d -> p t d", p=P)).then_inc(s_x[e], 16)
                        if isinstance(i, int) and i == -1:
                            for dst, src in ((rms_s[0:DVA, :], rms_w[:, None]),
                                             (rms_s[DVA:P, :], rms_w[:, None]),
                                             (wo_s[:], Wo.rearrange("(c p) d -> p c d", p=P))):
                                sp.dma_start(dst, src).then_inc(s_wl, 16)
                steps(sp, body)

            @block.gpsimd
            def _(pool):
                nc.gpsimd.memset(gk1_s[:], 0.0).then_inc(s_zero, 1)
                nc.gpsimd.memset(gk2_s[:], 0.0).then_inc(s_zero, 1)
                nc.gpsimd.memset(eps[:], EPS)
                nc.gpsimd.memset(head_mean[:], 0.0)
                nc.gpsimd.memset(causal[:], 1.0)
                nc.gpsimd.memset(ident[:], 0.0).then_inc(s_zero, 1)
                pool.wait_ge(s_zero, 3)
                nc.gpsimd.affine_select(out=ident[:], in_=ident[:], compare_op=ALU.not_equal,
                                        fill=1.0, base=0, pattern=[[-1, P]], channel_multiplier=1)
                nc.gpsimd.affine_select(out=causal[:], in_=causal[:], compare_op=ALU.is_ge,
                                        fill=0.0, base=0, pattern=[[1, P]],
                                        channel_multiplier=-1).then_inc(s_zero, 1)
                pool.wait_ge(s_zero, 4)
                nc.gpsimd.memset(causal[0:SEQ, SEQ:P], 0.0).then_inc(s_zero, 1)
                pool.wait_ge(s_zero, 5)
                nc.gpsimd.memset(head_mean[0:DVA, 0:DVA], 1.0 / DVA).then_inc(s_zero, 1)
                pool.wait_ge(s_zero, 6)
                nc.gpsimd.memset(head_mean[DVA:P, DVA:P], 1.0 / DVA).then_inc(s_const, 1)
                pool.wait_ge(s_const, 1)

                def body(i, p, er, early, mid, late):
                    if late:
                        for c in range(2):
                            pool.wait_ge(on_d, 2 * i - 1 + c)
                            pool.wait_ge(wo_mm, i - 1)
                            nc.gpsimd.tensor_tensor(ogate[:, c, :], onorm[:, c, :],
                                                    gate[:, 1 - p, c, :], ALU.mult).then_inc(og_d, 1)
                        pool.wait_ge(ln_d, i)
                        nc.gpsimd.tensor_copy(stream[:, bass.ds((i - 1) * GT, GT), 0:D], xn[:]
                                              ).then_inc(keep_d, 1)
                steps(pool, body)

            @block.tensor
            def _(pe):
                pe.wait_ge(s_w, 16 * 7)
                pe.wait_ge(s_const, 1)
                mm = nc.tensor.matmul

                def body(i, p, er, early, mid, late):
                    e = 1 - p
                    if late:
                        pe.wait_ge(gate_d, 2 * (i + 1) if early or mid else 2 * GROUPS)
                        pe.wait_ge(y_d, i - 1)
                        pe.wait_ge(xt_ev, i - 1)
                        for c in range(2):
                            pe.wait_ge(sq_d, 2 * i - 1 + c)
                            mm(banks[:, EV0 + c, :], head_mean[:], square[:, c, :],
                               start=True, stop=True).then_inc(ms_mm, 1)

                    def scores_mm(t):
                        if t == 0:
                            pe.wait_ge(qg_d, i + 1)
                            pe.wait_ge(kn_d, i + 1)
                        if t > 0 or past(i, 1):
                            pe.wait_ge(sc_ev, i * GT + t)
                        mm(banks[:, AT_BANK, :], kn[:, p, t * P:(t + 1) * P],
                           qg[:, p, t].rearrange("p h c -> p (h c)"),
                           start=True, stop=True).then_inc(at_mm, 1)

                    def out_mm(t):
                        pe.wait_ge(sc_ev, i * GT + (t + 1))
                        if t == 0:
                            pe.wait_ge(val_d, 2 * (i + 1))
                            if past(i, 1):
                                pe.wait_ge(on_d, 2 * i)
                        for h in range(HA):
                            half = DVA * (h % 2)
                            last = mm(banks[half:half + DVA, OT_BANK + h // 2, t * P:(t + 1) * P],
                                      val[:, p, t, h * DVA:(h + 1) * DVA], scores[:, t % 2, h, :],
                                      start=True, stop=True)
                        last.then_inc(ot_mm, 1)

                    if mid:
                        scores_mm(0)
                    if early:
                        pe.wait_ge(s_x[e], 32 * (er + 1))
                        if past(i, 0):
                            pe.wait_ge(ns_d, i + 1)
                        mm(banks[:, LR_BANK, :], gk1_s[:], xTs[:, e, :],
                           start=True, stop=True).then_inc(lr_mm, 1)
                        mm(banks[:, Q_BANK, :], wq_s[:], xTs[:, e, :],
                           start=True, stop=True).then_inc(q_mm, 1)
                    if mid:
                        scores_mm(1)
                        out_mm(0)
                    if early:
                        mm(banks[:, K_BANK, :], wk_s[:], xTs[:, e, :],
                           start=True, stop=True).then_inc(k_mm, 1)
                        pe.wait_ge(lr_ev, i + 2)
                        mm(banks[:, LR_BANK, :], gk2_s[:], lowrank[:],
                           start=True, stop=True).then_inc(u_mm, 1)
                    if mid:
                        scores_mm(2)
                        out_mm(1)
                    if early:
                        if late:
                            pe.wait_ge(lms_d, 2 * i)
                        elif mid:
                            pe.wait_ge(gate_d, 2)
                        for c in range(2):
                            for t in range(2):
                                first = (2 * c + t) * P
                                last = mm(banks[:, EV0 + c, t * VD:(t + 1) * VD],
                                          xTs[:, e, first:first + P], wv_s[:],
                                          start=True, stop=True)
                            last.then_inc(v_mm, 1)
                    if mid:
                        scores_mm(3)
                    if late:
                        pe.wait_ge(s_wo, 1)
                        if early:
                            pe.wait_ge(val_d, 2 * (i + 1) + 1)
                        else:
                            pe.wait_ge(lms_d, 2 * i)
                        pe.wait_ge(og_d, 2 * i)
                        for t in range(GT):
                            for c in range(2):
                                last = mm(banks[:, EV0, t * P:(t + 1) * P],
                                          ogate[:, c, t * P:(t + 1) * P], wo_s[:, c, :],
                                          start=c == 0, stop=c == 1)
                        last.then_inc(wo_mm, 1)
                    if mid:
                        out_mm(2)
                    if early:
                        pe.wait_ge(val_d, 2 * (i + 1) + 2)
                        mm(banks[:, EV1, :], wg_s[:, 0:P], xTs[:, e, :],
                           start=True, stop=True).then_inc(g_mm, 1)
                        if late:
                            pe.wait_ge(y_d, i)
                        mm(banks[:, EV0, :], wg_s[:, P:VD], xTs[:, e, :],
                           start=True, stop=True).then_inc(g_mm, 1)
                    if mid:
                        out_mm(3)
                    if late:
                        pe.wait_ge(ln_d, i)
                        if early:
                            pe.wait_ge(gate_d, 2 * (i + 1) + 1)
                        for t in range(GT):
                            last = nc.tensor.transpose(banks[:, EV1, t * P:(t + 1) * P],
                                                       xn[:, t, :], ident[:])
                        last.then_inc(xt_mm, 1)
                steps(pe, body)

            @block.scalar
            def _(act):
                af = nc.scalar.activation
                nc.scalar.preload_act_table_set("natural_log_exp_and_others")
                act.wait_ge(s_const, 1)

                def body(i, p, er, early, mid, late):
                    e = 1 - p
                    if late:
                        for c in range(2):
                            act.wait_ge(ms_mm, 2 * i - 1 + c)
                            if not isinstance(i, int) or i > 1:
                                act.wait_ge(wlog_d, 2 * (i - 1) + c - (1 if c else 0))
                            af(lms[:, c, :], banks[:, EV0 + c, :], ACT.Ln, bias=eps[:]
                               ).then_inc(lms_d, 1)
                        for c in range(2):
                            act.wait_ge(wlog_d, 2 * i - 1 + c)
                            act.wait_ge(on_d, 2 * (i - 1))
                            af(wexp[:, c, :], wlog[:, c, :], ACT.Exp, scale=-1.0).then_inc(wexp_d, 1)
                    if early:
                        act.wait_ge(lr_mm, i + 2)
                        if past(i, 0):
                            act.wait_ge(u_mm, i + 1)
                        af(lowrank[:], banks[:, LR_BANK, :], ACT.Copy, scale=-1.0).then_inc(lr_ev, 1)
                        act.wait_ge(uc_d, i + 2)
                        af(espl[:], uclamp[:], ACT.Exp).then_inc(espl_d, 1)
                        act.wait_ge(espl_d, i + 2)
                        if past(i, 0):
                            act.wait_ge(ns_d, i + 1)
                        af(lspl[:], espl[:], ACT.Ln, bias=1.0).then_inc(lspl_d, 1)
                        for c in range(2):
                            act.wait_ge(v_mm, 2 * (i + 1) + 1 + c)
                            if past(i, 1):
                                act.wait_ge(ot_mm, i * GT)
                            af(val[:, e, 2 * c:2 * c + 2, :].rearrange("p t v -> p (t v)"),
                               banks[:, EV0 + c, :], ACT.Copy).then_inc(val_d, 1)
                        act.wait_ge(ns_d, i + 2)
                        if past(i, 0):
                            act.wait_ge(kn_d, i + 1)
                        for c, sign in enumerate((-1.0, 1.0)):
                            af(egd[:, c, :], negsig[:], ACT.Exp, scale=sign / GATE_NORM
                               ).then_inc(egd_d, 1)
                    if late:
                        act.wait_ge(mom_d, i)
                        af(lvar[:], moments[:, :, 1], ACT.Ln, bias=eps[:]).then_inc(lvar_d, 1)
                        act.wait_ge(lvar_d, i)
                        act.wait_ge(ln_d, i - 1)
                        af(rstd[:], lvar[:], ACT.Exp, scale=-0.5).then_inc(rstd_d, 1)
                    if early:
                        for c in range(2):
                            act.wait_ge(gate_d, 2 * (i + 1) + 1 + c)
                            if past(i, 0):
                                act.wait_ge(glog_d, 2 * (i + 1))
                            af(gexp[:, c, :], gate[:, e, c, :], ACT.Exp, scale=-1.0
                               ).then_inc(gexp_d, 1)
                        for c in range(2):
                            act.wait_ge(gexp_d, 2 * (i + 1) + 1 + c)
                            af(glog[:, e, c, :], gexp[:, c, :], ACT.Ln, bias=1.0).then_inc(glog_d, 1)
                    if mid:
                        act.wait_ge(ot_mm, (i + 1) * GT)
                        if past(i, 1):
                            act.wait_ge(ms_mm, 2 * i)
                        for c in range(2):
                            af(square[:, c, :], banks[:, OT_BANK + c, :], ACT.Square
                               ).then_inc(sq_d, 1)
                    if late:
                        act.wait_ge(xt_mm, i)
                        af(streamT[:, bass.ds((i - 1) * GROUP, GROUP)], banks[:, EV1, :], ACT.Copy
                           ).then_inc(xt_ev, 1)
                steps(act, body)

            @block.vector
            def _(dve):
                nc.vector.memset(qg[:], 0.0)
                nc.vector.memset(scores[:], 0.0).then_inc(s_dz, 1)
                dve.wait_ge(s_wl, 16 * 3)
                for c in range(2):
                    last = nc.vector.tensor_scalar(wo_s[:, c, :], wo_s[:, c, :], rms_s[:], None,
                                                   ALU.mult)
                last.then_inc(s_wo, 1)
                dve.wait_ge(s_w, 16 * 7)
                dve.wait_ge(s_const, 1)
                dve.wait_ge(s_dz, 1)
                keep = causal[:].bitcast(I32)[:, None, :].to_broadcast([P, HA, P])

                def body(i, p, er, early, mid, late):
                    e = 1 - p

                    def scores_ev(t):
                        dve.wait_ge(at_mm, i * GT + (t + 1))
                        if t > 1 or past(i, 1):
                            dve.wait_ge(ot_mm, i * GT + (t - 1))
                        dve.sem_inc(carry_d, 1)
                        nc.vector.copy_predicated(
                            scores[:, t % 2], keep,
                            banks[:, AT_BANK, :].rearrange("p (h c) -> p h c", h=HA)
                        ).then_inc(sc_ev, 1)

                    if mid:
                        scores_ev(0)
                    if late:
                        for c in range(2):
                            dve.wait_ge(lms_d, 2 * i - 1 + c)
                            dve.wait_ge(glog_d, 2 * i - 1 + c)
                            dve.wait_ge(wexp_d, 2 * (i - 1))
                            nc.vector.scalar_tensor_tensor(
                                wlog[:, c, :], lms[:, c, :], 0.5, glog[:, 1 - p, c, :],
                                ALU.mult, ALU.add).then_inc(wlog_d, 1)
                    if mid:
                        scores_ev(1)
                    if late:
                        for c in range(2):
                            dve.wait_ge(wexp_d, 2 * i - 1 + c)
                            dve.wait_ge(og_d, 2 * (i - 1))
                            nc.vector.tensor_tensor(onorm[:, c, :], banks[:, OT_BANK + c, :],
                                                    wexp[:, c, :], ALU.mult).then_inc(on_d, 1)
                    if early:
                        dve.wait_ge(u_mm, i + 2)
                        nc.vector.tensor_scalar(uclamp[:], banks[:, LR_BANK, :], bgk_s[:], CLAMP,
                                                ALU.subtract, ALU.min).then_inc(uc_d, 1)
                    if mid:
                        scores_ev(2)
                    if early:
                        dve.wait_ge(lspl_d, i + 2)
                        if past(i, 0):
                            dve.wait_ge(egd_d, 2 * (i + 1))
                        nc.vector.scalar_tensor_tensor(
                            negsig[:], banks[:, LR_BANK, :], bgk_s[:], lspl[:],
                            ALU.subtract, ALU.max).then_inc(ns_d, 1)
                    if mid:
                        scores_ev(3)
                    if late:
                        dve.wait_ge(wo_mm, i)
                        nc.vector.tensor_tensor(
                            resid[:], banks[:, EV0, :].rearrange("p (t d) -> p t d", t=GT),
                            stream[:, bass.ds((i - 1) * GT, GT), 0:D], ALU.add).then_inc(y_d, 1)
                        dve.wait_ge(y_d, i)
                        for t in range(GT):
                            last = nc.vector.bn_stats(stats[:, t, :], resid[:, t, :])
                        last.then_inc(st_d, 1)
                        dve.wait_ge(st_d, i)
                        dve.sem_inc(carry_d, 1)
                        for t in range(GT):
                            last = nc.vector.bn_aggr(moments[:, t, :], stats[:, t, :])
                        last.then_inc(mom_d, 1)
                    if early:
                        for c in range(2):
                            dve.wait_ge(g_mm, 2 * (i + 1) + 1 + c)
                            if past(i, 1):
                                dve.wait_ge(og_d, 2 * i)
                            nc.vector.tensor_scalar(gate[:, e, c, :], banks[:, EV1 - c, :],
                                                    SILU_CLAMP, None, ALU.max).then_inc(gate_d, 1)
                    if late:
                        dve.wait_ge(rstd_d, i)
                        dve.wait_ge(xt_mm, i - 1)
                        dve.wait_ge(keep_d, i - 1)
                        for t in range(GT):
                            last = nc.vector.tensor_scalar(
                                xn[:, t, :], resid[:, t, :], moments[:, t, 0:1],
                                rstd[:, t:t + 1], ALU.subtract, ALU.mult)
                        last.then_inc(ln_d, 1)
                    if early:
                        dve.wait_ge(q_mm, i + 2)
                        dve.wait_ge(egd_d, 2 * (i + 1) + 1)
                        if past(i, 1):
                            dve.wait_ge(at_mm, i * GT)
                        for h in range(HA):
                            rows = slice(h * DKA, (h + 1) * DKA)
                            last = nc.vector.scalar_tensor_tensor(
                                qg[rows, e, :, h, :],
                                banks[rows, Q_BANK, :].rearrange("p (t c) -> p t c", t=GT),
                                float(DKA) ** -0.5,
                                egd[rows, 0, :].rearrange("p (t c) -> p t c", t=GT),
                                ALU.mult, ALU.mult)
                        last.then_inc(qg_d, 1)
                        dve.wait_ge(k_mm, i + 2)
                        dve.wait_ge(egd_d, 2 * (i + 1) + 2)
                        nc.vector.tensor_tensor(kn[:, e, :], banks[:, K_BANK, :], egd[:, 1, :],
                                                ALU.mult).then_inc(kn_d, 1)
                steps(dve, body)


def cross_attention(nc, ctxT, mask, wq, bq, wk, bk, wv, bv, wo, bo, switch_w, sorted_x,
                    stream, streamT, ident, eps, banks, logits):
    from contextlib import ExitStack
    ctx = ExitStack()
    with ctx:
        def sb(name, shape, dt=F32):
            return ctx.enter_context(nc.sbuf_tensor("b_" + name, shape, dt))

        def sem(name):
            return ctx.enter_context(nc.semaphore("b_" + name))

        ROWG = 4
        PAIRS = HX // 2
        DV = DX + 1
        SCALE = float(DX) ** -0.5
        wq_s, wk_s, wv_s, wo_s = (sb(n, [P, D]) for n in ("wq", "wk", "wv", "wo"))
        wv_par = sb("wv_par", [P, 2, SEQ])
        sw_s = sb("sw", [P, EXPERTS])
        bq_s, bk_s = sb("bq", [P, 1]), sb("bk", [P, 1])
        bv_s, bo_s = sb("bv", [P, D]), sb("bo", [P, D])
        headsel = sb("headsel", [P, ROWG])
        bksel = sb("bksel", [P, ROWG])
        mask_s = sb("mask", [P, TILES, SEQ], U8)
        padding = sb("padding", [P, ROW])
        ctx_s = sb("ctx", [P, 2, GROUP])
        qT = sb("qT", [P, 2, GROUP])
        kbd = sb("kbd", [P, 2, GB, ROWG, SEQ])
        vbd = sb("vbd", [P, 2, GB, PAIRS, 2, DV])
        masked = sb("masked", [P, GT, SEQ])
        kept = sb("kept", [P, GT, SEQ])
        limit = sb("limit", [P, 2, GT, SEQ])
        xb = sb("xb", [P, 2, GT, D])
        prob = sb("prob", [P, 2, HX, SEQ])
        top = sb("top", [P, HX])
        probT = sb("probT", [P, 2, PAIRS, P])
        rsum = sb("rsum", [P, HX])
        attn = sb("attn", [P, 2, D])
        attnT = sb("attnT", [P, 2, P])
        resid = sb("resid", [P, D])
        stats = sb("stats", [P, 6])
        moments = sb("moments", [P, 2])
        lvar, rstd = sb("lvar", [P, 1]), sb("rstd", [P, 1])
        xn = sb("xn", [P, 2, D])
        xnT = sb("xnT", [P, 2, P])

        s_w, s_m, s_z, s_init, s_const = map(sem, ("weights", "mask", "zero", "init", "const"))
        s_zf = sem("zero_fill")
        carry_d = sem("carry")
        s_c = [sem("ctx0"), sem("ctx1")]
        (q_mm, k_mm, v_mm, s_mm, tp_mm, av_mm, at_mm, wo_mm, xt_mm, lg_mm) = map(sem, (
            "q_mm", "k_mm", "v_mm", "s_mm", "tp_mm", "av_mm", "at_mm", "wo_mm", "xt_mm", "lg_mm"))
        (exp_d, pt_ev, at_ev, lvar_d, rstd_d, xt_ev, lg_ev, k_ev) = map(sem, (
            "exp", "pt_ev", "at_ev", "lvar", "rstd", "xt_ev", "lg_ev", "k_ev"))
        (min_d, max_d, sub_d, rs_d, an_d, y_d, st_d, mom_d, ln_d, q_ev, v_ev) = map(sem, (
            "min", "max", "sub", "rsum", "attn", "resid", "stats", "moments", "ln", "q_ev", "v_ev"))
        (mk_d, lim_d, xb_d, keep_d) = map(sem, ("masked", "limit", "xb", "keep"))

        T0, T1, O_BANK, M_BANK = 4, 5, 6, 7
        AT_COL, WO_COL, XT_COL, LG_COL = 256, 0, P, 2 * P
        HEADS4 = ROWG * SEQ
        BODY = 2 * GT

        with nc.Block() as block:
            def slots(eng, slot):
                for t in range(BODY):
                    slot(t, 0, t)
                with eng.Fori(1, TILES // BODY - 1) as it:
                    for k in range(BODY):
                        slot(it * BODY + k, it, k)
                for t in range(TILES - BODY, TILES + 5):
                    slot(t, t // BODY, t % BODY)

            def there(t, lag):
                return not isinstance(t, int) or 0 <= t - lag < TILES

            def past(t, n):
                return not isinstance(t, int) or t >= n

            def feeds(t, k, place):
                return k % GT == place and (not isinstance(t, int) or t // GT + 1 < GROUPS)

            @block.sync
            def _(sp):
                sp.dma_start(ctx_s[:, 0, :], ctxT[:, 0:GROUP]).then_inc(s_c[0], 16)
                for dst, src in ((wq_s[:], wq), (wk_s[:], wk), (wv_s[:], wv), (wo_s[:], wo),
                                 (sw_s[:], switch_w), (bq_s[:], bq[:, None]), (bk_s[:], bk[:, None]),
                                 (bv_s[:], bv[None, :].to_broadcast([P, D])),
                                 (bo_s[:], bo[None, :].to_broadcast([P, D]))):
                    sp.dma_start(dst, src).then_inc(s_w, 16)
                sp.dma_start(mask_s[:], mask.rearrange("(t p) k -> p t k", p=P)).then_inc(s_m, 16)
                sp.wait_ge(s_z, 2)
                sp.dma_start(sorted_x.rearrange("(t p) d -> p t d", p=P),
                             padding[:, None, :].to_broadcast([P, XTILES, ROW])).then_inc(s_zf, 16)

                def slot(t, it, k):
                    if feeds(t, k, 0):
                        g, e = 2 * it + k // GT, 1 - k // GT
                        if past(g, 1):
                            sp.wait_ge(v_mm, g)
                        sp.dma_start(ctx_s[:, e, :], ctxT[:, bass.ds((g + 1) * GROUP, GROUP)]
                                     ).then_inc(s_c[e], 16)
                slots(sp, slot)
                sp.wait_ge(s_zf, 16)

            @block.gpsimd
            def _(pool):
                nc.gpsimd.memset(padding[:, 0:D + 1], 0.0).then_inc(s_z, 1)
                nc.gpsimd.memset(padding[:, D + 1:ROW].bitcast(I32), TOKENS).then_inc(s_z, 1)
                pool.wait_ge(s_m, 16)
                pool.wait_ge(s_w, 16 * 9)

                def prepare(g, e):
                    if past(g, 1):
                        pool.wait_ge(lim_d, g)
                    nc.gpsimd.tensor_copy(masked[:], mask_s[:, bass.ds(g * GT, GT), :]
                                          ).then_inc(mk_d, 1)
                    pool.wait_ge(mk_d, 3 * g + 1)
                    pool.sem_inc(carry_d, 1)
                    nc.gpsimd.tensor_scalar(kept[:], masked[:], 0.0, KEEP, ALU.is_equal, ALU.mult
                                            ).then_inc(mk_d, 1)
                    if past(g, 2):
                        pool.wait_ge(min_d, (g - 1) * GT)
                        pool.sem_inc(carry_d, 1)
                    nc.gpsimd.tensor_scalar(limit[:, e], masked[:], NEG, 0.0, ALU.mult, ALU.add
                                            ).then_inc(mk_d, 1)
                    pool.wait_ge(mk_d, 3 * g + 3)
                    nc.gpsimd.tensor_tensor(limit[:, e], limit[:, e], kept[:], ALU.add
                                            ).then_inc(lim_d, 1)
                    if past(g, 2):
                        pool.wait_ge(y_d, (g - 1) * GT)
                    nc.gpsimd.tensor_tensor(xb[:, e], stream[:, bass.ds(g * GT, GT), 0:D],
                                            bo_s[:, None, :].to_broadcast([P, GT, D]), ALU.add
                                            ).then_inc(xb_d, 1)

                def slot(t, it, k):
                    if there(t, 3):
                        pool.wait_ge(ln_d, t - 2)
                        nc.gpsimd.tensor_copy(stream[:, bass.ds(t - 3, 1), 0:D],
                                              xn[:, (k - 3) % 2, None, :]).then_inc(keep_d, 1)
                    if feeds(t, k, 1):
                        prepare(2 * it + k // GT + 1, 1 - k // GT)
                prepare(0, 0)
                slots(pool, slot)

            @block.tensor
            def _(pe):
                pe.wait_ge(s_w, 16 * 9)
                pe.wait_ge(s_const, 1)
                mm = nc.tensor.matmul

                def project_qk(g, e, turn):
                    mm(banks[:, T0, :], wq_s[:], streamT[:, bass.ds(g * GROUP, GROUP)],
                       start=True, stop=True).then_inc(q_mm, 1)
                    pe.wait_ge(s_c[e], 16 * turn)
                    mm(banks[:, T1, :], wk_s[:], ctx_s[:, e, :], start=True, stop=True
                       ).then_inc(k_mm, 1)

                def project_v(e):
                    for b in range(GB):
                        for par in range(2):
                            last = mm(banks[SEQ * par:SEQ * par + SEQ, T0, b * SEQ:(b + 1) * SEQ],
                                      ctx_s[:, e, b * SEQ:(b + 1) * SEQ], wv_par[:, par, :],
                                      start=True, stop=True)
                    last.then_inc(v_mm, 1)

                def slot(t, it, k):
                    k1, k2, k3 = ((k - n) % BODY for n in (1, 2, 3))
                    for b in range(2):
                        if there(t, 0):
                            if b == 0:
                                pe.wait_ge(q_ev, 2 * it + k // GT + 1)
                                pe.wait_ge(k_ev, 2 * it + k // GT + 1)
                                if past(t, 1):
                                    pe.wait_ge(min_d, t)
                            seq = 2 * (k % GT) + b
                            for r in range(ROWG):
                                rows = slice(32 * r, 32 * r + 32)
                                last = mm(banks[SEQ * b:SEQ * b + SEQ, r, 0:HEADS4],
                                          qT[rows, k // GT, seq * SEQ:(seq + 1) * SEQ],
                                          kbd[rows, k // GT, seq].rearrange("p h k -> p (h k)"),
                                          start=True, stop=True)
                            if b == 1:
                                last.then_inc(s_mm, 1)
                        if b == 0 and there(t, 3):
                            pe.wait_ge(at_ev, t - 2)
                            if past(t, 4):
                                pe.wait_ge(xt_ev, t - 3)
                            mm(banks[:, M_BANK, WO_COL:WO_COL + D], attnT[:, k3 % 2, :], wo_s[:],
                               start=True, stop=True).then_inc(wo_mm, 1)
                    if there(t, 4):
                        if there(t, 3):
                            pe.wait_ge(y_d, t - 2)
                        pe.wait_ge(xt_ev, t - 3)
                        mm(banks[:, M_BANK, LG_COL:LG_COL + EXPERTS], xnT[:, k % 2, :], sw_s[:],
                           start=True, stop=True).then_inc(lg_mm, 1)
                    if there(t, 2):
                        pe.wait_ge(pt_ev, 2 * (t - 1))
                        pe.wait_ge(v_ev, 2 * it + (k - 2) // GT + 1)
                        if past(t, 3):
                            pe.wait_ge(at_ev, t - 2)
                        for b in range(2):
                            for j in range(PAIRS):
                                col = j * 2 * DV
                                last = mm(banks[SEQ * b:SEQ * b + SEQ, O_BANK, col:col + 2 * DV],
                                          probT[:, k2 % 2, j, SEQ * b:SEQ * b + SEQ],
                                          vbd[:, k2 // GT, 2 * (k2 % GT) + b, j].rearrange(
                                              "p h d -> p (h d)"),
                                          start=True, stop=True)
                        last.then_inc(av_mm, 1)
                    if there(t, 1):
                        pe.wait_ge(exp_d, t)
                        if past(t, 2):
                            pe.wait_ge(pt_ev, 2 * (t - 1))
                        if feeds(t, k, 2):
                            pe.wait_ge(q_ev, 2 * it + k // GT + 2)
                            pe.wait_ge(k_ev, 2 * it + k // GT + 2)
                        if feeds(t, k, 3):
                            pe.wait_ge(v_ev, 2 * it + k // GT + 2)
                        for j in range(PAIRS):
                            last = nc.tensor.transpose(
                                banks[:, T0 + j // 4, (j % 4) * P:(j % 4 + 1) * P],
                                prob[:, k1 % 2, 2 * j:2 * j + 2, :].rearrange("p h k -> p (h k)"),
                                ident[:])
                            if j % 4 == 3:
                                last.then_inc(tp_mm, 1)
                    if there(t, 3):
                        pe.wait_ge(ln_d, t - 2)
                        if there(t, 4):
                            pe.wait_ge(lg_ev, t - 3)
                        nc.tensor.transpose(banks[:, M_BANK, XT_COL:XT_COL + P],
                                            xn[:, k3 % 2, :], ident[:]).then_inc(xt_mm, 1)
                    if there(t, 2):
                        pe.wait_ge(an_d, t - 1)
                        nc.tensor.transpose(banks[:, O_BANK, AT_COL:AT_COL + P],
                                            attn[:, k2 % 2, :], ident[:]).then_inc(at_mm, 1)
                    if feeds(t, k, 1):
                        pe.wait_ge(pt_ev, 2 * t)
                        project_qk(2 * it + k // GT + 1, 1 - k // GT, it + 1 + k // GT)
                    if feeds(t, k, 2):
                        pe.wait_ge(pt_ev, 2 * t)
                        project_v(1 - k // GT)

                project_qk(0, 0, 1)
                pe.wait_ge(q_ev, 1)
                pe.wait_ge(k_ev, 1)
                project_v(0)
                pe.wait_ge(v_ev, 1)
                slots(pe, slot)

            @block.scalar
            def _(act):
                af = nc.scalar.activation
                nc.scalar.preload_act_table_set("natural_log_exp_and_others")
                act.wait_ge(s_const, 1)

                def keys_ev(g, e):
                    act.wait_ge(k_mm, g + 1)
                    if past(g, 2):
                        act.wait_ge(s_mm, (g - 1) * GT)
                    for h in range(ROWG):
                        last = af(kbd[:, e, :, h, :],
                                  banks[:, T1, :].rearrange("p (s k) -> p s k", s=GB),
                                  ACT.Identity, bias=bksel[:, h:h + 1], scale=headsel[:, h:h + 1])
                    last.then_inc(k_ev, 1)

                def slot(t, it, k):
                    k1, k2, k3 = ((k - n) % BODY for n in (1, 2, 3))
                    if there(t, 1):
                        act.wait_ge(sub_d, t)
                        af(prob[:, k1 % 2], prob[:, k1 % 2], ACT.Exp).then_inc(exp_d, 1)
                    if there(t, 3):
                        act.wait_ge(mom_d, t - 2)
                        af(lvar[:], moments[:, 1:2], ACT.Ln, bias=eps[:]).then_inc(lvar_d, 1)
                        act.wait_ge(lvar_d, t - 2)
                        af(rstd[:], lvar[:], ACT.Exp, scale=-0.5).then_inc(rstd_d, 1)
                    if there(t, 4):
                        act.wait_ge(lg_mm, t - 3)
                        af(logits[:, bass.ds(t - 4, 1), :],
                           banks[:, M_BANK, None, LG_COL:LG_COL + EXPERTS], ACT.Copy
                           ).then_inc(lg_ev, 1)
                    if there(t, 1):
                        if past(t, 3):
                            act.wait_ge(av_mm, t - 2)
                        for c in range(2):
                            act.wait_ge(tp_mm, 2 * (t - 1) + 1 + c)
                            af(probT[:, k1 % 2, 4 * c:4 * c + 4, :].rearrange("p j q -> p (j q)"),
                               banks[:, T0 + c, :], ACT.Copy).then_inc(pt_ev, 1)
                    if there(t, 3):
                        act.wait_ge(xt_mm, t - 2)
                        if past(t, 5):
                            act.wait_ge(lg_mm, t - 4)
                        af(xnT[:, k3 % 2, :], banks[:, M_BANK, XT_COL:XT_COL + P], ACT.Copy
                           ).then_inc(xt_ev, 1)
                    if there(t, 2):
                        act.wait_ge(at_mm, t - 1)
                        if past(t, 4):
                            act.wait_ge(wo_mm, t - 3)
                        af(attnT[:, k2 % 2, :], banks[:, O_BANK, AT_COL:AT_COL + P], ACT.Copy
                           ).then_inc(at_ev, 1)
                    if feeds(t, k, 1):
                        keys_ev(2 * it + k // GT + 1, 1 - k // GT)
                keys_ev(0, 0)
                slots(act, slot)

            @block.vector
            def _(dve):
                nc.vector.memset(vbd[:], 0.0).then_inc(s_init, 1)
                nc.vector.tensor_reduce(
                    headsel[:], ident[:].rearrange("p (r h d) -> p h r d", r=4, h=ROWG),
                    AX.XY, ALU.add).then_inc(s_init, 1)
                dve.wait_ge(s_init, 2)
                for par in range(2):
                    half = slice(SEQ * par, SEQ * par + SEQ)
                    nc.vector.memset(vbd[half, :, :, :, par, DX], 1.0)
                dve.wait_ge(s_w, 16 * 9)
                nc.vector.tensor_copy(
                    wv_par[:].rearrange("p h (j d) -> p h j d", j=PAIRS),
                    wv_s[:].rearrange("p (j h d) -> p h j d", j=PAIRS, h=2))
                nc.vector.tensor_scalar(bksel[:], headsel[:], bk_s[:], None, ALU.mult
                                        ).then_inc(s_const, 1)

                def queries_ev(g, e):
                    dve.wait_ge(q_mm, g + 1)
                    if past(g, 2):
                        dve.wait_ge(s_mm, (g - 1) * GT)
                    nc.vector.tensor_scalar(qT[:, e, :], banks[:, T0, :], bq_s[:], SCALE,
                                            ALU.add, ALU.mult).then_inc(q_ev, 1)

                def values_ev(g, e):
                    if past(g, 2):
                        dve.wait_ge(av_mm, (g - 1) * GT)
                    dve.wait_ge(v_mm, g + 1)
                    for par in range(2):
                        half = slice(SEQ * par, SEQ * par + SEQ)
                        last = nc.vector.tensor_tensor(
                            vbd[half, e, :, :, par, 0:DX],
                            banks[half, T0, :].rearrange("p (s j d) -> p s j d", s=GB, j=PAIRS),
                            bv_s[half, :].rearrange("p (j h d) -> p j h d", j=PAIRS, h=2)[
                                :, None, :, par, :].to_broadcast([SEQ, GB, PAIRS, DX]), ALU.add)
                    last.then_inc(v_ev, 1)

                def slot(t, it, k):
                    k1, k2, k3 = ((k - n) % BODY for n in (1, 2, 3))
                    if there(t, 3):
                        dve.wait_ge(wo_mm, t - 2)
                        if k3 % GT == 0:
                            dve.wait_ge(xb_d, 2 * it + (k - 3) // GT + 1)
                        nc.vector.tensor_tensor(resid[:], banks[:, M_BANK, WO_COL:WO_COL + D],
                                                xb[:, k3 // GT, k3 % GT, :], ALU.add
                                                ).then_inc(y_d, 1)
                        dve.wait_ge(y_d, t - 2)
                        nc.vector.bn_stats(stats[:], resid[:]).then_inc(st_d, 1)
                        dve.wait_ge(st_d, t - 2)
                        dve.sem_inc(carry_d, 1)
                        nc.vector.bn_aggr(moments[:], stats[:]).then_inc(mom_d, 1)
                        dve.wait_ge(rstd_d, t - 2)
                        if past(t, 5):
                            dve.wait_ge(xt_mm, t - 4)
                            dve.wait_ge(keep_d, t - 4)
                        nc.vector.tensor_scalar(xn[:, k3 % 2, :], resid[:], moments[:, 0:1],
                                                rstd[:], ALU.subtract, ALU.mult).then_inc(ln_d, 1)
                    p_all = prob[:, k % 2]
                    if there(t, 0):
                        dve.wait_ge(s_mm, t + 1)
                        if k % GT == 0:
                            dve.wait_ge(lim_d, 2 * it + k // GT + 1)
                        if past(t, 2):
                            dve.wait_ge(tp_mm, 2 * (t - 1))
                        nc.vector.tensor_tensor(
                            p_all.rearrange("p (r h) k -> p r h k", r=ROWG),
                            banks[:, 0:ROWG, 0:HEADS4].rearrange(
                                "p r (h k) -> p r h k", h=ROWG),
                            limit[:, k // GT, k % GT, None, None, :].to_broadcast(
                                [P, ROWG, ROWG, SEQ]), ALU.min).then_inc(min_d, 1)
                        dve.wait_ge(min_d, t + 1)
                        nc.vector.reduce_max(top[:], p_all, AX.X).then_inc(max_d, 1)
                    if there(t, 2):
                        dve.wait_ge(av_mm, t - 1)
                        o = banks[:, O_BANK, 0:HX * DV].rearrange(
                            "p (h d) -> p h d", h=HX)
                        nc.vector.reciprocal(rsum[:], o[:, :, DX]).then_inc(rs_d, 1)
                        dve.wait_ge(rs_d, t - 1)
                        if past(t, 4):
                            dve.wait_ge(at_mm, t - 3)
                        nc.vector.tensor_tensor(
                            attn[:, k2 % 2, :].rearrange("p (h d) -> p h d", h=HX), o[:, :, 0:DX],
                            rsum[:, :, None].to_broadcast([P, HX, DX]), ALU.mult
                        ).then_inc(an_d, 1)
                    if there(t, 0):
                        dve.wait_ge(max_d, t + 1)
                        nc.vector.tensor_tensor(p_all, p_all,
                                                top[:, :, None].to_broadcast([P, HX, SEQ]),
                                                ALU.subtract).then_inc(sub_d, 1)
                    if feeds(t, k, 1):
                        queries_ev(2 * it + k // GT + 1, 1 - k // GT)
                    if feeds(t, k, 2):
                        values_ev(2 * it + k // GT + 1, 1 - k // GT)
                queries_ev(0, 0)
                values_ev(0, 0)
                slots(dve, slot)


def experts(nc, switch_b, w1, b1T, w2, b2, sorted_x, out, stream, ident, eps, banks, logits):
    from contextlib import ExitStack
    with ExitStack() as ctx:
        def sb(name, shape, dt=F32):
            return ctx.enter_context(nc.sbuf_tensor("c_" + name, shape, dt))

        w1_s = sb("w1", [P, EXPERTS, FF])
        b1_s = sb("b1", [P, EXPERTS, FC])
        w2_s = sb("w2", [P, EXPERTS, FC, D])
        b2_s = sb("b2", [P, EXPERTS, D])
        tile_expert = sb("tile_expert", [P, XTILES], I32)
        route(nc, switch_b, w1, b1T, w2, b2, w1_s, b1_s, w2_s, b2_s, tile_expert, sorted_x,
              stream, banks, logits)
        expert_tiles(nc, w1_s, b1_s, w2_s, b2_s, tile_expert, sorted_x, out, ident, eps, banks)


def route(nc, switch_b, w1, b1T, w2, b2, w1_s, b1_s, w2_s, b2_s, tile_expert, sorted_x,
          stream, banks, logits):
    from contextlib import ExitStack
    ctx = ExitStack()
    with ctx:
        def sb(name, shape, dt=F32):
            return ctx.enter_context(nc.sbuf_tensor("c_" + name, shape, dt))

        def sem(name):
            return ctx.enter_context(nc.semaphore("c_" + name))

        COLS = TILES * EXPERTS
        sb_s = sb("switch_b", [P, EXPERTS])
        ones = sb("ones", [P, P])
        before = sb("before", [P, P])
        count_i = sb("count_i", [P, P], I32)
        count = sb("count", [P, P])
        full_at = sb("full_at", [P, TILES])
        late_e = sb("late_e", [P, EXPERTS])
        token = sb("token", [P, TILES], I32)
        going = sb("going", [P, EXPERTS, TILES])
        prob = sb("prob", [P, TILES, EXPERTS])
        top = sb("top", [P, TILES])
        rsum = sb("rsum", [P, TILES])
        gate = sb("gate", [P, TILES])
        choice = sb("choice", [P, TILES])
        cand = sb("cand", [P, TILES, EXPERTS])
        onehot = sb("onehot", [P, TILES, EXPERTS])
        total = sb("total", [P, EXPERTS, TILES])
        upto = sb("upto", [P, EXPERTS, TILES])
        excl = sb("excl", [P, EXPERTS, TILES])
        opens = sb("opens", [P, EXPERTS, TILES])
        etiles = sb("etiles", [P, EXPERTS])
        etend = sb("etend", [P, EXPERTS])
        etfirst = sb("etfirst", [P, EXPERTS])
        rank = sb("rank", [P, TILES, EXPERTS])
        slot_f = sb("slot_f", [P, TILES])
        slot_i = sb("slot_i", [P, TILES], I32)
        passed = sb("passed", [P, XTILES, EXPERTS])
        te = sb("te", [P, XTILES])

        s_sb, s_w, s_const, s_iota = map(sem, ("switch_b", "weights", "const", "iota"))
        v, s_exp, s_mm, s_slot, s_meta, s_scat = map(sem, (
            "vector_step", "exp", "rank_mm", "slot", "meta", "scatter"))
        RANK_BANK, TOTAL_BANK = 0, 1

        with nc.Block() as block:
            @block.sync
            def _(sp):
                sp.dma_start(sb_s[:], switch_b[None, :].to_broadcast([P, EXPERTS])
                             ).then_inc(s_sb, 16)
                sp.dma_start(w1_s[:], w1.rearrange("e d f -> d e f")).then_inc(s_w, 16)
                sp.dma_start(w2_s[:], w2.rearrange("e (c p) d -> p e c d", p=P)).then_inc(s_w, 16)
                sp.dma_start(b2_s[:], b2[None, :, :].to_broadcast([P, EXPERTS, D])
                             ).then_inc(s_w, 16)
                sp.dma_start(b1_s[:], b1T.rearrange("p (e c) -> p e c", c=FC)).then_inc(s_w, 16)
                sp.wait_ge(s_w, 16 * 4)

            @block.gpsimd
            def _(pool):
                nc.gpsimd.iota(token[:], pattern=[[P, TILES]], base=0, channel_multiplier=1
                               ).then_inc(s_iota, 1)
                nc.gpsimd.iota(count_i[:], pattern=[[1, P]], base=0, channel_multiplier=0
                               ).then_inc(s_iota, 1)
                nc.gpsimd.memset(ones[:], 1.0)
                nc.gpsimd.memset(before[:], 1.0)
                nc.gpsimd.memset(going[:], 1.0).then_inc(s_iota, 1)
                pool.wait_ge(s_iota, 3)
                nc.gpsimd.memset(going[:, :, 0], 0.0)
                nc.gpsimd.affine_select(out=before[:], in_=before[:], compare_op=ALU.is_ge,
                                        fill=0.0, base=-1, pattern=[[1, P]],
                                        channel_multiplier=-1).then_inc(s_const, 1)
                pool.wait_ge(s_slot, 1)
                pool.wait_ge(s_meta, 2)
                for t in range(TILES):
                    nc.gpsimd.indirect_dma_start(
                        out=sorted_x[:, :],
                        out_offset=bass.IndirectOffsetOnAxis(ap=slot_i[:, t:t + 1], axis=0),
                        in_=stream[:, t, :], in_offset=None).then_inc(s_scat, 16)
                pool.wait_ge(s_scat, 16 * TILES)

            @block.tensor
            def _(pe):
                pe.wait_ge(s_const, 1)
                pe.wait_ge(v, 9)
                flat = onehot[:].rearrange("p t e -> p (t e)")
                nc.tensor.matmul(banks[:, TOTAL_BANK, :], ones[:], flat, start=True, stop=True
                                 ).then_inc(s_mm, 1)
                nc.tensor.matmul(banks[:, RANK_BANK, :], before[:], flat, start=True, stop=True
                                 ).then_inc(s_mm, 1)

            @block.scalar
            def _(act):
                nc.scalar.preload_act_table_set("natural_log_exp_and_others")
                act.wait_ge(v, 3)
                nc.scalar.activation(prob[:], prob[:], ACT.Exp).then_inc(s_exp, 1)

            @block.vector
            def _(dve):
                tt, ts, stt = (nc.vector.tensor_tensor, nc.vector.tensor_scalar,
                               nc.vector.scalar_tensor_tensor)

                def per_tile(row):
                    return row[:, :, None].to_broadcast([P, TILES, EXPERTS])

                def done(instruction, step):
                    instruction.then_inc(v, 1)
                    dve.wait_ge(v, step)

                dve.wait_ge(s_iota, 2)
                nc.vector.tensor_copy(count[:], count_i[:]).then_inc(s_meta, 1)
                nc.vector.tensor_copy(stream[:, :, D + 1].bitcast(I32), token[:])
                dve.wait_ge(s_sb, 16)
                done(tt(prob[:], logits[:], sb_s[:, None, :].to_broadcast([P, TILES, EXPERTS]),
                        ALU.add), 1)
                done(nc.vector.reduce_max(top[:], prob[:], AX.X), 2)
                done(tt(prob[:], prob[:], per_tile(top), ALU.subtract), 3)
                dve.wait_ge(s_meta, 1)
                ts(late_e[:], count[:, 0:EXPERTS], float(EXPERTS), None, ALU.add)
                ts(full_at[:], count[:, 0:TILES], float(P), None, ALU.mult)
                dve.wait_ge(s_exp, 1)
                done(nc.vector.reduce_sum(rsum[:], prob[:], AX.X), 4)
                done(nc.vector.reciprocal(rsum[:], rsum[:]), 5)
                done(tt(prob[:], prob[:], per_tile(rsum), ALU.mult), 6)
                done(nc.vector.reduce_max(gate[:], prob[:], AX.X), 7)
                nc.vector.tensor_copy(stream[:, :, D], gate[:]).then_inc(s_meta, 1)
                tt(cand[:], prob[:], per_tile(gate), ALU.is_equal).then_inc(s_exp, 1)
                dve.wait_ge(s_exp, 2)
                stt(cand[:], cand[:], -float(EXPERTS),
                    late_e[:, None, :].to_broadcast([P, TILES, EXPERTS]), ALU.mult, ALU.add
                    ).then_inc(s_exp, 1)
                dve.wait_ge(s_exp, 3)
                done(nc.vector.tensor_reduce(choice[:], cand[:], AX.X, ALU.min), 8)
                done(tt(onehot[:], count[:, None, 0:EXPERTS].to_broadcast([P, TILES, EXPERTS]),
                        per_tile(choice), ALU.is_equal), 9)
                dve.wait_ge(s_mm, 1)
                done(nc.vector.tensor_copy(total[:].rearrange("p e t -> p t e"),
                                           banks[:, TOTAL_BANK, :].rearrange(
                                               "p (t e) -> p t e", t=TILES)), 10)
                dve.wait_ge(s_const, 1)
                done(nc.vector.tensor_tensor_scan(
                    upto[:].rearrange("p e t -> p (e t)"), going[:].rearrange("p e t -> p (e t)"),
                    total[:].rearrange("p e t -> p (e t)"), 0.0, ALU.mult, ALU.add), 11)
                tt(excl[:], upto[:], total[:], ALU.subtract)
                done(tt(opens[:], upto[:, :, TILES - 1:TILES].to_broadcast([P, EXPERTS, TILES]),
                        full_at[:, None, :].to_broadcast([P, EXPERTS, TILES]), ALU.is_gt), 12)
                done(nc.vector.reduce_sum(etiles[:], opens[:], AX.X), 13)
                done(nc.vector.tensor_tensor_scan(etend[:], ones[:, 0:EXPERTS], etiles[:], 0.0,
                                                  ALU.mult, ALU.add), 14)
                done(tt(etfirst[:], etend[:], etiles[:], ALU.subtract), 15)
                done(stt(excl[:], etfirst[:, :, None].to_broadcast([P, EXPERTS, TILES]), float(P),
                         excl[:], ALU.mult, ALU.add), 16)
                dve.wait_ge(s_mm, 2)
                done(tt(rank[:], banks[:, RANK_BANK, :].rearrange("p (t e) -> p t e", t=TILES),
                        excl[:].rearrange("p e t -> p t e"), ALU.add), 17)
                done(tt(rank[:], rank[:], onehot[:], ALU.mult), 18)
                done(nc.vector.reduce_sum(slot_f[:], rank[:], AX.X), 19)
                nc.vector.tensor_copy(slot_i[:], slot_f[:]).then_inc(s_slot, 1)
                done(tt(passed[:], count[:, 0:XTILES, None].to_broadcast([P, XTILES, EXPERTS]),
                        etend[:, None, :].to_broadcast([P, XTILES, EXPERTS]), ALU.is_ge), 20)
                done(nc.vector.reduce_sum(te[:], passed[:], AX.X), 21)
                ts(tile_expert[:], te[:], float(EXPERTS - 1), None, ALU.min)


def expert_tiles(nc, w1_s, b1_s, w2_s, b2_s, tile_expert, sorted_x, out, ident, eps, banks):
    from contextlib import ExitStack
    ctx = ExitStack()
    with ctx:
        def sb(name, shape, dt=F32):
            return ctx.enter_context(nc.sbuf_tensor("d_" + name, shape, dt))

        def sem(name):
            return ctx.enter_context(nc.semaphore("d_" + name))

        LOADS = 6
        BODY = 12
        rows = sb("rows", [P, LOADS, ROW])
        xT = sb("xT", [P, 2, P])
        w1_now = sb("w1_now", [P, 2, FF])
        b1_now = sb("b1_now", [P, 2, FC])
        hT = sb("hT", [P, 2, FC, P])
        y = sb("y", [P, D])
        resid = sb("resid", [P, 2, D])
        stats = sb("stats", [P, 6])
        moments = sb("moments", [P, 2])
        power = sb("power", [P, 1])
        veps = sb("veps", [P, 1])
        rstd = sb("rstd", [P, 1])
        final = sb("final", [P, 4, D])

        s_load = [sem("load%d" % n) for n in range(LOADS)]
        s_out = [sem("out%d" % n) for n in range(4)]
        (xt_mm, h_mm, y_mm, xt_ev, w_now, h_ev, y_ev, res_d, st_d, mom_d, ve_d, rstd_d, fin_d,
         s_pow) = map(sem, ("xt_mm", "h_mm", "y_mm", "xt_ev", "w_now", "h_ev", "y_ev", "resid",
                            "stats", "moments", "veps", "rstd", "final", "power"))
        carry_d = sem("carry")
        XT0, H0, Y0 = 0, 2, 6
        HALF = FC // 2

        with nc.Block() as block:
            def slots(eng, slot):
                for t in range(-1, BODY):
                    slot(t, 0, t)
                with eng.Fori(1, (XTILES - 2) // BODY) as it:
                    for k in range(BODY):
                        slot(it * BODY + k, it, k)
                for t in range((XTILES - 2) // BODY * BODY, XTILES + 2):
                    slot(t, t // BODY, t % BODY)

            def there(t, lag):
                return not isinstance(t, int) or 0 <= t - lag < XTILES

            def past(t, first):
                return not isinstance(t, int) or t >= first

            @block.sync
            def _(sp):
                def load(t, it, k):
                    if past(t, LOADS):
                        sp.wait_ge(s_out[(k - LOADS) % 4], 16 * scatters(it, k, LOADS))
                    sp.dma_start(rows[:, k % LOADS, :], sorted_x[bass.ds(t * P, P), :]
                                 ).then_inc(s_load[k % LOADS], 16)

                def scatters(it, k, lag):
                    return it * (BODY // 4) + (k - lag) // 4 + 1

                for t in range(BODY):
                    load(t, 0, t)
                with sp.Fori(1, XTILES // BODY) as it:
                    for k in range(BODY):
                        load(it * BODY + k, it, k)
                for t in range(XTILES // BODY * BODY, XTILES):
                    load(t, t // BODY, t % BODY)

            @block.gpsimd
            def _(pool):
                nc.gpsimd.memset(power[:], -0.5).then_inc(s_pow, 1)
                pool.wait_ge(s_pow, 1)

                def slot(t, it, k):
                    if there(t, 2):
                        pool.wait_ge(mom_d, t - 1)
                        if past(t, 3):
                            pool.wait_ge(fin_d, t - 2)
                        nc.gpsimd.tensor_tensor(veps[:], moments[:, 1:2], eps[:], ALU.add
                                                ).then_inc(ve_d, 1)
                        pool.wait_ge(ve_d, t - 1)
                        nc.gpsimd.tensor_tensor(rstd[:], veps[:], power[:], ALU.pow
                                                ).then_inc(rstd_d, 1)
                        pool.wait_ge(fin_d, t - 1)
                        pool.sem_inc(carry_d, 1)
                        nc.gpsimd.indirect_dma_start(
                            out=out[:, :],
                            out_offset=bass.IndirectOffsetOnAxis(
                                ap=rows[:, (k - 2) % LOADS, D + 1:D + 2].bitcast(I32), axis=0),
                            in_=final[:, (k - 2) % 4, :], in_offset=None,
                            bounds_check=TOKENS - 1, oob_is_err=False
                        ).then_inc(s_out[(k - 2) % 4], 16)
                slots(pool, slot)
                for n in range(4):
                    pool.wait_ge(s_out[n], 16 * ((XTILES - 1 - n) // 4 + 1))

            @block.tensor
            def _(pe):
                def slot(t, it, k):
                    if there(t, -1):
                        pe.wait_ge(s_load[(k + 1) % LOADS],
                                   16 * (it * (BODY // LOADS) + (k + 1) // LOADS + 1))
                        if past(t, 1):
                            pe.wait_ge(xt_ev, t)
                        nc.tensor.transpose(banks[:, XT0 + (k + 1) % 2, 0:P],
                                            rows[:, (k + 1) % LOADS, 0:D], ident[:]
                                            ).then_inc(xt_mm, 1)
                    if there(t, 0):
                        pe.wait_ge(xt_ev, t + 1)
                        pe.wait_ge(w_now, t + 1)
                        if past(t, 2):
                            pe.wait_ge(h_ev, (t - 1) * FC)
                        for c in range(FC):
                            bank = H0 + 2 * (k % 2) + c // HALF
                            last = nc.tensor.matmul(banks[:, bank, c % HALF * P:(c % HALF + 1) * P],
                                                    w1_now[:, k % 2, c * P:(c + 1) * P],
                                                    xT[:, k % 2, :], start=True, stop=True)
                            if c % HALF == HALF - 1:
                                last.then_inc(h_mm, 1)
                    if there(t, 1):
                        e = nc.tensor.value_load(tile_expert[0:1, bass.ds(t - 1, 1)],
                                                 min_val=0, max_val=EXPERTS - 1)
                        if past(t, 3):
                            pe.wait_ge(y_ev, t - 2)
                        for c in range(FC):
                            pe.wait_ge(h_ev, (t - 1) * FC + (c + 1))
                            last = nc.tensor.matmul(banks[:, Y0 + (k - 1) % 2, 0:D],
                                                    hT[:, (k - 1) % 2, c, :],
                                                    w2_s[:, bass.ds(e, 1), c, :].rearrange(
                                                        "p e d -> p (e d)"),
                                                    start=c == 0, stop=c == FC - 1)
                        last.then_inc(y_mm, 1)
                slots(pe, slot)

            @block.scalar
            def _(act):
                nc.scalar.preload_act_table_set("gelu_apprx_tanh_and_others")

                def slot(t, it, k):
                    if there(t, 0):
                        if past(t, 2):
                            act.wait_ge(y_mm, t - 1)
                        for c in range(FC):
                            bank = H0 + 2 * (k % 2) + c // HALF
                            if c % HALF == 0:
                                act.wait_ge(h_mm, t * 2 + (c // HALF + 1))
                            nc.scalar.activation(hT[:, k % 2, c, :],
                                                 banks[:, bank, c % HALF * P:(c % HALF + 1) * P],
                                                 ACT.Gelu_apprx_tanh,
                                                 bias=b1_now[:, k % 2, c:c + 1]).then_inc(h_ev, 1)
                slots(act, slot)

            @block.vector
            def _(dve):
                def slot(t, it, k):
                    if there(t, -1):
                        e = nc.vector.value_load(tile_expert[0:1, bass.ds(t + 1, 1)],
                                                 min_val=0, max_val=EXPERTS - 1)
                        if past(t, 1):
                            dve.wait_ge(h_ev, t * FC)
                        nc.vector.tensor_copy(w1_now[:, (k + 1) % 2, None, :],
                                              w1_s[:, bass.ds(e, 1), :])
                        nc.vector.tensor_copy(b1_now[:, (k + 1) % 2, None, :],
                                              b1_s[:, bass.ds(e, 1), :]).then_inc(w_now, 1)
                        dve.wait_ge(xt_mm, t + 2)
                        nc.vector.tensor_copy(xT[:, (k + 1) % 2, :],
                                              banks[:, XT0 + (k + 1) % 2, 0:P]).then_inc(xt_ev, 1)
                    if there(t, 2):
                        last_e = nc.vector.value_load(tile_expert[0:1, bass.ds(t - 2, 1)],
                                                      min_val=0, max_val=EXPERTS - 1)
                        dve.wait_ge(y_mm, t - 1)
                        if past(t, 3):
                            dve.wait_ge(res_d, t - 2)
                        nc.vector.tensor_tensor(y[:, None, :],
                                                banks[:, None, Y0 + (k - 2) % 2, 0:D],
                                                b2_s[:, bass.ds(last_e, 1), :], ALU.add
                                                ).then_inc(y_ev, 1)
                        dve.wait_ge(y_ev, t - 1)
                        nc.vector.scalar_tensor_tensor(
                            resid[:, k % 2, :], y[:], rows[:, (k - 2) % LOADS, D:D + 1],
                            rows[:, (k - 2) % LOADS, 0:D], ALU.mult, ALU.add).then_inc(res_d, 1)
                        dve.wait_ge(res_d, t - 1)
                        if past(t, 3):
                            dve.wait_ge(mom_d, t - 2)
                        nc.vector.bn_stats(stats[:], resid[:, k % 2, :]).then_inc(st_d, 1)
                        dve.wait_ge(st_d, t - 1)
                        if past(t, 3):
                            dve.wait_ge(ve_d, t - 2)
                            dve.wait_ge(fin_d, t - 2)
                        dve.sem_inc(carry_d, 1)
                        nc.vector.bn_aggr(moments[:], stats[:]).then_inc(mom_d, 1)
                        dve.wait_ge(rstd_d, t - 1)
                        if past(t, 6):
                            dve.wait_ge(s_out[(k - 2) % 4],
                                        16 * (it * (BODY // 4) + (k - 6) // 4 + 1))
                        nc.vector.tensor_scalar(final[:, (k - 2) % 4, :], resid[:, k % 2, :],
                                                moments[:, 0:1], rstd[:], ALU.subtract, ALU.mult
                                                ).then_inc(fin_d, 1)
                slots(dve, slot)


_ORDER = ["x", "xT", "ctxT", "mask", "Wq", "Wk", "Wv", "Wg", "Wgk1", "Wgk2", "bgk2", "rms_w", "Wo",
          "wq", "bq", "wk", "bk", "wv", "bv", "wo", "bo", "switch_w", "switch_b",
          "w1", "b1T", "w2", "b2"]


def kernel(**inputs):
    import numpy as _np
    import concourse.bacc as _bacc
    from concourse import mybir as _mybir
    from concourse.bass_utils import run_bass_kernel_spmd as _run

    given = {k: _np.asarray(v) for k, v in inputs.items()}
    x = given["x"].reshape(-1, given["x"].shape[-1])
    context = given["ctx_1024"].reshape(-1, given["ctx_1024"].shape[-1])
    mask = given["mask_Bx1xSxS2_bf0"]
    arrays = {"x": x, "xT": x.T, "ctxT": context.T,
              "mask": mask.reshape(-1, mask.shape[-1])}
    for name in _ORDER[4:]:
        stage = ("L0_attn_" if name in _ORDER[4:13] else
                 "L0_xattn_" if name in _ORDER[13:21] else "L0_ffn_")
        if name == "b1T":
            arrays[name] = given[stage + "b1"].reshape(-1, x.shape[-1]).T
        else:
            arrays[name] = given[stage + name]
    nc = _bacc.Bacc("TRN2", target_bir_lowering=False, num_devices=1)
    args = []
    for name in _ORDER:
        arrays[name] = _np.ascontiguousarray(arrays[name])
        args.append(nc.dram_tensor("in_" + name, arrays[name].shape,
                                   _mybir.dt.from_np(arrays[name].dtype), kind="ExternalInput").ap())
    args.append(nc.dram_tensor("out", x.shape, _mybir.dt.float32, kind="ExternalOutput").ap())
    decoder_layer(nc, *args)
    result = _run(nc, [{"in_" + k: v for k, v in arrays.items()}], core_ids=[0])
    return result.results[0]["out"].reshape(given["x"].shape)
```

```python
import concourse.bass as bass
from concourse import mybir

F32 = mybir.dt.float32
I32 = mybir.dt.int32
U8 = mybir.dt.uint8
ALU = mybir.AluOpType
ACT = mybir.ActivationFunctionType
AX = mybir.AxisListType

P = 128
BATCH, SEQ, D = 128, 64, 128
TOKENS = BATCH * SEQ
TILES = TOKENS // P
GROUP = 512
GT = GROUP // P
GB = GROUP // SEQ
GROUPS = TOKENS // GROUP
HA, DKA, DVA = 4, 32, 64
VD = HA * DVA
LOWRANK = 16
GATE_NORM = 16.0
HX, DX = 16, 8
NEG = -1.0e9
LARGE = 1.5e38
EPS = 1e-5
EXPERTS, FF = 8, 512
FC = FF // P
ROW = D + 2
XTILES = TILES + EXPERTS - 1
CLAMP = 40.0
SILU_CLAMP = -44.0


def decoder_layer(nc, x, xT, ctxT, mask, Wq, Wk, Wv, Wg, Wgk1, Wgk2, bgk2, rms_w, Wo,
                  wq, bq, wk, bk, wv, bv, wo, bo, switch_w, switch_b, w1, b1T, w2, b2, out):
    sorted_x = nc.dram_tensor("sorted_x", (XTILES * P, ROW), F32, kind="Internal").ap()

    with (
        nc.sbuf_tensor("stream", [P, TILES, ROW], F32) as stream,
        nc.sbuf_tensor("streamT", [P, TOKENS], F32) as streamT,
        nc.sbuf_tensor("ident", [P, P], F32) as ident,
        nc.sbuf_tensor("eps", [P, 1], F32) as eps,
        nc.psum_tensor("banks", [P, 8, 512], F32) as banks,
    ):
        linear_attention(nc, x, xT, Wq, Wk, Wv, Wg, Wgk1, Wgk2, bgk2, rms_w, Wo,
                         stream, streamT, ident, eps, banks)
        with nc.sbuf_tensor("logits", [P, TILES, EXPERTS], F32) as logits:
            cross_attention(nc, ctxT, mask, wq, bq, wk, bk, wv, bv, wo, bo, switch_w, sorted_x,
                            stream, streamT, ident, eps, banks, logits)
            experts(nc, switch_b, w1, b1T, w2, b2, sorted_x, out,
                    stream, ident, eps, banks, logits)


def linear_attention(nc, x, xT, Wq, Wk, Wv, Wg, Wgk1, Wgk2, bgk2, rms_w, Wo,
                     stream, streamT, ident, eps, banks):
    from contextlib import ExitStack
    ctx = ExitStack()
    with ctx:
        def sb(name, shape, dt=F32):
            return ctx.enter_context(nc.sbuf_tensor("a_" + name, shape, dt))

        def sem(name):
            return ctx.enter_context(nc.semaphore("a_" + name))

        wq_s, wk_s = sb("wq", [P, P]), sb("wk", [P, P])
        wv_s, wg_s = sb("wv", [P, VD]), sb("wg", [P, VD])
        gk1_s = sb("gk1", [P, P])
        gk2_s = sb("gk2", [P, P])
        bgk_s, rms_s = sb("bgk", [P, 1]), sb("rms", [P, 1])
        wo_s = sb("wo", [P, 2, D])
        head_mean = sb("head_mean", [P, P])
        causal = sb("causal", [P, P])
        lowrank = sb("lowrank", [P, GROUP])
        uclamp = sb("uclamp", [P, GROUP])
        espl = sb("espl", [P, GROUP])
        lspl = sb("lspl", [P, GROUP])
        negsig = sb("negsig", [P, GROUP])
        egd = sb("egd", [P, 2, GROUP])
        qg = sb("qg", [P, 2, GT, HA, P])
        kn = sb("kn", [P, 2, GROUP])
        val = sb("val", [P, 2, GT, VD])
        gate = sb("gate", [P, 2, 2, GROUP])
        gexp = sb("gexp", [P, 2, GROUP])
        glog = sb("glog", [P, 2, 2, GROUP])
        scores = sb("scores", [P, 2, HA, P])
        square = sb("square", [P, 2, GROUP])
        lms = sb("lms", [P, 2, GROUP])
        wlog = sb("wlog", [P, 2, GROUP])
        wexp = sb("wexp", [P, 2, GROUP])
        onorm = sb("onorm", [P, 2, GROUP])
        ogate = sb("ogate", [P, 2, GROUP])
        xTs = sb("xT", [P, 2, GROUP])
        resid = sb("resid", [P, GT, D])
        xn = sb("xn", [P, GT, D])
        stats = sb("stats", [P, GT, 6])
        moments = sb("moments", [P, GT, 2])
        lvar = sb("lvar", [P, GT])
        rstd = sb("rstd", [P, GT])

        s_w, s_wl = sem("weights"), sem("late_weights")
        s_zero, s_const, s_wo = sem("zeros"), sem("constants"), sem("wo_scaled")
        s_x = [sem("x0"), sem("x1")]
        (lr_mm, u_mm, q_mm, k_mm, v_mm, g_mm, at_mm, ot_mm, ms_mm, wo_mm, xt_mm) = map(sem, (
            "lr_mm", "u_mm", "q_mm", "k_mm", "v_mm", "g_mm", "at_mm", "ot_mm", "ms_mm", "wo_mm",
            "xt_mm"))
        (lr_ev, espl_d, lspl_d, val_d, egd_d, gexp_d, glog_d, sq_d, lms_d, wexp_d, lvar_d, rstd_d,
         xt_ev) = map(sem, ("lr_ev", "espl", "lspl", "val", "egd", "gexp", "glog", "sq", "lms",
                            "wexp", "lvar", "rstd", "xt_ev"))
        (sc_ev, wlog_d, on_d, uc_d, ns_d, y_d, st_d, mom_d, ln_d, gate_d, qg_d, kn_d) = map(
            sem, ("sc_ev", "wlog", "onorm", "uclamp", "negsig", "resid", "stats",
                  "moments", "ln", "gate", "qg", "kn"))
        og_d, keep_d, s_dz = sem("ogate"), sem("keep"), sem("dve_zeros")
        carry_d = sem("carry")

        LR_BANK, Q_BANK, K_BANK, EV0, EV1, AT_BANK, OT_BANK = 0, 1, 2, 3, 4, 5, 6

        with nc.Block() as block:
            def steps(eng, body):
                body(-1, 1, 0, True, False, False)
                body(0, 0, 0, True, True, False)
                with eng.Fori(0, (GROUPS - 2) // 2) as pair:
                    for k in range(2):
                        body(pair * 2 + (1 + k), 1 - k, pair + 1, True, True, True)
                body(GROUPS - 1, 1, None, False, True, True)
                body(GROUPS, 0, None, False, False, True)

            def past(i, first):
                return not isinstance(i, int) or i >= first

            @block.sync
            def _(sp):
                sp.wait_ge(s_zero, 2)
                for dst, src in ((gk1_s[:, 0:LOWRANK], Wgk1), (gk2_s[0:LOWRANK, :], Wgk2),
                                 (wq_s[:], Wq), (wk_s[:], Wk), (wv_s[:], Wv), (wg_s[:], Wg),
                                 (bgk_s[:], bgk2[:, None])):
                    sp.dma_start(dst, src).then_inc(s_w, 16)

                def body(i, p, er, early, mid, late):
                    e = 1 - p
                    if early:
                        if past(i, 1):
                            sp.wait_ge(g_mm, 2 * i)
                        sp.dma_start(xTs[:, e, :], xT[:, bass.ds((i + 1) * GROUP, GROUP)]
                                     ).then_inc(s_x[e], 16)
                        sp.dma_start(stream[:, bass.ds((i + 1) * GT, GT), 0:D],
                                     x[bass.ds((i + 1) * GROUP, GROUP), :].rearrange(
                                         "(t p) d -> p t d", p=P)).then_inc(s_x[e], 16)
                        if isinstance(i, int) and i == -1:
                            for dst, src in ((rms_s[0:DVA, :], rms_w[:, None]),
                                             (rms_s[DVA:P, :], rms_w[:, None]),
                                             (wo_s[:], Wo.rearrange("(c p) d -> p c d", p=P))):
                                sp.dma_start(dst, src).then_inc(s_wl, 16)
                steps(sp, body)

            @block.gpsimd
            def _(pool):
                nc.gpsimd.memset(gk1_s[:], 0.0).then_inc(s_zero, 1)
                nc.gpsimd.memset(gk2_s[:], 0.0).then_inc(s_zero, 1)
                nc.gpsimd.memset(eps[:], EPS)
                nc.gpsimd.memset(head_mean[:], 0.0)
                nc.gpsimd.memset(causal[:], 1.0)
                nc.gpsimd.memset(ident[:], 0.0).then_inc(s_zero, 1)
                pool.wait_ge(s_zero, 3)
                nc.gpsimd.affine_select(out=ident[:], in_=ident[:], compare_op=ALU.not_equal,
                                        fill=1.0, base=0, pattern=[[-1, P]], channel_multiplier=1)
                nc.gpsimd.affine_select(out=causal[:], in_=causal[:], compare_op=ALU.is_ge,
                                        fill=0.0, base=0, pattern=[[1, P]],
                                        channel_multiplier=-1).then_inc(s_zero, 1)
                pool.wait_ge(s_zero, 4)
                nc.gpsimd.memset(causal[0:SEQ, SEQ:P], 0.0).then_inc(s_zero, 1)
                pool.wait_ge(s_zero, 5)
                nc.gpsimd.memset(head_mean[0:DVA, 0:DVA], 1.0 / DVA).then_inc(s_zero, 1)
                pool.wait_ge(s_zero, 6)
                nc.gpsimd.memset(head_mean[DVA:P, DVA:P], 1.0 / DVA).then_inc(s_const, 1)
                pool.wait_ge(s_const, 1)

                def body(i, p, er, early, mid, late):
                    if late:
                        for c in range(2):
                            pool.wait_ge(on_d, 2 * i - 1 + c)
                            pool.wait_ge(wo_mm, i - 1)
                            nc.gpsimd.tensor_tensor(ogate[:, c, :], onorm[:, c, :],
                                                    gate[:, 1 - p, c, :], ALU.mult).then_inc(og_d, 1)
                        pool.wait_ge(ln_d, i)
                        nc.gpsimd.tensor_copy(stream[:, bass.ds((i - 1) * GT, GT), 0:D], xn[:]
                                              ).then_inc(keep_d, 1)
                steps(pool, body)

            @block.tensor
            def _(pe):
                pe.wait_ge(s_w, 16 * 7)
                pe.wait_ge(s_const, 1)
                mm = nc.tensor.matmul

                def body(i, p, er, early, mid, late):
                    e = 1 - p
                    if late:
                        pe.wait_ge(gate_d, 2 * (i + 1) if early or mid else 2 * GROUPS)
                        pe.wait_ge(y_d, i - 1)
                        pe.wait_ge(xt_ev, i - 1)
                        for c in range(2):
                            pe.wait_ge(sq_d, 2 * i - 1 + c)
                            mm(banks[:, EV0 + c, :], head_mean[:], square[:, c, :],
                               start=True, stop=True).then_inc(ms_mm, 1)

                    def scores_mm(t):
                        if t == 0:
                            pe.wait_ge(qg_d, i + 1)
                            pe.wait_ge(kn_d, i + 1)
                        if t > 0 or past(i, 1):
                            pe.wait_ge(sc_ev, i * GT + t)
                        mm(banks[:, AT_BANK, :], kn[:, p, t * P:(t + 1) * P],
                           qg[:, p, t].rearrange("p h c -> p (h c)"),
                           start=True, stop=True).then_inc(at_mm, 1)

                    def out_mm(t):
                        pe.wait_ge(sc_ev, i * GT + (t + 1))
                        if t == 0:
                            pe.wait_ge(val_d, 2 * (i + 1))
                            if past(i, 1):
                                pe.wait_ge(on_d, 2 * i)
                        for h in range(HA):
                            half = DVA * (h % 2)
                            last = mm(banks[half:half + DVA, OT_BANK + h // 2, t * P:(t + 1) * P],
                                      val[:, p, t, h * DVA:(h + 1) * DVA], scores[:, t % 2, h, :],
                                      start=True, stop=True)
                        last.then_inc(ot_mm, 1)

                    if mid:
                        scores_mm(0)
                    if early:
                        pe.wait_ge(s_x[e], 32 * (er + 1))
                        if past(i, 0):
                            pe.wait_ge(ns_d, i + 1)
                        mm(banks[:, LR_BANK, :], gk1_s[:], xTs[:, e, :],
                           start=True, stop=True).then_inc(lr_mm, 1)
                        mm(banks[:, Q_BANK, :], wq_s[:], xTs[:, e, :],
                           start=True, stop=True).then_inc(q_mm, 1)
                    if mid:
                        scores_mm(1)
                        out_mm(0)
                    if early:
                        mm(banks[:, K_BANK, :], wk_s[:], xTs[:, e, :],
                           start=True, stop=True).then_inc(k_mm, 1)
                        pe.wait_ge(lr_ev, i + 2)
                        mm(banks[:, LR_BANK, :], gk2_s[:], lowrank[:],
                           start=True, stop=True).then_inc(u_mm, 1)
                    if mid:
                        scores_mm(2)
                        out_mm(1)
                    if early:
                        if late:
                            pe.wait_ge(lms_d, 2 * i)
                        elif mid:
                            pe.wait_ge(gate_d, 2)
                        for c in range(2):
                            for t in range(2):
                                first = (2 * c + t) * P
                                last = mm(banks[:, EV0 + c, t * VD:(t + 1) * VD],
                                          xTs[:, e, first:first + P], wv_s[:],
                                          start=True, stop=True)
                            last.then_inc(v_mm, 1)
                    if mid:
                        scores_mm(3)
                    if late:
                        pe.wait_ge(s_wo, 1)
                        if early:
                            pe.wait_ge(val_d, 2 * (i + 1) + 1)
                        else:
                            pe.wait_ge(lms_d, 2 * i)
                        pe.wait_ge(og_d, 2 * i)
                        for t in range(GT):
                            for c in range(2):
                                last = mm(banks[:, EV0, t * P:(t + 1) * P],
                                          ogate[:, c, t * P:(t + 1) * P], wo_s[:, c, :],
                                          start=c == 0, stop=c == 1)
                        last.then_inc(wo_mm, 1)
                    if mid:
                        out_mm(2)
                    if early:
                        pe.wait_ge(val_d, 2 * (i + 1) + 2)
                        mm(banks[:, EV1, :], wg_s[:, 0:P], xTs[:, e, :],
                           start=True, stop=True).then_inc(g_mm, 1)
                        if late:
                            pe.wait_ge(y_d, i)
                        mm(banks[:, EV0, :], wg_s[:, P:VD], xTs[:, e, :],
                           start=True, stop=True).then_inc(g_mm, 1)
                    if mid:
                        out_mm(3)
                    if late:
                        pe.wait_ge(ln_d, i)
                        if early:
                            pe.wait_ge(gate_d, 2 * (i + 1) + 1)
                        for t in range(GT):
                            last = nc.tensor.transpose(banks[:, EV1, t * P:(t + 1) * P],
                                                       xn[:, t, :], ident[:])
                        last.then_inc(xt_mm, 1)
                steps(pe, body)

            @block.scalar
            def _(act):
                af = nc.scalar.activation
                nc.scalar.preload_act_table_set("natural_log_exp_and_others")
                act.wait_ge(s_const, 1)

                def body(i, p, er, early, mid, late):
                    e = 1 - p
                    if late:
                        for c in range(2):
                            act.wait_ge(ms_mm, 2 * i - 1 + c)
                            if not isinstance(i, int) or i > 1:
                                act.wait_ge(wlog_d, 2 * (i - 1) + c - (1 if c else 0))
                            af(lms[:, c, :], banks[:, EV0 + c, :], ACT.Ln, bias=eps[:]
                               ).then_inc(lms_d, 1)
                        for c in range(2):
                            act.wait_ge(wlog_d, 2 * i - 1 + c)
                            act.wait_ge(on_d, 2 * (i - 1))
                            af(wexp[:, c, :], wlog[:, c, :], ACT.Exp, scale=-1.0).then_inc(wexp_d, 1)
                    if early:
                        act.wait_ge(lr_mm, i + 2)
                        if past(i, 0):
                            act.wait_ge(u_mm, i + 1)
                        af(lowrank[:], banks[:, LR_BANK, :], ACT.Copy, scale=-1.0).then_inc(lr_ev, 1)
                        act.wait_ge(uc_d, i + 2)
                        af(espl[:], uclamp[:], ACT.Exp).then_inc(espl_d, 1)
                        act.wait_ge(espl_d, i + 2)
                        if past(i, 0):
                            act.wait_ge(ns_d, i + 1)
                        af(lspl[:], espl[:], ACT.Ln, bias=1.0).then_inc(lspl_d, 1)
                        for c in range(2):
                            act.wait_ge(v_mm, 2 * (i + 1) + 1 + c)
                            if past(i, 1):
                                act.wait_ge(ot_mm, i * GT)
                            af(val[:, e, 2 * c:2 * c + 2, :].rearrange("p t v -> p (t v)"),
                               banks[:, EV0 + c, :], ACT.Copy).then_inc(val_d, 1)
                        act.wait_ge(ns_d, i + 2)
                        if past(i, 0):
                            act.wait_ge(kn_d, i + 1)
                        for c, sign in enumerate((-1.0, 1.0)):
                            af(egd[:, c, :], negsig[:], ACT.Exp, scale=sign / GATE_NORM
                               ).then_inc(egd_d, 1)
                    if late:
                        act.wait_ge(mom_d, i)
                        af(lvar[:], moments[:, :, 1], ACT.Ln, bias=eps[:]).then_inc(lvar_d, 1)
                        act.wait_ge(lvar_d, i)
                        act.wait_ge(ln_d, i - 1)
                        af(rstd[:], lvar[:], ACT.Exp, scale=-0.5).then_inc(rstd_d, 1)
                    if early:
                        for c in range(2):
                            act.wait_ge(gate_d, 2 * (i + 1) + 1 + c)
                            if past(i, 0):
                                act.wait_ge(glog_d, 2 * (i + 1))
                            af(gexp[:, c, :], gate[:, e, c, :], ACT.Exp, scale=-1.0
                               ).then_inc(gexp_d, 1)
                        for c in range(2):
                            act.wait_ge(gexp_d, 2 * (i + 1) + 1 + c)
                            af(glog[:, e, c, :], gexp[:, c, :], ACT.Ln, bias=1.0).then_inc(glog_d, 1)
                    if mid:
                        act.wait_ge(ot_mm, (i + 1) * GT)
                        if past(i, 1):
                            act.wait_ge(ms_mm, 2 * i)
                        for c in range(2):
                            af(square[:, c, :], banks[:, OT_BANK + c, :], ACT.Square
                               ).then_inc(sq_d, 1)
                    if late:
                        act.wait_ge(xt_mm, i)
                        af(streamT[:, bass.ds((i - 1) * GROUP, GROUP)], banks[:, EV1, :], ACT.Copy
                           ).then_inc(xt_ev, 1)
                steps(act, body)

            @block.vector
            def _(dve):
                nc.vector.memset(qg[:], 0.0)
                nc.vector.memset(scores[:], 0.0).then_inc(s_dz, 1)
                dve.wait_ge(s_wl, 16 * 3)
                for c in range(2):
                    last = nc.vector.tensor_scalar(wo_s[:, c, :], wo_s[:, c, :], rms_s[:], None,
                                                   ALU.mult)
                last.then_inc(s_wo, 1)
                dve.wait_ge(s_w, 16 * 7)
                dve.wait_ge(s_const, 1)
                dve.wait_ge(s_dz, 1)
                keep = causal[:].bitcast(I32)[:, None, :].to_broadcast([P, HA, P])

                def body(i, p, er, early, mid, late):
                    e = 1 - p

                    def scores_ev(t):
                        dve.wait_ge(at_mm, i * GT + (t + 1))
                        if t > 1 or past(i, 1):
                            dve.wait_ge(ot_mm, i * GT + (t - 1))
                        dve.sem_inc(carry_d, 1)
                        nc.vector.copy_predicated(
                            scores[:, t % 2], keep,
                            banks[:, AT_BANK, :].rearrange("p (h c) -> p h c", h=HA)
                        ).then_inc(sc_ev, 1)

                    if mid:
                        scores_ev(0)
                    if late:
                        for c in range(2):
                            dve.wait_ge(lms_d, 2 * i - 1 + c)
                            dve.wait_ge(glog_d, 2 * i - 1 + c)
                            dve.wait_ge(wexp_d, 2 * (i - 1))
                            nc.vector.scalar_tensor_tensor(
                                wlog[:, c, :], lms[:, c, :], 0.5, glog[:, 1 - p, c, :],
                                ALU.mult, ALU.add).then_inc(wlog_d, 1)
                    if mid:
                        scores_ev(1)
                    if late:
                        for c in range(2):
                            dve.wait_ge(wexp_d, 2 * i - 1 + c)
                            dve.wait_ge(og_d, 2 * (i - 1))
                            nc.vector.tensor_tensor(onorm[:, c, :], banks[:, OT_BANK + c, :],
                                                    wexp[:, c, :], ALU.mult).then_inc(on_d, 1)
                    if early:
                        dve.wait_ge(u_mm, i + 2)
                        nc.vector.tensor_scalar(uclamp[:], banks[:, LR_BANK, :], bgk_s[:], CLAMP,
                                                ALU.subtract, ALU.min).then_inc(uc_d, 1)
                    if mid:
                        scores_ev(2)
                    if early:
                        dve.wait_ge(lspl_d, i + 2)
                        if past(i, 0):
                            dve.wait_ge(egd_d, 2 * (i + 1))
                        nc.vector.scalar_tensor_tensor(
                            negsig[:], banks[:, LR_BANK, :], bgk_s[:], lspl[:],
                            ALU.subtract, ALU.max).then_inc(ns_d, 1)
                    if mid:
                        scores_ev(3)
                    if late:
                        dve.wait_ge(wo_mm, i)
                        nc.vector.tensor_tensor(
                            resid[:], banks[:, EV0, :].rearrange("p (t d) -> p t d", t=GT),
                            stream[:, bass.ds((i - 1) * GT, GT), 0:D], ALU.add).then_inc(y_d, 1)
                        dve.wait_ge(y_d, i)
                        for t in range(GT):
                            last = nc.vector.bn_stats(stats[:, t, :], resid[:, t, :])
                        last.then_inc(st_d, 1)
                        dve.wait_ge(st_d, i)
                        dve.sem_inc(carry_d, 1)
                        for t in range(GT):
                            last = nc.vector.bn_aggr(moments[:, t, :], stats[:, t, :])
                        last.then_inc(mom_d, 1)
                    if early:
                        for c in range(2):
                            dve.wait_ge(g_mm, 2 * (i + 1) + 1 + c)
                            if past(i, 1):
                                dve.wait_ge(og_d, 2 * i)
                            nc.vector.tensor_scalar(gate[:, e, c, :], banks[:, EV1 - c, :],
                                                    SILU_CLAMP, None, ALU.max).then_inc(gate_d, 1)
                    if late:
                        dve.wait_ge(rstd_d, i)
                        dve.wait_ge(xt_mm, i - 1)
                        dve.wait_ge(keep_d, i - 1)
                        for t in range(GT):
                            last = nc.vector.tensor_scalar(
                                xn[:, t, :], resid[:, t, :], moments[:, t, 0:1],
                                rstd[:, t:t + 1], ALU.subtract, ALU.mult)
                        last.then_inc(ln_d, 1)
                    if early:
                        dve.wait_ge(q_mm, i + 2)
                        dve.wait_ge(egd_d, 2 * (i + 1) + 1)
                        if past(i, 1):
                            dve.wait_ge(at_mm, i * GT)
                        for h in range(HA):
                            rows = slice(h * DKA, (h + 1) * DKA)
                            last = nc.vector.scalar_tensor_tensor(
                                qg[rows, e, :, h, :],
                                banks[rows, Q_BANK, :].rearrange("p (t c) -> p t c", t=GT),
                                float(DKA) ** -0.5,
                                egd[rows, 0, :].rearrange("p (t c) -> p t c", t=GT),
                                ALU.mult, ALU.mult)
                        last.then_inc(qg_d, 1)
                        dve.wait_ge(k_mm, i + 2)
                        dve.wait_ge(egd_d, 2 * (i + 1) + 2)
                        nc.vector.tensor_tensor(kn[:, e, :], banks[:, K_BANK, :], egd[:, 1, :],
                                                ALU.mult).then_inc(kn_d, 1)
                steps(dve, body)


def cross_attention(nc, ctxT, mask, wq, bq, wk, bk, wv, bv, wo, bo, switch_w, sorted_x,
                    stream, streamT, ident, eps, banks, logits):
    from contextlib import ExitStack
    ctx = ExitStack()
    with ctx:
        def sb(name, shape, dt=F32):
            return ctx.enter_context(nc.sbuf_tensor("b_" + name, shape, dt))

        def sem(name):
            return ctx.enter_context(nc.semaphore("b_" + name))

        PAIRS = HX // 2
        DV = DX + 1
        SCALE = float(DX) ** -0.5
        wq_s, wk_s, wv_s, wo_s = (sb(n, [P, D]) for n in ("wq", "wk", "wv", "wo"))
        sw_s = sb("sw", [P, EXPERTS])
        bq_s, bk_s = sb("bq", [P, 1]), sb("bk", [P, 1])
        bq_scaled = sb("bq_scaled", [P, 1])
        bv_s, bo_s = sb("bv", [P, D]), sb("bo", [P, D])
        mask_s = sb("mask", [P, TILES, SEQ], U8)
        padding = sb("padding", [P, ROW])
        ctx_s = sb("ctx", [P, 2, GROUP])
        qT = sb("qT", [P, 2, GROUP])
        kT = sb("kT", [P, GROUP])
        kbd = sb("kbd", [P, 2, GB, HX, SEQ])
        vbd = sb("vbd", [P, 2, GB, PAIRS, 2, DV])
        masked = sb("masked", [P, GT, SEQ])
        limit = sb("limit", [P, 2, GT, SEQ])
        prob = sb("prob", [P, 4, HX, SEQ])
        top = sb("top", [P, 2, HX])
        probT = sb("probT", [P, 2, PAIRS, P])
        rsum = sb("rsum", [P, HX])
        attn = sb("attn", [P, 2, D])
        attnT = sb("attnT", [P, 2, P])
        resid = sb("resid", [P, 2, D])
        stats = sb("stats", [P, 6])
        moments = sb("moments", [P, 2, 2])
        lvar, rstd = sb("lvar", [P, 1]), sb("rstd", [P, 2])
        xn = sb("xn", [P, 2, D])
        xnT = sb("xnT", [P, 2, P])

        s_w, s_m, s_z, s_init, s_const = map(sem, ("weights", "mask", "zero", "init", "const"))
        s_zf, s_kz = sem("zero_fill"), sem("kbd_zero")
        carry_d = sem("carry")
        s_c = [sem("ctx0"), sem("ctx1")]
        s_k = [sem("kbd0"), sem("kbd1")]
        (q_mm, k_mm, v_mm, s_mm, tp_mm, av_mm, at_mm, wo_mm, xt_mm, lg_mm) = map(sem, (
            "q_mm", "k_mm", "v_mm", "s_mm", "tp_mm", "av_mm", "at_mm", "wo_mm", "xt_mm", "lg_mm"))
        (exp_d, pt_ev, at_ev, lvar_d, rstd_d, xt_ev, lg_ev, k_ev, q_ev) = map(sem, (
            "exp", "pt_ev", "at_ev", "lvar", "rstd", "xt_ev", "lg_ev", "k_ev", "q_ev"))
        (min_d, max_d, sub_d, rs_d, an_d, y_d, st_d, mom_d, ln_d, v_ev) = map(sem, (
            "min", "max", "sub", "rsum", "attn", "resid", "stats", "moments", "ln", "v_ev"))
        (mk_d, lim_d, xb_d, keep_d) = map(sem, ("masked", "limit", "xb", "keep"))

        S_BANK, O_BANK, T0, T1, M_BANK, W_BANK = 0, 2, 4, 5, 6, 7
        XT_COL, AT_COL, WO_COL, LG_COL = 0, P, 0, P
        HALF = HX // 2
        BODY = 2 * GT
        LAST = 6

        with nc.Block() as block:
            def slots(eng, slot):
                for t in range(BODY):
                    slot(t, 0, t)
                with eng.Fori(1, TILES // BODY - 1) as it:
                    for k in range(BODY):
                        slot(it * BODY + k, it, k)
                for t in range(TILES - BODY, TILES + LAST + 1):
                    slot(t, t // BODY, t % BODY)

            def there(t, lag):
                return not isinstance(t, int) or 0 <= t - lag < TILES

            def past(t, n):
                return not isinstance(t, int) or t >= n

            def feeds(t, k, place, ahead=1):
                return k % GT == place and (not isinstance(t, int) or t // GT + ahead < GROUPS)

            def turns(t, k):
                return k % GT == 0 and (not isinstance(t, int) or GT <= t < TILES)

            def group(it, k):
                return 2 * it + k // GT

            @block.sync
            def _(sp):
                for g in range(2):
                    sp.dma_start(ctx_s[:, g, :], ctxT[:, g * GROUP:(g + 1) * GROUP]
                                 ).then_inc(s_c[g], 16)
                for dst, src in ((wq_s[:], wq), (wk_s[:], wk), (wv_s[:], wv), (wo_s[:], wo),
                                 (sw_s[:], switch_w), (bq_s[:], bq[:, None]), (bk_s[:], bk[:, None]),
                                 (bv_s[:], bv[None, :].to_broadcast([P, D])),
                                 (bo_s[:], bo[None, :].to_broadcast([P, D]))):
                    sp.dma_start(dst, src).then_inc(s_w, 16)
                sp.dma_start(mask_s[:], mask.rearrange("(t p) k -> p t k", p=P)).then_inc(s_m, 16)

                def spread_keys(g, e):
                    sp.wait_ge(k_ev, g + 1)
                    if past(g, 2):
                        sp.sem_inc(carry_d, 1)
                        sp.wait_ge(s_mm, (g - 1) * GT)
                    for h in range(HX):
                        rows = slice(h * DX, (h + 1) * DX)
                        sp.dma_start(kbd[rows, e, :, h, :],
                                     kT[rows, :].rearrange("p (s k) -> p s k", s=GB)
                                     ).then_inc(s_k[e], 16)

                def slot(t, it, k):
                    g, e = group(it, k), k // GT
                    if feeds(t, k, 0, 2):
                        sp.wait_ge(v_mm, g + 1)
                        sp.dma_start(ctx_s[:, e, :], ctxT[:, bass.ds((g + 2) * GROUP, GROUP)]
                                     ).then_inc(s_c[e], 16)
                    if feeds(t, k, 0):
                        spread_keys(g + 1, 1 - e)
                sp.wait_ge(s_kz, 2)
                spread_keys(0, 0)
                sp.wait_ge(s_z, 2)
                sp.dma_start(sorted_x.rearrange("(t p) d -> p t d", p=P),
                             padding[:, None, :].to_broadcast([P, XTILES, ROW])).then_inc(s_zf, 16)
                slots(sp, slot)
                sp.wait_ge(s_zf, 16)

            @block.gpsimd
            def _(pool):
                nc.gpsimd.memset(kbd[:, 1], 0.0).then_inc(s_kz, 1)
                nc.gpsimd.memset(padding[:, 0:D + 1], 0.0).then_inc(s_z, 1)
                nc.gpsimd.memset(padding[:, D + 1:ROW].bitcast(I32), TOKENS).then_inc(s_z, 1)
                pool.wait_ge(s_w, 16 * 9)

                def add_bias(g):
                    nc.gpsimd.tensor_tensor(stream[:, bass.ds(g * GT, GT), 0:D],
                                            stream[:, bass.ds(g * GT, GT), 0:D],
                                            bo_s[:, None, :].to_broadcast([P, GT, D]), ALU.add
                                            ).then_inc(xb_d, 1)

                def slot(t, it, k):
                    if there(t, 6):
                        pool.wait_ge(ln_d, t - 5)
                        nc.gpsimd.tensor_copy(stream[:, bass.ds(t - 6, 1), 0:D],
                                              xn[:, k % 2, None, :]).then_inc(keep_d, 1)
                    if there(t, 0):
                        pool.wait_ge(max_d, t + 1)
                        nc.gpsimd.tensor_tensor(prob[:, k % 4], prob[:, k % 4],
                                                top[:, k % 2, :, None].to_broadcast([P, HX, SEQ]),
                                                ALU.subtract).then_inc(sub_d, 1)
                    if feeds(t, k, 1):
                        add_bias(group(it, k) + 1)
                add_bias(0)
                slots(pool, slot)

            @block.tensor
            def _(pe):
                pe.wait_ge(s_w, 16 * 9)
                pe.wait_ge(s_const, 1)
                mm = nc.tensor.matmul

                def project_qk(g, e, turn):
                    pe.wait_ge(s_c[e], 16 * turn)
                    mm(banks[:, T1, :], wk_s[:], ctx_s[:, e, :], start=True, stop=True
                       ).then_inc(k_mm, 1)
                    mm(banks[:, T0, :], wq_s[:], streamT[:, bass.ds(g * GROUP, GROUP)],
                       start=True, stop=True).then_inc(q_mm, 1)

                def project_v(e, bank):
                    for t in range(GT):
                        last = mm(banks[:, bank, t * D:(t + 1) * D],
                                  ctx_s[:, e, t * P:(t + 1) * P], wv_s[:], start=True, stop=True)
                    last.then_inc(v_mm, 1)

                def scores(t, it, k):
                    if k % GT == 0:
                        pe.wait_ge(q_ev, group(it, k) + 1)
                        pe.wait_ge(s_k[k // GT], 16 * HX * (it + 1))
                    if past(t, 1):
                        pe.wait_ge(min_d, t)
                    for half in range(2):
                        for b in range(2):
                            seq = 2 * (k % GT) + b
                            last = mm(banks[SEQ * b:SEQ * b + SEQ, S_BANK + half, :],
                                      qT[:, k // GT, seq * SEQ:(seq + 1) * SEQ],
                                      kbd[:, k // GT, seq, half * HALF:(half + 1) * HALF
                                          ].rearrange("p h k -> p (h k)"),
                                      start=True, stop=True)
                    last.then_inc(s_mm, 1)

                def slot(t, it, k):
                    if there(t, 0):
                        scores(t, it, k)
                    if there(t, 3):
                        pe.wait_ge(pt_ev, 2 * (t - 2))
                    if feeds(t, k, 0):
                        project_qk(group(it, k) + 1, 1 - k // GT, it + 1 + k // GT)
                    if there(t, 5):
                        pe.wait_ge(at_ev, t - 4)
                        if past(t, 7):
                            pe.wait_ge(lg_ev, t - 6)
                        elif past(t, 6):
                            pe.wait_ge(y_d, t - 5)
                        mm(banks[:, W_BANK, WO_COL:WO_COL + D], attnT[:, (k - 5) % 2, :], wo_s[:],
                           start=True, stop=True).then_inc(wo_mm, 1)
                    if there(t, 6):
                        pe.wait_ge(ln_d, t - 5)
                        if there(t, 5):
                            pe.wait_ge(at_ev, t - 4)
                        nc.tensor.transpose(banks[:, M_BANK, XT_COL:XT_COL + P],
                                            xn[:, k % 2, :], ident[:]).then_inc(xt_mm, 1)
                    for j in range(PAIRS):
                        if there(t, 2):
                            if j == 0:
                                pe.wait_ge(exp_d, t - 1)
                                if feeds(t, k, 0):
                                    pe.wait_ge(q_ev, group(it, k) + 2)
                                    pe.wait_ge(k_ev, group(it, k) + 2)
                            last = nc.tensor.transpose(
                                banks[:, T0 + j // 4, (j % 4) * P:(j % 4 + 1) * P],
                                prob[:, (k - 2) % 4, 2 * j:2 * j + 2, :].rearrange(
                                    "p h k -> p (h k)"), ident[:])
                            if j % 4 == 3:
                                last.then_inc(tp_mm, 1)
                        if there(t, 3):
                            if j == 0:
                                pe.wait_ge(v_ev, group(it, k - 3) + 1)
                                if past(t, 5):
                                    pe.wait_ge(an_d, t - 4)
                                if turns(t, k):
                                    pe.wait_ge(v_ev, group(it, k) + 1)
                            for b in range(2):
                                col = j * 2 * DV
                                last = mm(banks[SEQ * b:SEQ * b + SEQ, O_BANK + (k - 3) % 2,
                                                col:col + 2 * DV],
                                          probT[:, (k - 3) % 2, j, SEQ * b:SEQ * b + SEQ],
                                          vbd[:, (k - 3) // GT % 2, 2 * ((k - 3) % GT) + b, j
                                              ].rearrange("p h d -> p (h d)"),
                                          start=True, stop=True)
                            if j == PAIRS - 1:
                                last.then_inc(av_mm, 1)
                        if j == PAIRS // 2 and there(t, 4):
                            pe.wait_ge(an_d, t - 3)
                            if there(t, 6):
                                pe.wait_ge(xt_ev, t - 5)
                            nc.tensor.transpose(banks[:, M_BANK, AT_COL:AT_COL + P],
                                                attn[:, k % 2, :], ident[:]).then_inc(at_mm, 1)
                    if there(t, 6):
                        pe.wait_ge(xt_ev, t - 5)
                        if there(t, 5):
                            pe.wait_ge(y_d, t - 4)
                        mm(banks[:, W_BANK, LG_COL:LG_COL + EXPERTS], xnT[:, k % 2, :], sw_s[:],
                           start=True, stop=True).then_inc(lg_mm, 1)
                    if feeds(t, k, 3):
                        if there(t, 4):
                            pe.wait_ge(an_d, t - 3)
                        project_v(1 - k // GT, O_BANK + k % 2)

                project_qk(0, 0, 1)
                project_v(0, O_BANK)
                pe.wait_ge(v_ev, 1)
                slots(pe, slot)

            @block.scalar
            def _(act):
                af = nc.scalar.activation
                nc.scalar.preload_act_table_set("natural_log_exp_and_others")
                act.wait_ge(s_const, 1)

                def projections_ev(g, e, turn):
                    act.wait_ge(k_mm, g + 1)
                    if past(g, 1):
                        act.wait_ge(s_k[1 - e], 16 * HX * turn)
                    af(kT[:], banks[:, T1, :], ACT.Identity, bias=bk_s[:]).then_inc(k_ev, 1)
                    act.wait_ge(q_mm, g + 1)
                    if past(g, 2):
                        act.wait_ge(s_mm, (g - 1) * GT)
                    af(qT[:, e, :], banks[:, T0, :], ACT.Identity, bias=bq_scaled[:], scale=SCALE
                       ).then_inc(q_ev, 1)

                def slot(t, it, k):
                    if feeds(t, k, 0):
                        projections_ev(group(it, k) + 1, 1 - k // GT, it + 1)
                    if there(t, 6):
                        act.wait_ge(xt_mm, t - 5)
                        if past(t, 8):
                            act.wait_ge(lg_mm, t - 7)
                        af(xnT[:, k % 2, :], banks[:, M_BANK, XT_COL:XT_COL + P], ACT.Copy
                           ).then_inc(xt_ev, 1)
                    for c in range(2):
                        if there(t, 2):
                            if c == 0 and past(t, 4):
                                act.wait_ge(av_mm, t - 3)
                            act.wait_ge(tp_mm, 2 * (t - 2) + 1 + c)
                            af(probT[:, k % 2, 4 * c:4 * c + 4, :].rearrange("p j q -> p (j q)"),
                               banks[:, T0 + c, :], ACT.Copy).then_inc(pt_ev, 1)
                        if c == 0 and there(t, 4):
                            act.wait_ge(at_mm, t - 3)
                            if past(t, 6):
                                act.wait_ge(wo_mm, t - 5)
                            af(attnT[:, k % 2, :], banks[:, M_BANK, AT_COL:AT_COL + P], ACT.Copy
                               ).then_inc(at_ev, 1)
                        if c == 0 and there(t, 1):
                            act.wait_ge(sub_d, t)
                            af(prob[:, (k - 1) % 4], prob[:, (k - 1) % 4], ACT.Exp
                               ).then_inc(exp_d, 1)
                    if there(t, 5):
                        act.wait_ge(mom_d, t - 4)
                        af(lvar[:], moments[:, (k - 5) % 2, 1:2], ACT.Ln, bias=eps[:]
                           ).then_inc(lvar_d, 1)
                        act.wait_ge(lvar_d, t - 4)
                        if past(t, 7):
                            act.wait_ge(ln_d, t - 6)
                        af(rstd[:, (k - 5) % 2:(k - 5) % 2 + 1], lvar[:], ACT.Exp, scale=-0.5
                           ).then_inc(rstd_d, 1)
                    if there(t, 6):
                        act.wait_ge(lg_mm, t - 5)
                        af(logits[:, bass.ds(t - 6, 1), :],
                           banks[:, W_BANK, None, LG_COL:LG_COL + EXPERTS], ACT.Copy
                           ).then_inc(lg_ev, 1)
                projections_ev(0, 0, 0)
                slots(act, slot)

            @block.vector
            def _(dve):
                nc.vector.memset(kbd[:, 0], 0.0).then_inc(s_kz, 1)
                nc.vector.memset(vbd[:], 0.0).then_inc(s_init, 1)
                dve.wait_ge(s_init, 1)
                for par in range(2):
                    half = slice(SEQ * par, SEQ * par + SEQ)
                    nc.vector.memset(vbd[half, :, :, :, par, DX], 1.0)
                dve.wait_ge(s_w, 16 * 9)
                nc.vector.tensor_scalar(bq_scaled[:], bq_s[:], SCALE, None, ALU.mult
                                        ).then_inc(s_const, 1)

                def limits(g, e):
                    if past(g, 1):
                        dve.wait_ge(lim_d, g)
                    if past(g, 2):
                        dve.wait_ge(min_d, (g - 1) * GT)
                    nc.vector.tensor_copy(masked[:], mask_s[:, bass.ds(g * GT, GT), :]
                                          ).then_inc(mk_d, 1)
                    dve.wait_ge(mk_d, 2 * g + 1)
                    nc.vector.tensor_scalar(masked[:], masked[:], -2 * LARGE, LARGE,
                                            ALU.mult, ALU.add).then_inc(mk_d, 1)
                    dve.wait_ge(mk_d, 2 * g + 2)
                    nc.vector.tensor_scalar(limit[:, e], masked[:], NEG, None, ALU.max
                                            ).then_inc(lim_d, 1)

                def values_ev(g, e, bank):
                    dve.wait_ge(v_mm, g + 1)
                    if past(g, 2):
                        dve.wait_ge(av_mm, (g - 1) * GT)
                    for b in range(2):
                        for par in range(2):
                            rows = slice(SEQ * b, SEQ * b + SEQ)
                            half = slice(SEQ * par, SEQ * par + SEQ)
                            last = nc.vector.tensor_tensor(
                                vbd[half, e, b::2, :, par, 0:DX],
                                banks[rows, bank, :].rearrange(
                                    "p (t j h d) -> p t j h d", t=GT, j=PAIRS, h=2)[:, :, :, par, :],
                                bv_s[rows, :].rearrange("p (j h d) -> p j h d", j=PAIRS, h=2)[
                                    :, None, :, par, :].to_broadcast([SEQ, GT, PAIRS, DX]), ALU.add)
                    last.then_inc(v_ev, 1)

                def slot(t, it, k):
                    if there(t, 4):
                        dve.wait_ge(av_mm, t - 3)
                        o = banks[:, O_BANK + k % 2, 0:HX * DV].rearrange("p (h d) -> p h d", h=HX)
                        nc.vector.reciprocal(rsum[:], o[:, :, DX]).then_inc(rs_d, 1)
                    if there(t, 6):
                        dve.wait_ge(rstd_d, t - 5)
                        if past(t, 8):
                            dve.wait_ge(xt_mm, t - 7)
                            dve.wait_ge(keep_d, t - 7)
                        nc.vector.tensor_scalar(xn[:, k % 2, :], resid[:, k % 2, :],
                                                moments[:, k % 2, 0:1], rstd[:, k % 2:k % 2 + 1],
                                                ALU.subtract, ALU.mult).then_inc(ln_d, 1)
                    if there(t, 4):
                        dve.wait_ge(rs_d, t - 3)
                        if past(t, 6):
                            dve.wait_ge(at_mm, t - 5)
                        nc.vector.tensor_tensor(
                            attn[:, k % 2, :].rearrange("p (h d) -> p h d", h=HX), o[:, :, 0:DX],
                            rsum[:, :, None].to_broadcast([P, HX, DX]), ALU.mult
                        ).then_inc(an_d, 1)
                    p_all = prob[:, k % 4]
                    if there(t, 0):
                        dve.wait_ge(s_mm, t + 1)
                        if k % GT == 0:
                            dve.wait_ge(lim_d, group(it, k) + 1)
                        if past(t, 4):
                            dve.wait_ge(tp_mm, 2 * (t - 3))
                        nc.vector.tensor_tensor(
                            p_all, banks[:, S_BANK:S_BANK + 2, :].rearrange(
                                "p r (h k) -> p (r h) k", k=SEQ),
                            limit[:, k // GT, k % GT, None, :].to_broadcast([P, HX, SEQ]),
                            ALU.min).then_inc(min_d, 1)
                    if turns(t, k):
                        values_ev(group(it, k), k // GT, O_BANK + (k - 1) % 2)
                    if there(t, 5):
                        dve.wait_ge(wo_mm, t - 4)
                        if (k - 5) % GT == 0:
                            dve.wait_ge(xb_d, group(it, k - 5) + 1)
                        if past(t, 7):
                            dve.wait_ge(ln_d, t - 6)
                        nc.vector.tensor_tensor(resid[:, None, (k - 5) % 2, :],
                                                banks[:, None, W_BANK, WO_COL:WO_COL + D],
                                                stream[:, bass.ds(t - 5, 1), 0:D], ALU.add
                                                ).then_inc(y_d, 1)
                    if there(t, 5):
                        dve.wait_ge(y_d, t - 4)
                        nc.vector.bn_stats(stats[:], resid[:, (k - 5) % 2, :]).then_inc(st_d, 1)
                    if feeds(t, k, 1):
                        limits(group(it, k) + 1, 1 - k // GT)
                    if there(t, 5):
                        dve.wait_ge(st_d, t - 4)
                        dve.sem_inc(carry_d, 1)
                        nc.vector.bn_aggr(moments[:, (k - 5) % 2, :], stats[:]).then_inc(mom_d, 1)
                    if there(t, 0):
                        dve.wait_ge(min_d, t + 1)
                        if past(t, 2):
                            dve.wait_ge(sub_d, t - 1)
                        nc.vector.reduce_max(top[:, k % 2, :], p_all, AX.X).then_inc(max_d, 1)
                dve.wait_ge(s_m, 16)
                limits(0, 0)
                values_ev(0, 0, O_BANK)
                slots(dve, slot)


def experts(nc, switch_b, w1, b1T, w2, b2, sorted_x, out, stream, ident, eps, banks, logits):
    from contextlib import ExitStack
    with ExitStack() as ctx:
        def sb(name, shape, dt=F32):
            return ctx.enter_context(nc.sbuf_tensor("c_" + name, shape, dt))

        we_s = sb("we", [P, EXPERTS, FF + D + FC])
        w2_s = sb("w2", [P, EXPERTS, FC, D])
        tile_expert = sb("tile_expert", [P, XTILES], I32)
        route(nc, switch_b, w1, b1T, w2, b2, we_s, w2_s, tile_expert, sorted_x,
              stream, banks, logits)
        expert_tiles(nc, we_s, w2_s, tile_expert, sorted_x, out, ident, eps, banks)


def route(nc, switch_b, w1, b1T, w2, b2, we_s, w2_s, tile_expert, sorted_x,
          stream, banks, logits):
    from contextlib import ExitStack
    ctx = ExitStack()
    with ctx:
        def sb(name, shape, dt=F32):
            return ctx.enter_context(nc.sbuf_tensor("c_" + name, shape, dt))

        def sem(name):
            return ctx.enter_context(nc.semaphore("c_" + name))

        COLS = TILES * EXPERTS
        sb_s = sb("switch_b", [P, EXPERTS])
        ones = sb("ones", [P, P])
        before = sb("before", [P, P])
        count_i = sb("count_i", [P, P], I32)
        count = sb("count", [P, P])
        full_at = sb("full_at", [P, TILES])
        late_e = sb("late_e", [P, EXPERTS])
        token = sb("token", [P, TILES], I32)
        going = sb("going", [P, EXPERTS, TILES])
        prob = sb("prob", [P, TILES, EXPERTS])
        top = sb("top", [P, TILES])
        rsum = sb("rsum", [P, TILES])
        gate = sb("gate", [P, TILES])
        choice = sb("choice", [P, TILES])
        cand = sb("cand", [P, TILES, EXPERTS])
        onehot = sb("onehot", [P, TILES, EXPERTS])
        total = sb("total", [P, EXPERTS, TILES])
        upto = sb("upto", [P, EXPERTS, TILES])
        excl = sb("excl", [P, EXPERTS, TILES])
        opens = sb("opens", [P, EXPERTS, TILES])
        etiles = sb("etiles", [P, EXPERTS])
        etend = sb("etend", [P, EXPERTS])
        etfirst = sb("etfirst", [P, EXPERTS])
        rank = sb("rank", [P, TILES, EXPERTS])
        slot_f = sb("slot_f", [P, TILES])
        slot_i = sb("slot_i", [P, TILES], I32)
        passed = sb("passed", [P, XTILES, EXPERTS])
        te = sb("te", [P, XTILES])

        s_sb, s_w, s_const, s_iota = map(sem, ("switch_b", "weights", "const", "iota"))
        v, s_exp, s_mm, s_slot, s_meta, s_scat = map(sem, (
            "vector_step", "exp", "rank_mm", "slot", "meta", "scatter"))
        RANK_BANK, TOTAL_BANK = 0, 1

        with nc.Block() as block:
            @block.sync
            def _(sp):
                sp.dma_start(sb_s[:], switch_b[None, :].to_broadcast([P, EXPERTS])
                             ).then_inc(s_sb, 16)
                sp.dma_start(we_s[:, :, 0:FF], w1.rearrange("e d f -> d e f")).then_inc(s_w, 16)
                sp.dma_start(w2_s[:], w2.rearrange("e (c p) d -> p e c d", p=P)).then_inc(s_w, 16)
                sp.dma_start(we_s[:, :, FF:FF + D], b2[None, :, :].to_broadcast([P, EXPERTS, D])
                             ).then_inc(s_w, 16)
                sp.dma_start(we_s[:, :, FF + D:FF + D + FC], b1T.rearrange("p (e c) -> p e c", c=FC)).then_inc(s_w, 16)
                sp.wait_ge(s_w, 16 * 4)

            @block.gpsimd
            def _(pool):
                nc.gpsimd.iota(token[:], pattern=[[P, TILES]], base=0, channel_multiplier=1
                               ).then_inc(s_iota, 1)
                nc.gpsimd.iota(count_i[:], pattern=[[1, P]], base=0, channel_multiplier=0
                               ).then_inc(s_iota, 1)
                nc.gpsimd.memset(ones[:], 1.0)
                nc.gpsimd.memset(before[:], 1.0)
                nc.gpsimd.memset(going[:], 1.0).then_inc(s_iota, 1)
                pool.wait_ge(s_iota, 3)
                nc.gpsimd.memset(going[:, :, 0], 0.0)
                nc.gpsimd.affine_select(out=before[:], in_=before[:], compare_op=ALU.is_ge,
                                        fill=0.0, base=-1, pattern=[[1, P]],
                                        channel_multiplier=-1).then_inc(s_const, 1)
                pool.wait_ge(s_slot, 1)
                pool.wait_ge(s_meta, 2)
                for t in range(TILES):
                    nc.gpsimd.indirect_dma_start(
                        out=sorted_x[:, :],
                        out_offset=bass.IndirectOffsetOnAxis(ap=slot_i[:, t:t + 1], axis=0),
                        in_=stream[:, t, :], in_offset=None).then_inc(s_scat, 16)
                pool.wait_ge(s_scat, 16 * TILES)

            @block.tensor
            def _(pe):
                pe.wait_ge(s_const, 1)
                pe.wait_ge(v, 9)
                flat = onehot[:].rearrange("p t e -> p (t e)")
                nc.tensor.matmul(banks[:, TOTAL_BANK, :], ones[:], flat, start=True, stop=True
                                 ).then_inc(s_mm, 1)
                nc.tensor.matmul(banks[:, RANK_BANK, :], before[:], flat, start=True, stop=True
                                 ).then_inc(s_mm, 1)

            @block.scalar
            def _(act):
                nc.scalar.preload_act_table_set("natural_log_exp_and_others")
                act.wait_ge(v, 3)
                nc.scalar.activation(prob[:], prob[:], ACT.Exp).then_inc(s_exp, 1)

            @block.vector
            def _(dve):
                tt, ts, stt = (nc.vector.tensor_tensor, nc.vector.tensor_scalar,
                               nc.vector.scalar_tensor_tensor)

                def per_tile(row):
                    return row[:, :, None].to_broadcast([P, TILES, EXPERTS])

                def done(instruction, step):
                    instruction.then_inc(v, 1)
                    dve.wait_ge(v, step)

                dve.wait_ge(s_iota, 2)
                nc.vector.tensor_copy(count[:], count_i[:]).then_inc(s_meta, 1)
                nc.vector.tensor_copy(stream[:, :, D + 1].bitcast(I32), token[:])
                dve.wait_ge(s_sb, 16)
                done(tt(prob[:], logits[:], sb_s[:, None, :].to_broadcast([P, TILES, EXPERTS]),
                        ALU.add), 1)
                done(nc.vector.reduce_max(top[:], prob[:], AX.X), 2)
                done(tt(prob[:], prob[:], per_tile(top), ALU.subtract), 3)
                dve.wait_ge(s_meta, 1)
                ts(late_e[:], count[:, 0:EXPERTS], float(EXPERTS), None, ALU.add)
                ts(full_at[:], count[:, 0:TILES], float(P), None, ALU.mult)
                dve.wait_ge(s_exp, 1)
                done(nc.vector.reduce_sum(rsum[:], prob[:], AX.X), 4)
                done(nc.vector.reciprocal(rsum[:], rsum[:]), 5)
                done(tt(prob[:], prob[:], per_tile(rsum), ALU.mult), 6)
                done(nc.vector.reduce_max(gate[:], prob[:], AX.X), 7)
                nc.vector.tensor_copy(stream[:, :, D], gate[:]).then_inc(s_meta, 1)
                tt(cand[:], prob[:], per_tile(gate), ALU.is_equal).then_inc(s_exp, 1)
                dve.wait_ge(s_exp, 2)
                stt(cand[:], cand[:], -float(EXPERTS),
                    late_e[:, None, :].to_broadcast([P, TILES, EXPERTS]), ALU.mult, ALU.add
                    ).then_inc(s_exp, 1)
                dve.wait_ge(s_exp, 3)
                done(nc.vector.tensor_reduce(choice[:], cand[:], AX.X, ALU.min), 8)
                done(tt(onehot[:], count[:, None, 0:EXPERTS].to_broadcast([P, TILES, EXPERTS]),
                        per_tile(choice), ALU.is_equal), 9)
                dve.wait_ge(s_mm, 1)
                done(nc.vector.tensor_copy(total[:].rearrange("p e t -> p t e"),
                                           banks[:, TOTAL_BANK, :].rearrange(
                                               "p (t e) -> p t e", t=TILES)), 10)
                dve.wait_ge(s_const, 1)
                done(nc.vector.tensor_tensor_scan(
                    upto[:].rearrange("p e t -> p (e t)"), going[:].rearrange("p e t -> p (e t)"),
                    total[:].rearrange("p e t -> p (e t)"), 0.0, ALU.mult, ALU.add), 11)
                tt(excl[:], upto[:], total[:], ALU.subtract)
                done(tt(opens[:], upto[:, :, TILES - 1:TILES].to_broadcast([P, EXPERTS, TILES]),
                        full_at[:, None, :].to_broadcast([P, EXPERTS, TILES]), ALU.is_gt), 12)
                done(nc.vector.reduce_sum(etiles[:], opens[:], AX.X), 13)
                done(nc.vector.tensor_tensor_scan(etend[:], ones[:, 0:EXPERTS], etiles[:], 0.0,
                                                  ALU.mult, ALU.add), 14)
                done(tt(etfirst[:], etend[:], etiles[:], ALU.subtract), 15)
                done(stt(excl[:], etfirst[:, :, None].to_broadcast([P, EXPERTS, TILES]), float(P),
                         excl[:], ALU.mult, ALU.add), 16)
                dve.wait_ge(s_mm, 2)
                done(tt(rank[:], banks[:, RANK_BANK, :].rearrange("p (t e) -> p t e", t=TILES),
                        excl[:].rearrange("p e t -> p t e"), ALU.add), 17)
                done(tt(rank[:], rank[:], onehot[:], ALU.mult), 18)
                done(nc.vector.reduce_sum(slot_f[:], rank[:], AX.X), 19)
                nc.vector.tensor_copy(slot_i[:], slot_f[:]).then_inc(s_slot, 1)
                done(tt(passed[:], count[:, 0:XTILES, None].to_broadcast([P, XTILES, EXPERTS]),
                        etend[:, None, :].to_broadcast([P, XTILES, EXPERTS]), ALU.is_ge), 20)
                done(nc.vector.reduce_sum(te[:], passed[:], AX.X), 21)
                ts(tile_expert[:], te[:], float(EXPERTS - 1), None, ALU.min)


def expert_tiles(nc, we_s, w2_s, tile_expert, sorted_x, out, ident, eps, banks):
    from contextlib import ExitStack
    ctx = ExitStack()
    with ctx:
        def sb(name, shape, dt=F32):
            return ctx.enter_context(nc.sbuf_tensor("d_" + name, shape, dt))

        def sem(name):
            return ctx.enter_context(nc.semaphore("d_" + name))

        LOADS = 12
        BODY = 12
        SCATTERS = 6
        rows = sb("rows", [P, LOADS, ROW])
        xT = sb("xT", [P, 2, P])
        we_now = sb("we_now", [P, 4, FF + D + FC])
        hT = sb("hT", [P, 2, FC, P])
        y = sb("y", [P, D])
        resid = sb("resid", [P, 2, D])
        stats = sb("stats", [P, 6])
        moments = sb("moments", [P, 2, 2])
        power = sb("power", [P, 1])
        veps = sb("veps", [P, 1])
        rstd = sb("rstd", [P, 2])
        final = sb("final", [P, SCATTERS, D])

        s_load = [sem("load%d" % n) for n in range(LOADS)]
        s_out = [sem("out%d" % n) for n in range(SCATTERS)]
        (xt_mm, h_mm, y_mm, xt_ev, w_now, h_ev, y_ev, res_d, st_d, mom_d, rstd_d, fin_d, ve_d,
         s_pow) = map(sem, ("xt_mm", "h_mm", "y_mm", "xt_ev", "w_now", "h_ev", "y_ev", "resid",
                            "stats", "moments", "rstd", "final", "veps", "power"))
        carry_d = sem("carry")
        XT0, H0, Y0 = 0, 2, 6
        HALF = FC // 2

        with nc.Block() as block:
            def slots(eng, slot):
                for t in range(-2, BODY):
                    slot(t, 0, t)
                with eng.Fori(1, (XTILES - 2) // BODY) as it:
                    for k in range(BODY):
                        slot(it * BODY + k, it, k)
                for t in range((XTILES - 2) // BODY * BODY, XTILES + 3):
                    slot(t, t // BODY, t % BODY)

            def there(t, lag):
                return not isinstance(t, int) or 0 <= t - lag < XTILES

            def past(t, first):
                return not isinstance(t, int) or t >= first

            @block.sync
            def _(sp):
                def load(t, it, k):
                    if past(t, LOADS):
                        sp.wait_ge(s_out[(k - LOADS) % SCATTERS], 16 * scatters(it, k, LOADS))
                    sp.dma_start(rows[:, k % LOADS, :], sorted_x[bass.ds(t * P, P), :]
                                 ).then_inc(s_load[k % LOADS], 16)

                def scatters(it, k, lag):
                    return it * (BODY // SCATTERS) + (k - lag) // SCATTERS + 1

                for t in range(BODY):
                    load(t, 0, t)
                with sp.Fori(1, XTILES // BODY) as it:
                    for k in range(BODY):
                        load(it * BODY + k, it, k)
                for t in range(XTILES // BODY * BODY, XTILES):
                    load(t, t // BODY, t % BODY)

            @block.gpsimd
            def _(pool):
                nc.gpsimd.memset(power[:], -0.5).then_inc(s_pow, 1)
                pool.wait_ge(s_pow, 1)

                def slot(t, it, k):
                    if there(t, 2):
                        pool.wait_ge(mom_d, t - 1)
                        nc.gpsimd.tensor_tensor(veps[:], moments[:, k % 2, 1:2], eps[:], ALU.add
                                                ).then_inc(ve_d, 1)
                        pool.wait_ge(ve_d, t - 1)
                        if past(t, 4):
                            pool.wait_ge(fin_d, t - 3)
                        nc.gpsimd.tensor_tensor(rstd[:, k % 2:k % 2 + 1], veps[:], power[:], ALU.pow
                                                ).then_inc(rstd_d, 1)
                    if there(t, 3):
                        pool.wait_ge(fin_d, t - 2)
                        pool.sem_inc(carry_d, 1)
                        nc.gpsimd.indirect_dma_start(
                            out=out[:, :],
                            out_offset=bass.IndirectOffsetOnAxis(
                                ap=rows[:, (k - 3) % LOADS, D + 1:D + 2].bitcast(I32), axis=0),
                            in_=final[:, (k - 3) % SCATTERS, :], in_offset=None,
                            bounds_check=TOKENS - 1, oob_is_err=False
                        ).then_inc(s_out[(k - 3) % SCATTERS], 16)
                slots(pool, slot)
                for n in range(SCATTERS):
                    pool.wait_ge(s_out[n], 16 * ((XTILES - 1 - n) // SCATTERS + 1))

            @block.tensor
            def _(pe):
                def slot(t, it, k):
                    if there(t, 0):
                        pe.wait_ge(xt_ev, t + 1)
                        pe.wait_ge(w_now, t + 1)
                        if past(t, 2):
                            pe.wait_ge(h_ev, (t - 1) * FC)
                        for c in range(FC):
                            bank = H0 + 2 * (k % 2) + c // HALF
                            last = nc.tensor.matmul(banks[:, bank, c % HALF * P:(c % HALF + 1) * P],
                                                    we_now[:, k % 4, c * P:(c + 1) * P],
                                                    xT[:, k % 2, :], start=True, stop=True)
                            if c % HALF == HALF - 1:
                                last.then_inc(h_mm, 1)
                    if there(t, 1):
                        e = nc.tensor.value_load(tile_expert[0:1, bass.ds(t - 1, 1)],
                                                 min_val=0, max_val=EXPERTS - 1)
                    if there(t, -1):
                        pe.wait_ge(s_load[(k + 1) % LOADS],
                                   16 * (it * (BODY // LOADS) + (k + 1) // LOADS + 1))
                        if past(t, 1):
                            pe.wait_ge(xt_ev, t)
                        nc.tensor.transpose(banks[:, XT0 + (k + 1) % 2, 0:P],
                                            rows[:, (k + 1) % LOADS, 0:D], ident[:]
                                            ).then_inc(xt_mm, 1)
                    if there(t, 1):
                        if past(t, 3):
                            pe.wait_ge(y_ev, t - 2)
                        for c in range(FC):
                            pe.wait_ge(h_ev, (t - 1) * FC + (c + 1))
                            last = nc.tensor.matmul(banks[:, Y0 + (k - 1) % 2, 0:D],
                                                    hT[:, (k - 1) % 2, c, :],
                                                    w2_s[:, bass.ds(e, 1), c, :].rearrange(
                                                        "p e d -> p (e d)"),
                                                    start=c == 0, stop=c == FC - 1)
                        last.then_inc(y_mm, 1)
                slots(pe, slot)

            @block.scalar
            def _(act):
                nc.scalar.preload_act_table_set("gelu_apprx_tanh_and_others")

                def slot(t, it, k):
                    if there(t, 0):
                        if past(t, 2):
                            act.wait_ge(y_mm, t - 1)
                        for c in range(FC):
                            bank = H0 + 2 * (k % 2) + c // HALF
                            if c % HALF == 0:
                                act.wait_ge(h_mm, t * 2 + (c // HALF + 1))
                            nc.scalar.activation(hT[:, k % 2, c, :],
                                                 banks[:, bank, c % HALF * P:(c % HALF + 1) * P],
                                                 ACT.Gelu_apprx_tanh,
                                                 bias=we_now[:, k % 4, FF + D + c:FF + D + c + 1]).then_inc(h_ev, 1)
                    if there(t, -1):
                        act.wait_ge(xt_mm, t + 2)
                        if past(t, 1):
                            act.wait_ge(h_mm, 2 * t)
                        nc.scalar.activation(xT[:, (k + 1) % 2, :],
                                             banks[:, XT0 + (k + 1) % 2, 0:P], ACT.Copy
                                             ).then_inc(xt_ev, 1)
                slots(act, slot)

            @block.vector
            def _(dve):
                def slot(t, it, k):
                    if there(t, 2):
                        dve.wait_ge(y_mm, t - 1)
                        if past(t, 3):
                            dve.wait_ge(res_d, t - 2)
                        nc.vector.tensor_tensor(y[:], banks[:, Y0 + k % 2, 0:D],
                                                we_now[:, (k - 2) % 4, FF:FF + D], ALU.add
                                                ).then_inc(y_ev, 1)
                    if there(t, 2):
                        dve.wait_ge(y_ev, t - 1)
                        if past(t, 4):
                            dve.wait_ge(fin_d, t - 3)
                        nc.vector.scalar_tensor_tensor(
                            resid[:, k % 2, :], y[:], rows[:, (k - 2) % LOADS, D:D + 1],
                            rows[:, (k - 2) % LOADS, 0:D], ALU.mult, ALU.add).then_inc(res_d, 1)
                        dve.wait_ge(res_d, t - 1)
                        if past(t, 3):
                            dve.wait_ge(mom_d, t - 2)
                        nc.vector.bn_stats(stats[:], resid[:, k % 2, :]).then_inc(st_d, 1)
                    if there(t, 3):
                        dve.wait_ge(rstd_d, t - 2)
                        if past(t, 3 + SCATTERS):
                            dve.wait_ge(s_out[(k - 3) % SCATTERS],
                                        16 * (it * (BODY // SCATTERS) + (k - 3 - SCATTERS) // SCATTERS + 1))
                        nc.vector.tensor_scalar(final[:, (k - 3) % SCATTERS, :], resid[:, (k - 3) % 2, :],
                                                moments[:, (k - 3) % 2, 0:1],
                                                rstd[:, (k - 3) % 2:(k - 3) % 2 + 1],
                                                ALU.subtract, ALU.mult).then_inc(fin_d, 1)
                    if there(t, -2):
                        e = nc.vector.value_load(tile_expert[0:1, bass.ds(t + 2, 1)],
                                                 min_val=0, max_val=EXPERTS - 1)
                    if there(t, 2):
                        dve.wait_ge(st_d, t - 1)
                        if past(t, 4):
                            dve.wait_ge(fin_d, t - 3)
                        dve.sem_inc(carry_d, 1)
                        nc.vector.bn_aggr(moments[:, k % 2, :], stats[:]).then_inc(mom_d, 1)
                    if there(t, -2):
                        if past(t, 2):
                            dve.wait_ge(y_ev, t - 1)
                        nc.vector.tensor_copy(we_now[:, (k + 2) % 4, None, :],
                                              we_s[:, bass.ds(e, 1), :]).then_inc(w_now, 1)
                slots(dve, slot)


_ORDER = ["x", "xT", "ctxT", "mask", "Wq", "Wk", "Wv", "Wg", "Wgk1", "Wgk2", "bgk2", "rms_w", "Wo",
          "wq", "bq", "wk", "bk", "wv", "bv", "wo", "bo", "switch_w", "switch_b",
          "w1", "b1T", "w2", "b2"]


def kernel(**inputs):
    import numpy as _np
    import concourse.bacc as _bacc
    from concourse import mybir as _mybir
    from concourse.bass_utils import run_bass_kernel_spmd as _run

    given = {k: _np.asarray(v) for k, v in inputs.items()}
    x = given["x"].reshape(-1, given["x"].shape[-1])
    context = given["ctx_1024"].reshape(-1, given["ctx_1024"].shape[-1])
    mask = given["mask_Bx1xSxS2_bf0"]
    arrays = {"x": x, "xT": x.T, "ctxT": context.T,
              "mask": mask.reshape(-1, mask.shape[-1])}
    for name in _ORDER[4:]:
        stage = ("L0_attn_" if name in _ORDER[4:13] else
                 "L0_xattn_" if name in _ORDER[13:21] else "L0_ffn_")
        if name == "b1T":
            arrays[name] = given[stage + "b1"].reshape(-1, x.shape[-1]).T
        else:
            arrays[name] = given[stage + name]
    nc = _bacc.Bacc("TRN2", target_bir_lowering=False, num_devices=1)
    args = []
    for name in _ORDER:
        arrays[name] = _np.ascontiguousarray(arrays[name])
        args.append(nc.dram_tensor("in_" + name, arrays[name].shape,
                                   _mybir.dt.from_np(arrays[name].dtype), kind="ExternalInput").ap())
    args.append(nc.dram_tensor("out", x.shape, _mybir.dt.float32, kind="ExternalOutput").ap())
    decoder_layer(nc, *args)
    result = _run(nc, [{"in_" + k: v for k, v in arrays.items()}], core_ids=[0])
    return result.results[0]["out"].reshape(given["x"].shape)
```

```python
import concourse.bass as bass
from concourse import mybir

F32 = mybir.dt.float32
I32 = mybir.dt.int32
U8 = mybir.dt.uint8
ALU = mybir.AluOpType
ACT = mybir.ActivationFunctionType
AX = mybir.AxisListType

P = 128
BATCH, SEQ, D = 128, 64, 128
TOKENS = BATCH * SEQ
TILES = TOKENS // P
GROUP = 512
GT = GROUP // P
GB = GROUP // SEQ
GROUPS = TOKENS // GROUP
HA, DKA, DVA = 4, 32, 64
VD = HA * DVA
LOWRANK = 16
GATE_NORM = 16.0
HX, DX = 16, 8
NEG = -1.0e9
LARGE = 1.5e38
EPS = 1e-5
EXPERTS, FF = 8, 512
FC = FF // P
ROW = D + 2
XTILES = TILES + EXPERTS - 1
ETILES = TILES + 1
CHUNK = 8
CLAMP = 40.0
SILU_CLAMP = -44.0


def decoder_layer(nc, x, xT, ctxT, mask, Wq, Wk, Wv, Wg, Wgk1, Wgk2, bgk2, rms_w, Wo,
                  wq, bq, wk, bk, wv, bv, wo, bo, switch_w, switch_b, w1, b1T, w2, b2, out):
    sorted_x = nc.dram_tensor("sorted_x", (EXPERTS * (ETILES + 1) * P, ROW), F32,
                              kind="Internal").ap()

    with (
        nc.sbuf_tensor("stream", [P, TILES, ROW], F32) as stream,
        nc.sbuf_tensor("streamT", [P, TOKENS], F32) as streamT,
        nc.sbuf_tensor("ident", [P, P], F32) as ident,
        nc.sbuf_tensor("eps", [P, 1], F32) as eps,
        nc.psum_tensor("banks", [P, 8, 512], F32) as banks,
        nc.sbuf_tensor("b_ctx", [P, 2, GROUP], F32) as ctx_s,
        nc.sbuf_tensor("b_mask", [P, TILES, SEQ], U8) as mask_s,
        nc.sbuf_tensor("b_wq", [P, D], F32) as wq_s, nc.sbuf_tensor("b_wk", [P, D], F32) as wk_s,
        nc.sbuf_tensor("b_wv", [P, D], F32) as wv_s, nc.sbuf_tensor("b_wo", [P, D], F32) as wo_s,
        nc.sbuf_tensor("b_sw", [P, EXPERTS], F32) as sw_s,
        nc.sbuf_tensor("b_bq", [P, 1], F32) as bq_s, nc.sbuf_tensor("b_bk", [P, 1], F32) as bk_s,
        nc.sbuf_tensor("b_bv", [P, D], F32) as bv_s, nc.sbuf_tensor("b_bo", [P, D], F32) as bo_s,
        nc.sbuf_tensor("b_sb", [P, EXPERTS], F32) as sb_s,
    ):
        loads_b = ((wq_s[:], wq), (wk_s[:], wk), (wv_s[:], wv), (wo_s[:], wo), (sw_s[:], switch_w),
                   (bq_s[:], bq[:, None]), (bk_s[:], bk[:, None]),
                   (bv_s[:], bv[None, :].to_broadcast([P, D])),
                   (bo_s[:], bo[None, :].to_broadcast([P, D])),
                   (sb_s[:], switch_b[None, :].to_broadcast([P, EXPERTS])),
                   (ctx_s[:], ctxT[:, 0:2 * GROUP].rearrange("p (g t) -> p g t", g=2)),
                   (mask_s[:], mask.rearrange("(t p) k -> p t k", p=P)))
        weights_b = (wq_s, wk_s, wv_s, wo_s, sw_s, bq_s, bk_s, bv_s, bo_s, sb_s)
        linear_attention(nc, x, xT, Wq, Wk, Wv, Wg, Wgk1, Wgk2, bgk2, rms_w, Wo,
                         loads_b, stream, streamT, ident, eps, banks)
        with (
            nc.sbuf_tensor("be", [P, EXPERTS, D + FC], F32) as be_s,
            nc.sbuf_tensor("tile_expert", [P, XTILES], I32) as tile_expert,
            nc.sbuf_tensor("tile_row", [P, XTILES], I32) as tile_row,
        ):
            w1_s = streamT[:, 0:EXPERTS * FF].rearrange("p (e f) -> p e f", e=EXPERTS)
            w2_s = streamT[:, EXPERTS * FF:].rearrange("p (e c d) -> p e c d", e=EXPERTS, c=FC)
            cross_attention(nc, ctxT, ctx_s, mask_s, weights_b,
                            w1, b1T, w2, b2, sorted_x, stream, streamT, ident, eps, banks,
                            w1_s, w2_s, be_s, tile_expert, tile_row)
            expert_tiles(nc, w1_s, w2_s, be_s, tile_expert, tile_row, sorted_x, out, ident, eps,
                         banks)


def linear_attention(nc, x, xT, Wq, Wk, Wv, Wg, Wgk1, Wgk2, bgk2, rms_w, Wo, loads_b,
                     stream, streamT, ident, eps, banks):
    from contextlib import ExitStack
    ctx = ExitStack()
    with ctx:
        def sb(name, shape, dt=F32):
            return ctx.enter_context(nc.sbuf_tensor("a_" + name, shape, dt))

        def sem(name):
            return ctx.enter_context(nc.semaphore("a_" + name))

        wq_s, wk_s = sb("wq", [P, P]), sb("wk", [P, P])
        wv_s, wg_s = sb("wv", [P, VD]), sb("wg", [P, VD])
        gk1_s = sb("gk1", [P, P])
        gk1T = sb("gk1T", [P, P])
        gk2_s = sb("gk2", [P, P])
        wgk_s = sb("wgk", [P, P])
        bgk_s, rms_s = sb("bgk", [P, 1]), sb("rms", [P, 1])
        wo_s = sb("wo", [P, 2, D])
        head_mean = sb("head_mean", [P, P])
        causal = sb("causal", [P, P])
        xTs = sb("xT", [P, 2, GROUP])
        uclamp = sb("uclamp", [P, GROUP])
        espl = sb("espl", [P, GROUP])
        lspl = sb("lspl", [P, GROUP])
        negsig = sb("negsig", [P, GROUP])
        egd = sb("egd", [P, 2, GROUP])
        qg = sb("qg", [P, 2, GT, HA, P])
        kn = sb("kn", [P, 2, GROUP])
        val = sb("val", [P, 2, GT, VD])
        gate = sb("gate", [P, 2, 2, GROUP])
        gexp = sb("gexp", [P, 2, GROUP])
        glog = sb("glog", [P, 2, 2, GROUP])
        scores = sb("scores", [P, 2, HA, P])
        square = sb("square", [P, 2, GROUP])
        o_s = sb("o", [P, 2, GROUP])
        og = sb("og", [P, 2, GROUP])
        lms = sb("lms", [P, 2, GROUP])
        wlog = sb("wlog", [P, 2, GROUP])
        wexp = sb("wexp", [P, 2, GROUP])
        ogate = sb("ogate", [P, 2, GROUP])
        resid = sb("resid", [P, GT, D])
        xn = sb("xn", [P, GT, D])
        stats = sb("stats", [P, GT, 6])
        moments = sb("moments", [P, GT, 2])
        lvar = sb("lvar", [P, GT])
        rstd = sb("rstd", [P, GT])

        s_w, s_wqk, s_wl, s_wb = map(sem, ("weights", "qk_weights", "late_weights", "b_weights"))
        s_zero, s_const, s_wo, s_dz = map(sem, ("zeros", "constants", "wo_scaled", "dve_zeros"))
        g_tr, g_ev, w_mm, w_ev = map(sem, ("gk1_mm", "gk1_ev", "wgk_mm", "wgk_ev"))
        carry_d = sem("carry")
        s_x = [sem("x0"), sem("x1")]
        (u_mm, q_mm, k_mm, v_mm, g_mm, at_mm, ot_mm, ms_mm, wo_mm, xt_mm) = map(sem, (
            "u_mm", "q_mm", "k_mm", "v_mm", "g_mm", "at_mm", "ot_mm", "ms_mm", "wo_mm", "xt_mm"))
        (espl_d, lspl_d, val_d, egd_d, gexp_d, glog_d, sq_d, os_d, lms_d, wexp_d, lvar_d, rstd_d,
         xt_ev) = map(sem, ("espl", "lspl", "val", "egd", "gexp", "glog", "sq", "o", "lms",
                            "wexp", "lvar", "rstd", "xt_ev"))
        (sc_ev, wlog_d, uc_d, ns_d, y_d, st_d, mom_d, ln_d, gate_d, qg_d, kn_d, fin_d) = map(
            sem, ("sc_ev", "wlog", "uclamp", "negsig", "resid", "stats", "moments", "ln", "gate",
                  "qg", "kn", "ogate"))
        og_d, keep_d = sem("og"), sem("keep")

        U_BANK, A_BANK, B_BANK, V_BANK, AT_BANK, OT_BANK = 0, 1, 2, 3, 5, 6

        with nc.Block() as block:
            def steps(eng, body):
                for i in range(-1, 3):
                    body(i, i % 2, (i + 1) // 2)
                with eng.Fori(0, (GROUPS - 6) // 2) as pair:
                    for k in range(2):
                        body(pair * 2 + (3 + k), 1 - k, pair + 2)
                for i in range(GROUPS - 3, GROUPS + 2):
                    body(i, i % 2, (i + 1) // 2)

            def there(i, step):
                return not isinstance(i, int) or 0 <= i + step < GROUPS

            @block.sync
            def _(sp):
                def load(step, e):
                    sp.dma_start(xTs[:, e, :], xT[:, bass.ds(step * GROUP, GROUP)]
                                 ).then_inc(s_x[e], 16)
                    sp.dma_start(stream[:, bass.ds(step * GT, GT), 0:D],
                                 x[bass.ds(step * GROUP, GROUP), :].rearrange(
                                     "(t p) d -> p t d", p=P)).then_inc(s_x[e], 16)

                sp.wait_ge(s_zero, 2)
                for dst, src in ((gk1_s[:, 0:LOWRANK], Wgk1), (gk2_s[0:LOWRANK, :], Wgk2),
                                 (wv_s[:], Wv), (bgk_s[:], bgk2[:, None])):
                    sp.dma_start(dst, src).then_inc(s_w, 16)
                load(0, 0)
                for dst, src in ((wg_s[:], Wg), (wq_s[:], Wq), (wk_s[:], Wk)):
                    sp.dma_start(dst, src).then_inc(s_wqk, 16)
                load(1, 1)
                for dst, src in ((rms_s[0:DVA, :], rms_w[:, None]),
                                 (rms_s[DVA:P, :], rms_w[:, None]),
                                 (wo_s[:], Wo.rearrange("(c p) d -> p c d", p=P))):
                    sp.dma_start(dst, src).then_inc(s_wl, 16)

                def body(i, p, er):
                    if there(i, 0) and there(i, 2):
                        sp.wait_ge(q_mm, i + 1)
                        load(i + 2, p)
                    if isinstance(i, int) and i == 0:
                        for dst, src in loads_b:
                            sp.dma_start(dst, src).then_inc(s_wb, 16)
                steps(sp, body)
                sp.wait_ge(s_wb, 16 * len(loads_b))

            @block.gpsimd
            def _(pool):
                nc.gpsimd.memset(gk1_s[:], 0.0).then_inc(s_zero, 1)
                nc.gpsimd.memset(gk2_s[:], 0.0).then_inc(s_zero, 1)
                nc.gpsimd.memset(eps[:], EPS)
                nc.gpsimd.memset(head_mean[:], 0.0)
                nc.gpsimd.memset(causal[:], 1.0)
                nc.gpsimd.memset(ident[:], 0.0).then_inc(s_zero, 1)
                pool.wait_ge(s_zero, 3)
                nc.gpsimd.affine_select(out=ident[:], in_=ident[:], compare_op=ALU.not_equal,
                                        fill=1.0, base=0, pattern=[[-1, P]], channel_multiplier=1)
                nc.gpsimd.affine_select(out=causal[:], in_=causal[:], compare_op=ALU.is_ge,
                                        fill=0.0, base=0, pattern=[[1, P]],
                                        channel_multiplier=-1).then_inc(s_zero, 1)
                pool.wait_ge(s_zero, 4)
                nc.gpsimd.memset(causal[0:SEQ, SEQ:P], 0.0).then_inc(s_zero, 1)
                pool.wait_ge(s_zero, 5)
                nc.gpsimd.memset(head_mean[0:DVA, 0:DVA], 1.0 / DVA).then_inc(s_zero, 1)
                pool.wait_ge(s_zero, 6)
                nc.gpsimd.memset(head_mean[DVA:P, DVA:P], 1.0 / DVA).then_inc(s_const, 1)
                pool.wait_ge(s_const, 1)

                def body(i, p, er):
                    if there(i, -1):
                        for c in range(2):
                            pool.wait_ge(os_d, 2 * i - 1 + c)
                            pool.wait_ge(gate_d, 2 * i)
                            if there(i, -2):
                                pool.wait_ge(fin_d, 2 * (i - 1))
                            nc.gpsimd.tensor_tensor(og[:, c, :], o_s[:, c, :],
                                                    gate[:, 1 - p, c, :], ALU.mult).then_inc(og_d, 1)
                    if there(i, -2):
                        pool.wait_ge(ln_d, i - 1)
                        nc.gpsimd.tensor_copy(stream[:, bass.ds((i - 2) * GT, GT), 0:D], xn[:]
                                              ).then_inc(keep_d, 1)
                steps(pool, body)

            @block.tensor
            def _(pe):
                mm = nc.tensor.matmul
                pe.wait_ge(s_w, 16 * 4)
                pe.wait_ge(s_const, 1)
                nc.tensor.transpose(banks[:, AT_BANK, 0:P], gk1_s[:], ident[:]).then_inc(g_tr, 1)
                pe.wait_ge(g_ev, 1)
                mm(banks[:, OT_BANK, 0:P], gk1T[:], gk2_s[:], start=True, stop=True
                   ).then_inc(w_mm, 1)
                pe.wait_ge(w_ev, 1)

                def body(i, p, er):
                    e = 1 - p
                    early, mid, late, end = (there(i, n) for n in (1, 0, -1, -2))

                    def scores_mm(t):
                        if not mid:
                            return
                        if t == 0:
                            pe.wait_ge(qg_d, i + 1)
                            pe.wait_ge(kn_d, i + 1)
                        if t > 0 or late:
                            pe.wait_ge(sc_ev, i * GT + t)
                        mm(banks[:, AT_BANK, :], kn[:, p, t * P:(t + 1) * P],
                           qg[:, p, t].rearrange("p h c -> p (h c)"),
                           start=True, stop=True).then_inc(at_mm, 1)

                    def out_mm(t):
                        if not mid:
                            return
                        pe.wait_ge(sc_ev, i * GT + (t + 1))
                        if t == 0:
                            pe.wait_ge(val_d, 2 * (i + 1))
                            if late:
                                pe.wait_ge(os_d, 2 * i)
                                pe.wait_ge(sq_d, 2 * i)
                        for h in range(HA):
                            half = DVA * (h % 2)
                            last = mm(banks[half:half + DVA, OT_BANK + h // 2, t * P:(t + 1) * P],
                                      val[:, p, t, h * DVA:(h + 1) * DVA], scores[:, t % 2, h, :],
                                      start=True, stop=True)
                        last.then_inc(ot_mm, 1)

                    def gate_mm(c):
                        if not early:
                            return
                        if c == 0 and not mid:
                            pe.wait_ge(s_wqk, 16 * 3)
                        if late:
                            pe.wait_ge(lms_d, 2 * i - 1 + c)
                        elif mid:
                            pe.wait_ge(qg_d, i + 1)
                            pe.wait_ge(kn_d, i + 1)
                        mm(banks[:, A_BANK + c, :], wg_s[:, c * P:(c + 1) * P], xTs[:, e, :],
                           start=True, stop=True).then_inc(g_mm, 1)

                    if early:
                        pe.wait_ge(s_x[e], 32 * (er + 1))
                        if mid:
                            pe.wait_ge(ns_d, i + 1)
                        mm(banks[:, U_BANK, :], wgk_s[:], xTs[:, e, :],
                           start=True, stop=True).then_inc(u_mm, 1)
                        for c in range(2):
                            if c == 0 and end:
                                pe.wait_ge(y_d, i - 1)
                            if c == 1 and there(i, -3):
                                pe.wait_ge(xt_ev, i - 2)
                            for t in range(2):
                                first = (2 * c + t) * P
                                last = mm(banks[:, V_BANK + c, t * VD:(t + 1) * VD],
                                          xTs[:, e, first:first + P], wv_s[:],
                                          start=True, stop=True)
                            last.then_inc(v_mm, 1)
                    if late:
                        for c in range(2):
                            if mid:
                                pe.wait_ge((kn_d, qg_d)[c], i + 1)
                            pe.wait_ge(sq_d, 2 * i - 1 + c)
                            mm(banks[:, A_BANK + c, :], head_mean[:], square[:, c, :],
                               start=True, stop=True).then_inc(ms_mm, 1)
                    scores_mm(0)
                    gate_mm(0)
                    scores_mm(1)
                    out_mm(0)
                    gate_mm(1)
                    scores_mm(2)
                    out_mm(1)
                    if end:
                        pe.wait_ge(ln_d, i - 1)
                        if early:
                            pe.wait_ge(val_d, 2 * (i + 2))
                        elif there(i, -3):
                            pe.wait_ge(xt_ev, i - 2)
                        for t in range(GT):
                            last = nc.tensor.transpose(banks[:, V_BANK + 1, t * P:(t + 1) * P],
                                                       xn[:, t, :], ident[:])
                        last.then_inc(xt_mm, 1)
                    scores_mm(3)
                    out_mm(2)
                    if late:
                        pe.wait_ge(s_wo, 1)
                        if early:
                            pe.wait_ge(val_d, 2 * (i + 1) + 1)
                        elif end:
                            pe.wait_ge(y_d, i - 1)
                        pe.wait_ge(fin_d, 2 * i)
                        for t in range(GT):
                            for c in range(2):
                                last = mm(banks[:, V_BANK, t * P:(t + 1) * P],
                                          ogate[:, c, t * P:(t + 1) * P], wo_s[:, c, :],
                                          start=c == 0, stop=c == 1)
                        last.then_inc(wo_mm, 1)
                    out_mm(3)
                    if early:
                        pe.wait_ge(gate_d, 2 * (i + 2))
                        mm(banks[:, A_BANK, :], wk_s[:], xTs[:, e, :],
                           start=True, stop=True).then_inc(k_mm, 1)
                        mm(banks[:, B_BANK, :], wq_s[:], xTs[:, e, :],
                           start=True, stop=True).then_inc(q_mm, 1)
                steps(pe, body)

            @block.scalar
            def _(act):
                af = nc.scalar.activation
                nc.scalar.preload_act_table_set("natural_log_exp_and_others")
                act.wait_ge(s_const, 1)
                act.wait_ge(g_tr, 1)
                af(gk1T[:], banks[:, AT_BANK, 0:P], ACT.Copy).then_inc(g_ev, 1)
                act.wait_ge(w_mm, 1)
                af(wgk_s[:], banks[:, OT_BANK, 0:P], ACT.Copy, scale=-1.0).then_inc(w_ev, 1)

                def body(i, p, er):
                    e = 1 - p
                    early, mid, late, end = (there(i, n) for n in (1, 0, -1, -2))
                    if late:
                        act.wait_ge(ot_mm, i * GT)
                        if end:
                            act.wait_ge(ms_mm, 2 * (i - 1))
                        for c in range(2):
                            af(square[:, c, :], banks[:, OT_BANK + c, :], ACT.Square
                               ).then_inc(sq_d, 1)
                        for c in range(2):
                            if end:
                                act.wait_ge(og_d, 2 * (i - 1))
                            af(o_s[:, c, :], banks[:, OT_BANK + c, :], ACT.Copy).then_inc(os_d, 1)
                    if end:
                        act.wait_ge(mom_d, i - 1)
                        af(lvar[:], moments[:, :, 1], ACT.Ln, bias=eps[:]).then_inc(lvar_d, 1)
                        act.wait_ge(lvar_d, i - 1)
                        if there(i, -3):
                            act.wait_ge(ln_d, i - 2)
                        af(rstd[:], lvar[:], ACT.Exp, scale=-0.5).then_inc(rstd_d, 1)
                    if early:
                        for c in range(2):
                            act.wait_ge(v_mm, 2 * (i + 1) + 1 + c)
                            if late:
                                act.wait_ge(ot_mm, i * GT)
                            af(val[:, e, 2 * c:2 * c + 2, :].rearrange("p t v -> p (t v)"),
                               banks[:, V_BANK + c, :], ACT.Copy).then_inc(val_d, 1)
                    if late:
                        for c in range(2):
                            act.wait_ge(ms_mm, 2 * i - 1 + c)
                            if end:
                                act.wait_ge(wlog_d, 2 * (i - 1))
                            af(lms[:, c, :], banks[:, A_BANK + c, :], ACT.Ln, bias=eps[:]
                               ).then_inc(lms_d, 1)
                    if early:
                        act.wait_ge(uc_d, i + 2)
                        af(espl[:], uclamp[:], ACT.Exp).then_inc(espl_d, 1)
                        act.wait_ge(espl_d, i + 2)
                        if mid:
                            act.wait_ge(ns_d, i + 1)
                        af(lspl[:], espl[:], ACT.Ln, bias=1.0).then_inc(lspl_d, 1)
                    if late:
                        for c in range(2):
                            act.wait_ge(wlog_d, 2 * i - 1 + c)
                            if end:
                                act.wait_ge(fin_d, 2 * (i - 1))
                            af(wexp[:, c, :], wlog[:, c, :], ACT.Exp, scale=-1.0).then_inc(wexp_d, 1)
                    if early:
                        act.wait_ge(ns_d, i + 2)
                        if mid:
                            act.wait_ge(kn_d, i + 1)
                            act.wait_ge(qg_d, i + 1)
                        for c, sign in enumerate((-1.0, 1.0)):
                            af(egd[:, c, :], negsig[:], ACT.Exp, scale=sign / GATE_NORM
                               ).then_inc(egd_d, 1)
                        for c in range(2):
                            act.wait_ge(gate_d, 2 * (i + 1) + 1 + c)
                            if mid:
                                act.wait_ge(glog_d, 2 * (i + 1))
                            af(gexp[:, c, :], gate[:, e, c, :], ACT.Exp, scale=-1.0
                               ).then_inc(gexp_d, 1)
                            act.wait_ge(gexp_d, 2 * (i + 1) + 1 + c)
                            if late:
                                act.wait_ge(wlog_d, 2 * i)
                            af(glog[:, e, c, :], gexp[:, c, :], ACT.Ln, bias=1.0).then_inc(glog_d, 1)
                    if end:
                        act.wait_ge(xt_mm, i - 1)
                        af(streamT[:, bass.ds((i - 2) * GROUP, GROUP)], banks[:, V_BANK + 1, :],
                           ACT.Copy).then_inc(xt_ev, 1)
                steps(act, body)

            @block.vector
            def _(dve):
                nc.vector.memset(qg[:], 0.0)
                nc.vector.memset(scores[:], 0.0).then_inc(s_dz, 1)
                dve.wait_ge(s_const, 1)
                dve.wait_ge(s_dz, 1)
                keep = causal[:].bitcast(I32)[:, None, :].to_broadcast([P, HA, P])

                def body(i, p, er):
                    e = 1 - p
                    early, mid, late, end = (there(i, n) for n in (1, 0, -1, -2))

                    def scores_ev(t):
                        if not mid:
                            return
                        dve.wait_ge(at_mm, i * GT + (t + 1))
                        if t > 1 or late:
                            dve.wait_ge(ot_mm, i * GT + (t - 1))
                        dve.sem_inc(carry_d, 1)
                        nc.vector.copy_predicated(
                            scores[:, t % 2], keep,
                            banks[:, AT_BANK, :].rearrange("p (h c) -> p h c", h=HA)
                        ).then_inc(sc_ev, 1)

                    def gate_ev(c):
                        if not early:
                            return
                        dve.wait_ge(g_mm, 2 * (i + 1) + 1 + c)
                        if late:
                            dve.wait_ge(og_d, 2 * i)
                            dve.wait_ge(gexp_d, 2 * i)
                        nc.vector.tensor_scalar(gate[:, e, c, :], banks[:, A_BANK + c, :],
                                                SILU_CLAMP, None, ALU.max).then_inc(gate_d, 1)

                    if mid:
                        dve.wait_ge(k_mm, i + 1)
                        dve.wait_ge(egd_d, 2 * (i + 1))
                        if end:
                            dve.wait_ge(at_mm, (i - 1) * GT)
                        nc.vector.tensor_tensor(kn[:, p, :], banks[:, A_BANK, :], egd[:, 1, :],
                                                ALU.mult).then_inc(kn_d, 1)
                        dve.wait_ge(q_mm, i + 1)
                        for h in range(HA):
                            rows = slice(h * DKA, (h + 1) * DKA)
                            last = nc.vector.scalar_tensor_tensor(
                                qg[rows, p, :, h, :],
                                banks[rows, B_BANK, :].rearrange("p (t c) -> p t c", t=GT),
                                float(DKA) ** -0.5,
                                egd[rows, 0, :].rearrange("p (t c) -> p t c", t=GT),
                                ALU.mult, ALU.mult)
                        last.then_inc(qg_d, 1)
                    if early:
                        dve.wait_ge(u_mm, i + 2)
                        if mid:
                            dve.wait_ge(espl_d, i + 1)
                        nc.vector.tensor_scalar(uclamp[:], banks[:, U_BANK, :], bgk_s[:], CLAMP,
                                                ALU.subtract, ALU.min).then_inc(uc_d, 1)
                    if end:
                        dve.wait_ge(rstd_d, i - 1)
                        if there(i, -3):
                            dve.wait_ge(xt_mm, i - 2)
                            dve.wait_ge(keep_d, i - 2)
                        for t in range(GT):
                            last = nc.vector.tensor_scalar(
                                xn[:, t, :], resid[:, t, :], moments[:, t, 0:1],
                                rstd[:, t:t + 1], ALU.subtract, ALU.mult)
                        last.then_inc(ln_d, 1)
                    if late:
                        for c in range(2):
                            dve.wait_ge(lms_d, 2 * i - 1 + c)
                            dve.wait_ge(glog_d, 2 * i - 1 + c)
                            if end:
                                dve.wait_ge(wexp_d, 2 * (i - 1))
                            nc.vector.scalar_tensor_tensor(
                                wlog[:, c, :], lms[:, c, :], 0.5, glog[:, e, c, :],
                                ALU.mult, ALU.add).then_inc(wlog_d, 1)
                    scores_ev(0)
                    if early:
                        dve.wait_ge(lspl_d, i + 2)
                        if mid:
                            dve.wait_ge(egd_d, 2 * (i + 1))
                        nc.vector.scalar_tensor_tensor(
                            negsig[:], banks[:, U_BANK, :], bgk_s[:], lspl[:],
                            ALU.subtract, ALU.max).then_inc(ns_d, 1)
                    gate_ev(0)
                    scores_ev(1)
                    if late:
                        for c in range(2):
                            dve.wait_ge(wexp_d, 2 * i - 1 + c)
                            dve.wait_ge(og_d, 2 * i - 1 + c)
                            if end:
                                dve.wait_ge(wo_mm, i - 1)
                            nc.vector.tensor_tensor(ogate[:, c, :], og[:, c, :], wexp[:, c, :],
                                                    ALU.mult).then_inc(fin_d, 1)
                    gate_ev(1)
                    scores_ev(2)
                    scores_ev(3)
                    if late:
                        dve.wait_ge(wo_mm, i)
                        if end:
                            dve.wait_ge(ln_d, i - 1)
                        nc.vector.tensor_tensor(
                            resid[:], banks[:, V_BANK, :].rearrange("p (t d) -> p t d", t=GT),
                            stream[:, bass.ds((i - 1) * GT, GT), 0:D], ALU.add).then_inc(y_d, 1)
                        dve.wait_ge(y_d, i)
                        for t in range(GT):
                            last = nc.vector.bn_stats(stats[:, t, :], resid[:, t, :])
                        last.then_inc(st_d, 1)
                        dve.wait_ge(st_d, i)
                        dve.sem_inc(carry_d, 1)
                        for t in range(GT):
                            last = nc.vector.bn_aggr(moments[:, t, :], stats[:, t, :])
                        last.then_inc(mom_d, 1)
                    if isinstance(i, int) and i == -1:
                        dve.wait_ge(s_wl, 16 * 3)
                        for c in range(2):
                            last = nc.vector.tensor_scalar(wo_s[:, c, :], wo_s[:, c, :], rms_s[:],
                                                           None, ALU.mult)
                        last.then_inc(s_wo, 1)
                steps(dve, body)


def cross_attention(nc, ctxT, ctx_s, mask_s, weights,
                    w1, b1T, w2, b2, sorted_x, stream, streamT, ident, eps, banks,
                    w1_s, w2_s, be_s, tile_expert, tile_row):
    from contextlib import ExitStack
    ctx = ExitStack()
    with ctx:
        def sb(name, shape, dt=F32):
            return ctx.enter_context(nc.sbuf_tensor("b_" + name, shape, dt))

        def sem(name):
            return ctx.enter_context(nc.semaphore("b_" + name))

        PAIRS = HX // 2
        DV = DX + 1
        SCALE = float(DX) ** -0.5
        wq_s, wk_s, wv_s, wo_s, sw_s, bq_s, bk_s, bv_s, bo_s, sb_s = weights
        bq_scaled = sb("bq_scaled", [P, 1])
        qT = sb("qT", [P, 2, GROUP])
        kT = sb("kT", [P, GROUP])
        kbd = sb("kbd", [P, 2, GB, HX, SEQ])
        vbd = sb("vbd", [P, 2, GB, PAIRS, 2, DV])
        masked = sb("masked", [P, GT, SEQ])
        limit = sb("limit", [P, 2, GT, SEQ])
        prob = sb("prob", [P, 4, HX, SEQ])
        top = sb("top", [P, 2, HX])
        probT = sb("probT", [P, 2, PAIRS, P])
        rsum = sb("rsum", [P, HX])
        attn = sb("attn", [P, 2, D])
        attnT = sb("attnT", [P, 2, P])
        resid = sb("resid", [P, 2, D])
        stats = sb("stats", [P, 6])
        moments = sb("moments", [P, 2, 2])
        lvar, rstd = sb("lvar", [P, 1]), sb("rstd", [P, 2])
        xn = sb("xn", [P, 2, D])
        xnT = sb("xnT", [P, 2, P])

        padding = sb("padding", [P, ROW])
        counts = sb("counts", [P, EXPERTS])
        STAGED = CHUNK // 2
        logits = sb("logits", [P, CHUNK, EXPERTS])
        ones = sb("ones", [P, P])
        before = sb("before", [P, P])
        number_i = sb("number_i", [P, EXPERTS], I32)
        token = sb("token", [P, TILES], I32)
        number = sb("number", [P, EXPERTS])
        late_number = sb("late_number", [P, EXPERTS])
        going = sb("going", [P, EXPERTS, CHUNK])
        eprob = sb("eprob", [P, CHUNK, EXPERTS])
        etop, esum, gate, choice, place = (sb(n, [P, CHUNK]) for n in (
            "etop", "esum", "gate", "choice", "place"))
        cand = sb("cand", [P, CHUNK, EXPERTS])
        onehot = sb("onehot", [P, EXPERTS, CHUNK])
        found = sb("found", [P, 2, EXPERTS, CHUNK])
        upto = sb("upto", [P, EXPERTS, CHUNK])
        rank = sb("rank", [P, EXPERTS, CHUNK])
        staged = sb("staged", [P, STAGED, ROW])
        slot_i = sb("slot_i", [P, CHUNK], I32)
        region_i = sb("region_i", [P, EXPERTS], I32)
        after_f = sb("after_f", [P, EXPERTS])
        after_i = sb("after_i", [P, EXPERTS], I32)
        sorted_i = sb("sorted_i", [P, XTILES], I32)
        sorted_n = sb("sorted_n", [P, XTILES])
        full_at = sb("full_at", [P, TILES])
        etiles = sb("etiles", [P, EXPERTS])
        etend = sb("etend", [P, EXPERTS])
        te = sb("te", [P, XTILES])
        first = sb("first", [P, XTILES])

        s_z, s_init, s_const = map(sem, ("zero", "init", "const"))
        s_zf, s_kz, s_kz1 = map(sem, ("zero_fill", "kbd0_zero", "kbd1_zero"))
        carry_d = sem("carry")
        s_c = [sem("ctx0"), sem("ctx1")]
        s_k = [sem("kbd0"), sem("kbd1")]
        (q_mm, k_mm, v_mm, s_mm, tp_mm, av_mm, at_mm, wo_mm, xt_mm, lg_mm) = map(sem, (
            "q_mm", "k_mm", "v_mm", "s_mm", "tp_mm", "av_mm", "at_mm", "wo_mm", "xt_mm", "lg_mm"))
        (exp_d, pt_ev, at_ev, lvar_d, rstd_d, xt_ev, lg_ev, k_ev, q_ev) = map(sem, (
            "exp", "pt_ev", "at_ev", "lvar", "rstd", "xt_ev", "lg_ev", "k_ev", "q_ev"))
        (min_d, max_d, sub_d, rs_d, an_d, y_d, st_d, mom_d, ln_d, v_ev) = map(sem, (
            "min", "max", "sub", "rsum", "attn", "resid", "stats", "moments", "ln", "v_ev"))
        (mk_d, lim_d, xb_d, keep_d) = map(sem, ("masked", "limit", "xb", "keep"))
        (rt_d, rt_exp, rt_mm, rt_ev, rt_slot, stage_d, s_rt) = map(sem, (
            "route_step", "route_exp", "route_mm", "route_ev", "route_slot", "staged",
            "route_const"))
        s_after, s_pad, s_list, s_we = map(sem, ("after", "padded", "list_step", "expert_weights"))
        s_scat = [sem("scatter%d" % n) for n in range(STAGED)]
        RCOLS = EXPERTS * CHUNK
        STEPS = 19
        SCATTERS = {4: (0,), 5: (1,), 6: (2,), 7: (3,), 0: (4, 5), 1: (6,), 2: (7,)}

        S_BANK, O_BANK, T0, T1, M_BANK, W_BANK = 0, 2, 4, 5, 6, 7
        XT_COL, AT_COL, WO_COL, LG_COL = 0, P, 0, P
        HALF = HX // 2
        BODY = 2 * GT

        with nc.Block() as block:
            def slots(eng, slot):
                for t in range(3 * BODY):
                    slot(t, t // BODY, t % BODY)
                with eng.Fori(3, TILES // BODY - 1) as it:
                    for k in range(BODY):
                        slot(it * BODY + k, it, k)
                for t in range(TILES - BODY, TILES + 2 * BODY + 3):
                    slot(t, t // BODY, t % BODY)

            def weighs(t, k, slot):
                return k == slot and (not isinstance(t, int) or BODY <= t < TILES + BODY)

            def places(t, k, slot):
                return k == slot and (not isinstance(t, int) or 2 * BODY <= t < TILES + 2 * BODY)

            def scatters(t, it, k):
                c = it - 2 if k >= BODY // 2 else it - 3
                there = not isinstance(t, int) or 0 <= c < TILES // CHUNK
                return [(n, c) for n in SCATTERS.get(k, ()) if there]

            def there(t, lag):
                return not isinstance(t, int) or 0 <= t - lag < TILES

            def past(t, n):
                return not isinstance(t, int) or t >= n

            def feeds(t, k, place, ahead=1):
                return k % GT == place and (not isinstance(t, int) or t // GT + ahead < GROUPS)

            def turns(t, k):
                return k % GT == 0 and (not isinstance(t, int) or GT <= t < TILES)

            def group(it, k):
                return 2 * it + k // GT

            @block.sync
            def _(sp):
                def spread_keys(g, e):
                    sp.wait_ge(k_ev, g + 1)
                    if past(g, 2):
                        sp.sem_inc(carry_d, 1)
                        sp.wait_ge(s_mm, (g - 1) * GT)
                    for h in range(HX):
                        rows = slice(h * DX, (h + 1) * DX)
                        sp.dma_start(kbd[rows, e, :, h, :],
                                     kT[rows, :].rearrange("p (s k) -> p s k", s=GB)
                                     ).then_inc(s_k[e], 16)

                def slot(t, it, k):
                    g, e = group(it, k), k // GT
                    if feeds(t, k, 0, 2):
                        sp.wait_ge(v_mm, g + 1)
                        sp.dma_start(ctx_s[:, e, :], ctxT[:, bass.ds((g + 2) * GROUP, GROUP)]
                                     ).then_inc(s_c[e], 16)
                    if feeds(t, k, 0):
                        spread_keys(g + 1, 1 - e)
                    expert = t - (TILES - BODY + 1) if isinstance(t, int) else -1
                    if 0 <= expert < EXPERTS:
                        if expert == 0:
                            sp.wait_ge(q_mm, GROUPS)
                        sp.wait_ge(s_mm, min(t, TILES))
                        sp.dma_start(w1_s[:, expert, :], w1[expert]).then_inc(s_we, 16)
                        sp.dma_start(w2_s[:, expert], w2[expert].rearrange(
                            "(c p) d -> p c d", p=P)).then_inc(s_we, 16)
                for dst, src in ((be_s[:, :, 0:D], b2[None, :, :].to_broadcast([P, EXPERTS, D])),
                                 (be_s[:, :, D:D + FC], b1T.rearrange("p (e c) -> p e c", c=FC))):
                    sp.dma_start(dst, src).then_inc(s_we, 16)
                sp.wait_ge(s_kz, 2)
                spread_keys(0, 0)
                sp.wait_ge(s_kz1, 1)
                sp.wait_ge(s_z, 2)
                sp.dma_start(sorted_x[EXPERTS * ETILES * P:, :].rearrange("(t p) d -> p t d", p=P),
                             padding[:, None, :].to_broadcast([P, EXPERTS, ROW])).then_inc(s_zf, 16)
                slots(sp, slot)
                sp.wait_ge(s_we, 16 * (2 + 2 * EXPERTS))
                sp.wait_ge(s_zf, 16)

            @block.gpsimd
            def _(pool):
                nc.gpsimd.memset(kbd[:, 0, GB // 2:], 0.0).then_inc(s_kz, 1)
                nc.gpsimd.iota(token[:], pattern=[[P, TILES]], base=0, channel_multiplier=1
                               ).then_inc(s_rt, 1)
                nc.gpsimd.iota(number_i[:], pattern=[[1, EXPERTS]], base=0, channel_multiplier=0
                               ).then_inc(s_rt, 1)
                nc.gpsimd.memset(ones[:], 1.0)
                nc.gpsimd.memset(counts[:], 0.0)
                nc.gpsimd.memset(before[:], 1.0)
                nc.gpsimd.memset(going[:], 1.0).then_inc(s_rt, 1)
                nc.gpsimd.iota(region_i[:], pattern=[[ETILES * P, EXPERTS]], base=0,
                               channel_multiplier=1)
                nc.gpsimd.iota(sorted_i[:], pattern=[[1, XTILES]], base=0, channel_multiplier=0)
                pool.wait_ge(s_rt, 3)
                nc.gpsimd.memset(going[:, :, 0], 0.0)
                nc.gpsimd.affine_select(out=before[:], in_=before[:], compare_op=ALU.is_ge,
                                        fill=0.0, base=-1, pattern=[[1, P]],
                                        channel_multiplier=-1).then_inc(s_rt, 1)
                nc.gpsimd.memset(kbd[:, 1], 0.0).then_inc(s_kz1, 1)
                nc.gpsimd.memset(padding[:, 0:D + 1], 0.0).then_inc(s_z, 1)
                nc.gpsimd.memset(padding[:, D + 1:ROW], float(TOKENS)).then_inc(s_z, 1)

                def add_bias(g):
                    nc.gpsimd.tensor_tensor(stream[:, bass.ds(g * GT, GT), 0:D],
                                            stream[:, bass.ds(g * GT, GT), 0:D],
                                            bo_s[:, None, :].to_broadcast([P, GT, D]), ALU.add
                                            ).then_inc(xb_d, 1)

                def fill_last_tiles():
                    pool.wait_ge(s_after, 1)
                    for e in range(EXPERTS):
                        nc.gpsimd.indirect_dma_start(
                            out=sorted_x[:, :],
                            out_offset=bass.IndirectOffsetOnAxis(ap=after_i[:, e:e + 1], axis=0),
                            in_=padding[:], in_offset=None).then_inc(s_pad, 16)

                def slot(t, it, k):
                    if there(t, 6):
                        pool.wait_ge(ln_d, t - 5)
                        nc.gpsimd.tensor_copy(stream[:, bass.ds(t - 6, 1), 0:D],
                                              xn[:, k % 2, None, :]).then_inc(keep_d, 1)
                    if there(t, 0):
                        pool.wait_ge(max_d, t + 1)
                        nc.gpsimd.tensor_tensor(prob[:, k % 4], prob[:, k % 4],
                                                top[:, k % 2, :, None].to_broadcast([P, HX, SEQ]),
                                                ALU.subtract).then_inc(sub_d, 1)
                    if feeds(t, k, 1):
                        add_bias(group(it, k) + 1)
                    if isinstance(t, int) and t == TILES + BODY + BODY // 2:
                        fill_last_tiles()
                    for n, c in scatters(t, it, k):
                        pool.wait_ge(stage_d, c * CHUNK + (n + 1))
                        pool.sem_inc(carry_d, 1)
                        nc.gpsimd.indirect_dma_start(
                            out=sorted_x[:, :],
                            out_offset=bass.IndirectOffsetOnAxis(ap=slot_i[:, n:n + 1], axis=0),
                            in_=staged[:, n % STAGED, :], in_offset=None
                        ).then_inc(s_scat[n % STAGED], 16)
                add_bias(0)
                slots(pool, slot)
                for n in range(STAGED):
                    pool.wait_ge(s_scat[n], 16 * (TILES // STAGED))
                pool.wait_ge(s_pad, 16 * EXPERTS)

            @block.tensor
            def _(pe):
                pe.wait_ge(s_const, 1)
                mm = nc.tensor.matmul

                def project_qk(g, e, turn):
                    if past(turn, 1):
                        pe.wait_ge(s_c[e], 16 * turn)
                    mm(banks[:, T1, :], wk_s[:], ctx_s[:, e, :], start=True, stop=True
                       ).then_inc(k_mm, 1)
                    mm(banks[:, T0, :], wq_s[:], streamT[:, bass.ds(g * GROUP, GROUP)],
                       start=True, stop=True).then_inc(q_mm, 1)

                def project_v(e, bank):
                    for t in range(GT):
                        last = mm(banks[:, bank, t * D:(t + 1) * D],
                                  ctx_s[:, e, t * P:(t + 1) * P], wv_s[:], start=True, stop=True)
                    last.then_inc(v_mm, 1)

                def scores(t, it, k):
                    if k % GT == 0:
                        pe.wait_ge(q_ev, group(it, k) + 1)
                        pe.wait_ge(s_k[k // GT], 16 * HX * (it + 1))
                    if past(t, 1):
                        pe.wait_ge(min_d, t)
                    for half in range(2):
                        for b in range(2):
                            seq = 2 * (k % GT) + b
                            last = mm(banks[SEQ * b:SEQ * b + SEQ, S_BANK + half, :],
                                      qT[:, k // GT, seq * SEQ:(seq + 1) * SEQ],
                                      kbd[:, k // GT, seq, half * HALF:(half + 1) * HALF
                                          ].rearrange("p h k -> p (h k)"),
                                      start=True, stop=True)
                    last.then_inc(s_mm, 1)

                def slot(t, it, k):
                    if there(t, 0):
                        scores(t, it, k)
                    if there(t, 3):
                        pe.wait_ge(pt_ev, 2 * (t - 2))
                    if feeds(t, k, 0):
                        project_qk(group(it, k) + 1, 1 - k // GT, it + k // GT)
                    if there(t, 5):
                        pe.wait_ge(at_ev, t - 4)
                        if past(t, 7):
                            pe.wait_ge(lg_ev, t - 6)
                        elif past(t, 6):
                            pe.wait_ge(y_d, t - 5)
                        mm(banks[:, W_BANK, WO_COL:WO_COL + D], attnT[:, (k - 5) % 2, :], wo_s[:],
                           start=True, stop=True).then_inc(wo_mm, 1)
                    if there(t, 6):
                        pe.wait_ge(ln_d, t - 5)
                        if there(t, 5):
                            pe.wait_ge(at_ev, t - 4)
                        nc.tensor.transpose(banks[:, M_BANK, XT_COL:XT_COL + P],
                                            xn[:, k % 2, :], ident[:]).then_inc(xt_mm, 1)
                    for j in range(PAIRS):
                        if there(t, 2):
                            if j == 0:
                                pe.wait_ge(exp_d, t - 1)
                                if feeds(t, k, 0):
                                    pe.wait_ge(q_ev, group(it, k) + 2)
                                    pe.wait_ge(k_ev, group(it, k) + 2)
                            last = nc.tensor.transpose(
                                banks[:, T0 + j // 4, (j % 4) * P:(j % 4 + 1) * P],
                                prob[:, (k - 2) % 4, 2 * j:2 * j + 2, :].rearrange(
                                    "p h k -> p (h k)"), ident[:])
                            if j % 4 == 3:
                                last.then_inc(tp_mm, 1)
                        if there(t, 3):
                            if j == 0:
                                pe.wait_ge(v_ev, group(it, k - 3) + 1)
                                if past(t, 5):
                                    pe.wait_ge(an_d, t - 4)
                                if turns(t, k):
                                    pe.wait_ge(v_ev, group(it, k) + 1)
                                if places(t, k, 1):
                                    pe.wait_ge(rt_ev, it - 1)
                            for b in range(2):
                                col = j * 2 * DV
                                last = mm(banks[SEQ * b:SEQ * b + SEQ, O_BANK + (k - 3) % 2,
                                                col:col + 2 * DV],
                                          probT[:, (k - 3) % 2, j, SEQ * b:SEQ * b + SEQ],
                                          vbd[:, (k - 3) // GT % 2, 2 * ((k - 3) % GT) + b, j
                                              ].rearrange("p h d -> p (h d)"),
                                          start=True, stop=True)
                            if j == PAIRS - 1:
                                last.then_inc(av_mm, 1)
                        if j == PAIRS // 2 and there(t, 4):
                            pe.wait_ge(an_d, t - 3)
                            if there(t, 6):
                                pe.wait_ge(xt_ev, t - 5)
                            nc.tensor.transpose(banks[:, M_BANK, AT_COL:AT_COL + P],
                                                attn[:, k % 2, :], ident[:]).then_inc(at_mm, 1)
                    if there(t, 6):
                        pe.wait_ge(xt_ev, t - 5)
                        if there(t, 5):
                            pe.wait_ge(y_d, t - 4)
                        mm(banks[:, W_BANK, LG_COL:LG_COL + EXPERTS], xnT[:, k % 2, :], sw_s[:],
                           start=True, stop=True).then_inc(lg_mm, 1)
                    if places(t, k, 0):
                        pe.wait_ge(rt_d, (it - 2) * STEPS + 11)
                        if there(t, 4):
                            pe.wait_ge(an_d, t - 3)
                        for n, weights in enumerate((ones, before)):
                            last = mm(banks[:, O_BANK + k % 2, n * RCOLS:(n + 1) * RCOLS],
                                      weights[:], onehot[:].rearrange("p e t -> p (e t)"),
                                      start=True, stop=True)
                        last.then_inc(rt_mm, 1)
                    if feeds(t, k, 3):
                        if there(t, 4):
                            pe.wait_ge(an_d, t - 3)
                        project_v(1 - k // GT, O_BANK + k % 2)

                project_qk(0, 0, 0)
                project_v(0, O_BANK)
                pe.wait_ge(v_ev, 1)
                pe.wait_ge(s_rt, 4)
                slots(pe, slot)

            @block.scalar
            def _(act):
                af = nc.scalar.activation
                nc.scalar.preload_act_table_set("natural_log_exp_and_others")
                act.wait_ge(s_const, 1)

                def projections_ev(g, e, turn):
                    act.wait_ge(k_mm, g + 1)
                    if past(g, 1):
                        act.wait_ge(s_k[1 - e], 16 * HX * turn)
                    af(kT[:], banks[:, T1, :], ACT.Identity, bias=bk_s[:]).then_inc(k_ev, 1)
                    act.wait_ge(q_mm, g + 1)
                    if past(g, 2):
                        act.wait_ge(s_mm, (g - 1) * GT)
                    af(qT[:, e, :], banks[:, T0, :], ACT.Identity, bias=bq_scaled[:], scale=SCALE
                       ).then_inc(q_ev, 1)

                def slot(t, it, k):
                    if feeds(t, k, 0):
                        projections_ev(group(it, k) + 1, 1 - k // GT, it + 1)
                    if there(t, 6):
                        act.wait_ge(xt_mm, t - 5)
                        if past(t, 8):
                            act.wait_ge(lg_mm, t - 7)
                        af(xnT[:, k % 2, :], banks[:, M_BANK, XT_COL:XT_COL + P], ACT.Copy
                           ).then_inc(xt_ev, 1)
                    for c in range(2):
                        if there(t, 2):
                            if c == 0 and past(t, 4):
                                act.wait_ge(av_mm, t - 3)
                            act.wait_ge(tp_mm, 2 * (t - 2) + 1 + c)
                            af(probT[:, k % 2, 4 * c:4 * c + 4, :].rearrange("p j q -> p (j q)"),
                               banks[:, T0 + c, :], ACT.Copy).then_inc(pt_ev, 1)
                        if c == 0 and there(t, 4):
                            act.wait_ge(at_mm, t - 3)
                            if past(t, 6):
                                act.wait_ge(wo_mm, t - 5)
                            af(attnT[:, k % 2, :], banks[:, M_BANK, AT_COL:AT_COL + P], ACT.Copy
                               ).then_inc(at_ev, 1)
                        if c == 0 and there(t, 1):
                            act.wait_ge(sub_d, t)
                            af(prob[:, (k - 1) % 4], prob[:, (k - 1) % 4], ACT.Exp
                               ).then_inc(exp_d, 1)
                    if there(t, 5):
                        act.wait_ge(mom_d, t - 4)
                        af(lvar[:], moments[:, (k - 5) % 2, 1:2], ACT.Ln, bias=eps[:]
                           ).then_inc(lvar_d, 1)
                        act.wait_ge(lvar_d, t - 4)
                        if past(t, 7):
                            act.wait_ge(ln_d, t - 6)
                        af(rstd[:, (k - 5) % 2:(k - 5) % 2 + 1], lvar[:], ACT.Exp, scale=-0.5
                           ).then_inc(rstd_d, 1)
                    if there(t, 6):
                        act.wait_ge(lg_mm, t - 5)
                        if (k - 6) % CHUNK == 0 and past(t, 6 + CHUNK):
                            act.wait_ge(rt_d, (it - 1) * STEPS + 1)
                        af(logits[:, (k - 6) % CHUNK, :],
                           banks[:, W_BANK, LG_COL:LG_COL + EXPERTS], ACT.Copy
                           ).then_inc(lg_ev, 1)
                    for n, c in scatters(t, it, k):
                        act.wait_ge(rt_slot, c + 1)
                        act.wait_ge(keep_d, (c + 1) * CHUNK)
                        if n >= STAGED:
                            act.wait_ge(s_scat[n % STAGED], 16 * (c * 2 + 1))
                        af(staged[:, n % STAGED, None, :],
                           stream[:, bass.ds(c * CHUNK + n, 1), :], ACT.Copy).then_inc(stage_d, 1)
                    if weighs(t, k, 6):
                        act.wait_ge(rt_d, (it - 1) * STEPS + 3)
                        af(eprob[:], eprob[:], ACT.Exp).then_inc(rt_exp, 1)
                projections_ev(0, 0, 0)
                slots(act, slot)

            @block.vector
            def _(dve):
                nc.vector.tensor_scalar(bq_scaled[:], bq_s[:], SCALE, None, ALU.mult
                                        ).then_inc(s_const, 1)
                nc.vector.memset(kbd[:, 0, 0:GB // 2], 0.0).then_inc(s_kz, 1)
                nc.vector.memset(vbd[:], 0.0).then_inc(s_init, 1)
                dve.wait_ge(s_init, 1)
                for par in range(2):
                    half = slice(SEQ * par, SEQ * par + SEQ)
                    nc.vector.memset(vbd[half, :, :, :, par, DX], 1.0)
                def limits(g, e):
                    if past(g, 1):
                        dve.wait_ge(lim_d, g)
                    if past(g, 2):
                        dve.wait_ge(min_d, (g - 1) * GT)
                    nc.vector.tensor_copy(masked[:], mask_s[:, bass.ds(g * GT, GT), :]
                                          ).then_inc(mk_d, 1)
                    dve.wait_ge(mk_d, 2 * g + 1)
                    nc.vector.tensor_scalar(masked[:], masked[:], -2 * LARGE, LARGE,
                                            ALU.mult, ALU.add).then_inc(mk_d, 1)
                    dve.wait_ge(mk_d, 2 * g + 2)
                    nc.vector.tensor_scalar(limit[:, e], masked[:], NEG, None, ALU.max
                                            ).then_inc(lim_d, 1)

                def values_ev(g, e, bank):
                    dve.wait_ge(v_mm, g + 1)
                    if past(g, 2):
                        dve.wait_ge(av_mm, (g - 1) * GT)
                    for b in range(2):
                        for par in range(2):
                            rows = slice(SEQ * b, SEQ * b + SEQ)
                            half = slice(SEQ * par, SEQ * par + SEQ)
                            last = nc.vector.tensor_tensor(
                                vbd[half, e, b::2, :, par, 0:DX],
                                banks[rows, bank, :].rearrange(
                                    "p (t j h d) -> p t j h d", t=GT, j=PAIRS, h=2)[:, :, :, par, :],
                                bv_s[rows, :].rearrange("p (j h d) -> p j h d", j=PAIRS, h=2)[
                                    :, None, :, par, :].to_broadcast([SEQ, GT, PAIRS, DX]), ALU.add)
                    last.then_inc(v_ev, 1)

                def on_experts(row):
                    return row[:, :, None].to_broadcast([P, CHUNK, EXPERTS])

                def step(c, n):
                    dve.wait_ge(rt_d, c * STEPS + n)

                def weigh(c, place_in_slot):
                    if place_in_slot == 1:
                        dve.wait_ge(lg_ev, (c + 1) * CHUNK)
                        nc.vector.tensor_tensor(
                            eprob[:], logits[:], sb_s[:, None, :].to_broadcast(
                                [P, CHUNK, EXPERTS]), ALU.add).then_inc(rt_d, 1)
                    if place_in_slot == 2:
                        step(c, 1)
                        nc.vector.reduce_max(etop[:], eprob[:], AX.X).then_inc(rt_d, 1)
                    if place_in_slot == 3:
                        step(c, 2)
                        nc.vector.tensor_tensor(eprob[:], eprob[:], on_experts(etop),
                                                ALU.subtract).then_inc(rt_d, 1)

                def softmax(c, place_in_slot):
                    if place_in_slot == 0:
                        dve.wait_ge(rt_exp, c + 1)
                        nc.vector.reduce_sum(esum[:], eprob[:], AX.X).then_inc(rt_d, 1)
                    if place_in_slot == 1:
                        step(c, 4)
                        nc.vector.reciprocal(esum[:], esum[:]).then_inc(rt_d, 1)
                    if place_in_slot == 2:
                        step(c, 5)
                        nc.vector.tensor_tensor(eprob[:], eprob[:], on_experts(esum), ALU.mult
                                                ).then_inc(rt_d, 1)
                    if place_in_slot == 3:
                        step(c, 6)
                        nc.vector.reduce_max(gate[:], eprob[:], AX.X).then_inc(rt_d, 1)
                    if place_in_slot == 4:
                        step(c, 7)
                        nc.vector.tensor_tensor(cand[:], eprob[:], on_experts(gate), ALU.is_equal
                                                ).then_inc(rt_d, 1)
                        nc.vector.tensor_copy(stream[:, bass.ds(c * CHUNK, CHUNK), D], gate[:])
                    if place_in_slot == 5:
                        step(c, 8)
                        nc.vector.scalar_tensor_tensor(
                            cand[:], cand[:], -float(EXPERTS),
                            late_number[:, None, :].to_broadcast([P, CHUNK, EXPERTS]),
                            ALU.mult, ALU.add).then_inc(rt_d, 1)

                def choose(c, place_in_slot):
                    if place_in_slot == 0:
                        step(c, 9)
                        nc.vector.tensor_reduce(choice[:], cand[:], AX.X, ALU.min
                                                ).then_inc(rt_d, 1)
                    if place_in_slot == 1:
                        step(c, 10)
                        nc.vector.tensor_tensor(
                            onehot[:], number[:, :, None].to_broadcast([P, EXPERTS, CHUNK]),
                            choice[:, None, :].to_broadcast([P, EXPERTS, CHUNK]), ALU.is_equal
                            ).then_inc(rt_d, 1)

                def rank_rows(c, place_in_slot, bank):
                    if place_in_slot == 0:
                        dve.wait_ge(rt_mm, c + 1)
                        nc.vector.tensor_copy(found[:].rearrange("p n e t -> p (n e t)"),
                                              banks[:, bank, 0:2 * RCOLS]).then_inc(rt_ev, 1)
                    if place_in_slot == 1:
                        dve.wait_ge(rt_ev, c + 1)
                        nc.vector.tensor_tensor_scan(
                            upto[:].rearrange("p e t -> p (e t)"),
                            going[:].rearrange("p e t -> p (e t)"),
                            found[:, 0].rearrange("p e t -> p (e t)"), 0.0, ALU.mult, ALU.add
                            ).then_inc(rt_d, 1)
                    if place_in_slot == 2:
                        step(c, 12)
                        nc.vector.tensor_tensor(rank[:], upto[:], found[:, 0], ALU.subtract
                                                ).then_inc(rt_d, 1)
                    if place_in_slot == 3:
                        step(c, 13)
                        nc.vector.tensor_tensor(rank[:], rank[:], found[:, 1], ALU.add
                                                ).then_inc(rt_d, 1)
                    if place_in_slot == 4:
                        step(c, 14)
                        nc.vector.tensor_tensor(rank[:], rank[:], counts[:, :, None].to_broadcast(
                            [P, EXPERTS, CHUNK]), ALU.add).then_inc(rt_d, 1)
                    if place_in_slot == 5:
                        step(c, 15)
                        nc.vector.tensor_tensor(rank[:], rank[:], onehot[:], ALU.mult
                                                ).then_inc(rt_d, 1)

                def place_rows(c, place_in_slot):
                    if place_in_slot == 0:
                        step(c, 16)
                        if past(c, 1):
                            dve.wait_ge(rt_slot, c)
                        nc.vector.reduce_sum(place[:], rank[:].rearrange("p e t -> p t e"), AX.X
                                             ).then_inc(rt_d, 1)
                    if place_in_slot == 1:
                        step(c, 17)
                        nc.vector.scalar_tensor_tensor(
                            place[:], choice[:], float(ETILES * P), place[:], ALU.mult, ALU.add
                            ).then_inc(rt_d, 1)
                    if place_in_slot == 2:
                        step(c, 18)
                        nc.vector.tensor_tensor(counts[:], counts[:], upto[:, :, CHUNK - 1], ALU.add
                                                ).then_inc(rt_d, 1)

                def address_rows(c, place_in_slot):
                    if place_in_slot == 5:
                        step(c, 19)
                        if isinstance(c, int) and c == TILES // CHUNK - 1:
                            nc.vector.tensor_copy(after_f[:], region_i[:]).then_inc(s_list, 1)
                            dve.wait_ge(s_list, 1)
                            nc.vector.tensor_tensor(after_f[:], after_f[:], counts[:], ALU.add
                                                    ).then_inc(s_list, 1)
                            dve.wait_ge(s_list, 2)
                            nc.vector.tensor_copy(after_i[:], after_f[:]).then_inc(s_after, 1)
                        if past(c, 1):
                            for n in range(STAGED):
                                dve.wait_ge(s_scat[n], 16 * (CHUNK // STAGED) * c)
                        nc.vector.tensor_copy(slot_i[:], place[:]).then_inc(rt_slot, 1)

                def route(t, it, k, place_in_slot):
                    if weighs(t, k, 6):
                        weigh(it - 1, place_in_slot)
                    if weighs(t, k, 7):
                        softmax(it - 1, place_in_slot)
                    if places(t, k, 0):
                        choose(it - 2, place_in_slot)
                    if places(t, k, 1):
                        rank_rows(it - 2, place_in_slot, O_BANK + (k - 1) % 2)
                    if places(t, k, 2):
                        place_rows(it - 2, place_in_slot)
                    if places(t, k, 3):
                        address_rows(it - 2, place_in_slot)

                def slot(t, it, k):
                    if there(t, 4):
                        dve.wait_ge(av_mm, t - 3)
                        o = banks[:, O_BANK + k % 2, 0:HX * DV].rearrange("p (h d) -> p h d", h=HX)
                        nc.vector.reciprocal(rsum[:], o[:, :, DX]).then_inc(rs_d, 1)
                    route(t, it, k, 0)
                    if there(t, 6):
                        dve.wait_ge(rstd_d, t - 5)
                        if past(t, 8):
                            dve.wait_ge(xt_mm, t - 7)
                            dve.wait_ge(keep_d, t - 7)
                        nc.vector.tensor_scalar(xn[:, k % 2, :], resid[:, k % 2, :],
                                                moments[:, k % 2, 0:1], rstd[:, k % 2:k % 2 + 1],
                                                ALU.subtract, ALU.mult).then_inc(ln_d, 1)
                    if there(t, 4):
                        dve.wait_ge(rs_d, t - 3)
                        if past(t, 6):
                            dve.wait_ge(at_mm, t - 5)
                        nc.vector.tensor_tensor(
                            attn[:, k % 2, :].rearrange("p (h d) -> p h d", h=HX), o[:, :, 0:DX],
                            rsum[:, :, None].to_broadcast([P, HX, DX]), ALU.mult
                        ).then_inc(an_d, 1)
                    p_all = prob[:, k % 4]
                    if there(t, 0):
                        dve.wait_ge(s_mm, t + 1)
                        if k % GT == 0:
                            dve.wait_ge(lim_d, group(it, k) + 1)
                        if past(t, 4):
                            dve.wait_ge(tp_mm, 2 * (t - 3))
                        nc.vector.tensor_tensor(
                            p_all, banks[:, S_BANK:S_BANK + 2, :].rearrange(
                                "p r (h k) -> p (r h) k", k=SEQ),
                            limit[:, k // GT, k % GT, None, :].to_broadcast([P, HX, SEQ]),
                            ALU.min).then_inc(min_d, 1)
                    route(t, it, k, 1)
                    if turns(t, k):
                        values_ev(group(it, k), k // GT, O_BANK + (k - 1) % 2)
                    if there(t, 5):
                        dve.wait_ge(wo_mm, t - 4)
                        if (k - 5) % GT == 0:
                            dve.wait_ge(xb_d, group(it, k - 5) + 1)
                        if past(t, 7):
                            dve.wait_ge(ln_d, t - 6)
                        nc.vector.tensor_tensor(resid[:, None, (k - 5) % 2, :],
                                                banks[:, None, W_BANK, WO_COL:WO_COL + D],
                                                stream[:, bass.ds(t - 5, 1), 0:D], ALU.add
                                                ).then_inc(y_d, 1)
                    route(t, it, k, 2)
                    if there(t, 5):
                        dve.wait_ge(y_d, t - 4)
                        nc.vector.bn_stats(stats[:], resid[:, (k - 5) % 2, :]).then_inc(st_d, 1)
                    route(t, it, k, 3)
                    if feeds(t, k, 1):
                        limits(group(it, k) + 1, 1 - k // GT)
                    if there(t, 5):
                        dve.wait_ge(st_d, t - 4)
                        dve.sem_inc(carry_d, 1)
                        nc.vector.bn_aggr(moments[:, (k - 5) % 2, :], stats[:]).then_inc(mom_d, 1)
                    route(t, it, k, 4)
                    if there(t, 0):
                        dve.wait_ge(min_d, t + 1)
                        if past(t, 2):
                            dve.wait_ge(sub_d, t - 1)
                        nc.vector.reduce_max(top[:, k % 2, :], p_all, AX.X).then_inc(max_d, 1)
                    route(t, it, k, 5)
                dve.wait_ge(s_rt, 4)
                nc.vector.tensor_copy(stream[:, :, D + 1], token[:])
                nc.vector.tensor_copy(number[:], number_i[:]).then_inc(s_init, 1)
                dve.wait_ge(s_init, 2)
                nc.vector.tensor_scalar(late_number[:], number[:], float(EXPERTS), None, ALU.add
                                        ).then_inc(s_init, 1)
                dve.wait_ge(s_init, 3)
                limits(0, 0)
                values_ev(0, 0, O_BANK)
                slots(dve, slot)

                tt, ts = nc.vector.tensor_tensor, nc.vector.tensor_scalar

                def done(instruction, n):
                    instruction.then_inc(s_list, 1)
                    dve.wait_ge(s_list, n)

                dve.wait_ge(tp_mm, 2 * TILES)
                opens = prob[:, 0, 0:EXPERTS, :]
                passed, skipped = (prob[:, n].rearrange("p h k -> p (h k)")[
                    :, 0:XTILES * EXPERTS].rearrange("p (i e) -> p i e", e=EXPERTS) for n in (1, 2))
                done(nc.vector.tensor_copy(sorted_n[:], sorted_i[:]), 3)
                done(ts(full_at[:], sorted_n[:, 0:TILES], float(P), None, ALU.mult), 4)
                done(tt(opens, counts[:, :, None].to_broadcast([P, EXPERTS, TILES]),
                        full_at[:, None, :].to_broadcast([P, EXPERTS, TILES]), ALU.is_gt), 5)
                done(nc.vector.reduce_sum(etiles[:], opens, AX.X), 6)
                done(nc.vector.tensor_tensor_scan(etend[:], ones[:, 0:EXPERTS], etiles[:], 0.0,
                                                  ALU.mult, ALU.add), 7)
                done(tt(passed, sorted_n[:, :, None].to_broadcast([P, XTILES, EXPERTS]),
                        etend[:, None, :].to_broadcast([P, XTILES, EXPERTS]), ALU.is_ge), 8)
                done(nc.vector.reduce_sum(te[:], passed, AX.X), 9)
                ts(tile_expert[:], te[:], float(EXPERTS - 1), None, ALU.min)
                done(tt(skipped, passed, etiles[:, None, :].to_broadcast(
                    [P, XTILES, EXPERTS]), ALU.mult), 10)
                done(nc.vector.reduce_sum(first[:], skipped, AX.X), 11)
                done(tt(first[:], sorted_n[:], first[:], ALU.subtract), 12)
                nc.vector.scalar_tensor_tensor(tile_row[:], te[:], float(ETILES), first[:],
                                               ALU.mult, ALU.add)


def expert_tiles(nc, w1_s, w2_s, be_s, tile_expert, tile_row, sorted_x, out, ident, eps, banks):
    from contextlib import ExitStack
    ctx = ExitStack()
    with ctx:
        def sb(name, shape, dt=F32):
            return ctx.enter_context(nc.sbuf_tensor("c_" + name, shape, dt))

        def sem(name):
            return ctx.enter_context(nc.semaphore("c_" + name))

        LOADS = 12
        BODY = 12
        SCATTERS = 6
        rows = sb("rows", [P, LOADS, ROW])
        xT = sb("xT", [P, 2, P])
        w1_now = sb("w1_now", [P, 4, FF])
        be_now = sb("be_now", [P, 4, D + FC])
        hT = sb("hT", [P, 2, FC, P])
        y = sb("y", [P, D])
        resid = sb("resid", [P, 2, D])
        stats = sb("stats", [P, 6])
        moments = sb("moments", [P, 2, 2])
        power = sb("power", [P, 1])
        veps = sb("veps", [P, 1])
        rstd = sb("rstd", [P, 2])
        token = sb("token", [P, SCATTERS], I32)
        final = sb("final", [P, SCATTERS, D])

        s_load = [sem("load%d" % n) for n in range(LOADS)]
        s_out = [sem("out%d" % n) for n in range(SCATTERS)]
        (xt_mm, h_mm, y_mm, xt_ev, w_now, h_ev, y_ev, res_d, st_d, mom_d, rstd_d, fin_d, ve_d,
         s_pow) = map(sem, ("xt_mm", "h_mm", "y_mm", "xt_ev", "w_now", "h_ev", "y_ev", "resid",
                            "stats", "moments", "rstd", "final", "veps", "power"))
        carry_d = sem("carry")
        XT0, H0, Y0 = 0, 2, 6
        HALF = FC // 2

        with nc.Block() as block:
            def slots(eng, slot):
                for t in range(-2, BODY):
                    slot(t, 0, t)
                with eng.Fori(1, (XTILES - 2) // BODY) as it:
                    for k in range(BODY):
                        slot(it * BODY + k, it, k)
                for t in range((XTILES - 2) // BODY * BODY, XTILES + 3):
                    slot(t, t // BODY, t % BODY)

            def there(t, lag):
                return not isinstance(t, int) or 0 <= t - lag < XTILES

            def past(t, first):
                return not isinstance(t, int) or t >= first

            @block.sync
            def _(sp):
                def load(t, it, k):
                    if past(t, LOADS):
                        sp.wait_ge(s_out[(k - LOADS) % SCATTERS], 16 * scatters(it, k, LOADS))
                    row = nc.sync.value_load(tile_row[0:1, bass.ds(t, 1)], min_val=0,
                                             max_val=EXPERTS * (ETILES + 1) - 1)
                    sp.dma_start(rows[:, k % LOADS, :], sorted_x[bass.ds(row * P, P), :]
                                 ).then_inc(s_load[k % LOADS], 16)

                def scatters(it, k, lag):
                    return it * (BODY // SCATTERS) + (k - lag) // SCATTERS + 1

                for t in range(BODY):
                    load(t, 0, t)
                with sp.Fori(1, XTILES // BODY) as it:
                    for k in range(BODY):
                        load(it * BODY + k, it, k)
                for t in range(XTILES // BODY * BODY, XTILES):
                    load(t, t // BODY, t % BODY)

            @block.gpsimd
            def _(pool):
                nc.gpsimd.memset(power[:], -0.5).then_inc(s_pow, 1)
                pool.wait_ge(s_pow, 1)

                def slot(t, it, k):
                    if there(t, 2):
                        pool.wait_ge(mom_d, t - 1)
                        nc.gpsimd.tensor_tensor(veps[:], moments[:, k % 2, 1:2], eps[:], ALU.add
                                                ).then_inc(ve_d, 1)
                        pool.wait_ge(ve_d, t - 1)
                        if past(t, 4):
                            pool.wait_ge(fin_d, t - 3)
                        nc.gpsimd.tensor_tensor(rstd[:, k % 2:k % 2 + 1], veps[:], power[:], ALU.pow
                                                ).then_inc(rstd_d, 1)
                    if there(t, 3):
                        pool.wait_ge(fin_d, t - 2)
                        pool.sem_inc(carry_d, 1)
                        nc.gpsimd.indirect_dma_start(
                            out=out[:, :],
                            out_offset=bass.IndirectOffsetOnAxis(
                                ap=token[:, (k - 3) % SCATTERS:(k - 3) % SCATTERS + 1], axis=0),
                            in_=final[:, (k - 3) % SCATTERS, :], in_offset=None,
                            bounds_check=TOKENS - 1, oob_is_err=False
                        ).then_inc(s_out[(k - 3) % SCATTERS], 16)
                slots(pool, slot)
                for n in range(SCATTERS):
                    pool.wait_ge(s_out[n], 16 * ((XTILES - 1 - n) // SCATTERS + 1))

            @block.tensor
            def _(pe):
                def slot(t, it, k):
                    if there(t, 0):
                        pe.wait_ge(xt_ev, t + 1)
                        pe.wait_ge(w_now, t + 1)
                        if past(t, 2):
                            pe.wait_ge(h_ev, (t - 1) * FC)
                        for c in range(FC):
                            bank = H0 + 2 * (k % 2) + c // HALF
                            last = nc.tensor.matmul(banks[:, bank, c % HALF * P:(c % HALF + 1) * P],
                                                    w1_now[:, k % 4, c * P:(c + 1) * P],
                                                    xT[:, k % 2, :], start=True, stop=True)
                            if c % HALF == HALF - 1:
                                last.then_inc(h_mm, 1)
                    if there(t, 1):
                        e = nc.tensor.value_load(tile_expert[0:1, bass.ds(t - 1, 1)],
                                                 min_val=0, max_val=EXPERTS - 1)
                    if there(t, -1):
                        pe.wait_ge(s_load[(k + 1) % LOADS],
                                   16 * (it * (BODY // LOADS) + (k + 1) // LOADS + 1))
                        if past(t, 1):
                            pe.wait_ge(xt_ev, t)
                        nc.tensor.transpose(banks[:, XT0 + (k + 1) % 2, 0:P],
                                            rows[:, (k + 1) % LOADS, 0:D], ident[:]
                                            ).then_inc(xt_mm, 1)
                    if there(t, 1):
                        if past(t, 3):
                            pe.wait_ge(y_ev, t - 2)
                        for c in range(FC):
                            pe.wait_ge(h_ev, (t - 1) * FC + (c + 1))
                            last = nc.tensor.matmul(banks[:, Y0 + (k - 1) % 2, 0:D],
                                                    hT[:, (k - 1) % 2, c, :],
                                                    w2_s[:, bass.ds(e, 1), c, :].rearrange(
                                                        "p e d -> p (e d)"),
                                                    start=c == 0, stop=c == FC - 1)
                        last.then_inc(y_mm, 1)
                slots(pe, slot)

            @block.scalar
            def _(act):
                nc.scalar.preload_act_table_set("gelu_apprx_tanh_and_others")

                def slot(t, it, k):
                    if there(t, 0):
                        if past(t, 2):
                            act.wait_ge(y_mm, t - 1)
                        for c in range(FC):
                            bank = H0 + 2 * (k % 2) + c // HALF
                            if c % HALF == 0:
                                act.wait_ge(h_mm, t * 2 + (c // HALF + 1))
                            nc.scalar.activation(hT[:, k % 2, c, :],
                                                 banks[:, bank, c % HALF * P:(c % HALF + 1) * P],
                                                 ACT.Gelu_apprx_tanh,
                                                 bias=be_now[:, k % 4, D + c:D + c + 1]).then_inc(h_ev, 1)
                    if there(t, -1):
                        act.wait_ge(xt_mm, t + 2)
                        if past(t, 1):
                            act.wait_ge(h_mm, 2 * t)
                        nc.scalar.activation(xT[:, (k + 1) % 2, :],
                                             banks[:, XT0 + (k + 1) % 2, 0:P], ACT.Copy
                                             ).then_inc(xt_ev, 1)
                slots(act, slot)

            @block.vector
            def _(dve):
                held = [None]

                def expert_of(t):
                    return nc.vector.value_load(tile_expert[0:1, bass.ds(t, 1)],
                                                min_val=0, max_val=EXPERTS - 1)

                def slot(t, it, k):
                    if there(t, 2):
                        dve.wait_ge(y_mm, t - 1)
                        if past(t, 3):
                            dve.wait_ge(res_d, t - 2)
                        nc.vector.tensor_tensor(y[:], banks[:, Y0 + k % 2, 0:D],
                                                be_now[:, (k - 2) % 4, 0:D], ALU.add
                                                ).then_inc(y_ev, 1)
                    if there(t, 2):
                        dve.wait_ge(y_ev, t - 1)
                        if past(t, 4):
                            dve.wait_ge(fin_d, t - 3)
                        nc.vector.scalar_tensor_tensor(
                            resid[:, k % 2, :], y[:], rows[:, (k - 2) % LOADS, D:D + 1],
                            rows[:, (k - 2) % LOADS, 0:D], ALU.mult, ALU.add).then_inc(res_d, 1)
                        dve.wait_ge(res_d, t - 1)
                        if past(t, 3):
                            dve.wait_ge(mom_d, t - 2)
                        nc.vector.bn_stats(stats[:], resid[:, k % 2, :]).then_inc(st_d, 1)
                    if there(t, 3):
                        dve.wait_ge(rstd_d, t - 2)
                        if past(t, 3 + SCATTERS):
                            dve.wait_ge(s_out[(k - 3) % SCATTERS],
                                        16 * (it * (BODY // SCATTERS) + (k - 3 - SCATTERS) // SCATTERS + 1))
                        nc.vector.tensor_copy(
                            token[:, (k - 3) % SCATTERS:(k - 3) % SCATTERS + 1],
                            rows[:, (k - 3) % LOADS, D + 1:D + 2])
                        nc.vector.tensor_scalar(final[:, (k - 3) % SCATTERS, :], resid[:, (k - 3) % 2, :],
                                                moments[:, (k - 3) % 2, 0:1],
                                                rstd[:, (k - 3) % 2:(k - 3) % 2 + 1],
                                                ALU.subtract, ALU.mult).then_inc(fin_d, 1)
                    if there(t, -2):
                        if k in (-2, 0):
                            held[0] = expert_of(t + 2)
                        if past(t, 2):
                            dve.wait_ge(y_ev, t - 1)
                        nc.vector.tensor_copy(w1_now[:, (k + 2) % 4, None, :],
                                              w1_s[:, bass.ds(held[0], 1), :])
                        nc.vector.tensor_copy(be_now[:, (k + 2) % 4, None, :],
                                              be_s[:, bass.ds(held[0], 1), :]).then_inc(w_now, 1)
                        if k < BODY - 1 and there(t, -3):
                            held[0] = expert_of(t + 3)
                    if there(t, 2):
                        dve.wait_ge(st_d, t - 1)
                        if past(t, 4):
                            dve.wait_ge(fin_d, t - 3)
                        dve.sem_inc(carry_d, 1)
                        nc.vector.bn_aggr(moments[:, k % 2, :], stats[:]).then_inc(mom_d, 1)
                slots(dve, slot)


_ORDER = ["x", "xT", "ctxT", "mask", "Wq", "Wk", "Wv", "Wg", "Wgk1", "Wgk2", "bgk2", "rms_w", "Wo",
          "wq", "bq", "wk", "bk", "wv", "bv", "wo", "bo", "switch_w", "switch_b",
          "w1", "b1T", "w2", "b2"]


def kernel(**inputs):
    import numpy as _np
    import concourse.bacc as _bacc
    from concourse import mybir as _mybir
    from concourse.bass_utils import run_bass_kernel_spmd as _run

    given = {k: _np.asarray(v) for k, v in inputs.items()}
    x = given["x"].reshape(-1, given["x"].shape[-1])
    context = given["ctx_1024"].reshape(-1, given["ctx_1024"].shape[-1])
    mask = given["mask_Bx1xSxS2_bf0"]
    arrays = {"x": x, "xT": x.T, "ctxT": context.T,
              "mask": mask.reshape(-1, mask.shape[-1])}
    for name in _ORDER[4:]:
        stage = ("L0_attn_" if name in _ORDER[4:13] else
                 "L0_xattn_" if name in _ORDER[13:21] else "L0_ffn_")
        if name == "b1T":
            arrays[name] = given[stage + "b1"].reshape(-1, x.shape[-1]).T
        else:
            arrays[name] = given[stage + name]
    nc = _bacc.Bacc("TRN2", target_bir_lowering=False, num_devices=1)
    args = []
    for name in _ORDER:
        arrays[name] = _np.ascontiguousarray(arrays[name])
        args.append(nc.dram_tensor("in_" + name, arrays[name].shape,
                                   _mybir.dt.from_np(arrays[name].dtype), kind="ExternalInput").ap())
    args.append(nc.dram_tensor("out", x.shape, _mybir.dt.float32, kind="ExternalOutput").ap())
    decoder_layer(nc, *args)
    result = _run(nc, [{"in_" + k: v for k, v in arrays.items()}], core_ids=[0])
    return result.results[0]["out"].reshape(given["x"].shape)
```
